# Optimizing a Trainium2 kernel written in Bass

```python
import numpy as np
import jax
import jax.numpy as jnp

def _softmax(x, axis=-1):
    return jax.nn.softmax(x, axis=axis)

def _gelu(x):
    return jax.nn.gelu(x, approximate=True)

def _silu(x):
    return jax.nn.silu(x)

def _sigmoid(x):
    return jax.nn.sigmoid(x)

def _layernorm(x, axis=-1, eps=1e-05):
    m = jnp.mean(x, axis=axis, keepdims=True)
    v = jnp.var(x, axis=axis, keepdims=True)
    return (x - m) / jnp.sqrt(v + eps)

def _scatter_add(tgt, idx, src, axis=0):
    return tgt.at[idx].add(src)

def _segment_sum(src, seg, n):
    return jax.ops.segment_sum(src, seg, n)
kernel_name = 'mk_gnn_ffn_d4_gnn_r32_81090e'

def setup_inputs(seed: int=0):
    np.random.seed(seed)
    _w = jnp.asarray

    def _rec_inputs():
        import jax
        import jax.numpy as jnp
        _gk = jax.random.key(seed)
        x = -0.0002117 + 1 * jax.random.normal(jax.random.fold_in(_gk, 1), (3125, 256), jnp.float32)
        _s = jax.random.randint(jax.random.fold_in(_gk, 2), (25000,), 0, 3125, jnp.int32)
        _d = jax.random.randint(jax.random.fold_in(_gk, 3), (25000,), 0, 3125, jnp.int32)
        _loop = jnp.arange(3125, dtype=jnp.int32)
        src = jnp.concatenate([_s, _d, _loop])
        dst = jnp.concatenate([_d, _s, _loop])
        _o = jnp.argsort(dst, stable=True)
        src = src[_o]
        dst = dst[_o]
        return (x, src, dst)
    x, src, dst = _rec_inputs()

    def _L0_gnn_setup():
        import jax, jax.numpy as jnp
        import numpy as np
        EPS = 1e-12

        def l2_normalize_rows(x):
            nrm = jnp.sqrt(jnp.sum(x * x, axis=1, keepdims=True))
            return x / jnp.maximum(nrm, EPS)
        key = jax.random.key(seed)
        k1, k2, k3, k4 = jax.random.split(key, 4)
        n, din, dout, E = (3125, 256, 256, 50000)
        x = jax.random.normal(k1, (n, din), dtype=jnp.float32)
        edge_index = jax.random.randint(k2, (2, E), 0, n, dtype=jnp.int64)
        s = float(np.sqrt(6.0 / (din + dout)))
        W_gcn = jax.random.uniform(k3, (din, dout), jnp.float32, -s, s)
        b_gcn = jnp.zeros((dout,), jnp.float32)
        W_V = jax.random.uniform(k4, (din, dout), jnp.float32, -s, s)
        return {'x': x, 'edge_index': edge_index, 'W_gcn': W_gcn, 'b_gcn': b_gcn, 'W_V': W_V}
    _L0_gnn_all = _L0_gnn_setup()
    _L0_gnn_in = {k: v for k, v in _L0_gnn_all.items() if k in ('W_gcn', 'b_gcn', 'W_V')}
    del _L0_gnn_all

    def _L0_ffn_setup():
        import jax, jax.numpy as jnp
        import numpy as np
        B, N, D = (16, 128, 256)
        NUM_EXPERTS, TOP_K, HEADS = (4, 2, 4)
        N_EDGES = 32768
        LN_EPS = 1e-05

        def _layernorm(x, g, b):
            mu = x.mean(-1, keepdims=True)
            var = ((x - mu) ** 2).mean(-1, keepdims=True)
            return (x - mu) * jax.lax.rsqrt(var + LN_EPS) * g + b

        def _forward(x, edge_index, W_gat, att_src, att_dst, b_gat, ln_gamma, ln_beta, W1, b1, W2, b2):
            Bc, Nc, Dc = x.shape
            M = Bc * Nc
            x_flat = x.reshape(M, Dc)
            h = (x_flat @ W_gat).reshape(M, HEADS, NUM_EXPERTS)
            loops = jnp.arange(M, dtype=edge_index.dtype)
            src = jnp.concatenate([edge_index[0], loops])
            dst = jnp.concatenate([edge_index[1], loops])
            a_src = (h * att_src).sum(-1)
            a_dst = (h * att_dst).sum(-1)
            e = jax.nn.leaky_relu(a_src[src] + a_dst[dst], negative_slope=0.2)
            e_max = jax.ops.segment_max(e, dst, num_segments=M)
            ee = jnp.exp(e - e_max[dst])
            denom = jax.ops.segment_sum(ee, dst, num_segments=M)
            alpha = ee / (denom[dst] + 1e-16)
            msg = h[src] * alpha[:, :, None]
            agg = jax.ops.segment_sum(msg, dst, num_segments=M).reshape(M, HEADS * NUM_EXPERTS) + b_gat
            scores = _layernorm(agg, ln_gamma, ln_beta).reshape(M, HEADS, NUM_EXPERTS).mean(1)
            scores = scores.reshape(Bc, Nc, NUM_EXPERTS)
            topk_s, topk_i = jax.lax.top_k(scores, TOP_K)
            w = jax.nn.softmax(topk_s, axis=-1)
            out = jnp.zeros_like(x)
            for ei in range(NUM_EXPERTS):
                g = jnp.where(topk_i == ei, w, 0.0).sum(-1)
                hh = jax.nn.gelu(x @ W1[ei] + b1[ei], approximate=False)
                out = out + g[..., None] * (hh @ W2[ei] + b2[ei])
            return out
        key = jax.random.key(seed)
        ks = jax.random.split(key, 8)
        s = 0.05
        return {'x': jax.random.normal(ks[0], (B, N, D), jnp.float32), 'W_gat': jax.random.normal(ks[1], (D, HEADS * NUM_EXPERTS), jnp.float32) * s, 'att_src': jax.random.normal(ks[2], (HEADS, NUM_EXPERTS), jnp.float32) * s, 'att_dst': jax.random.normal(ks[3], (HEADS, NUM_EXPERTS), jnp.float32) * s, 'b_gat': jnp.zeros((HEADS * NUM_EXPERTS,), jnp.float32), 'ln_gamma': jnp.ones((HEADS * NUM_EXPERTS,), jnp.float32), 'ln_beta': jnp.zeros((HEADS * NUM_EXPERTS,), jnp.float32), 'W1': jax.random.normal(ks[4], (NUM_EXPERTS, D, 2 * D), jnp.float32) * s, 'b1': jnp.zeros((NUM_EXPERTS, 2 * D), jnp.float32), 'W2': jax.random.normal(ks[5], (NUM_EXPERTS, 2 * D, D), jnp.float32) * s, 'b2': jnp.zeros((NUM_EXPERTS, D), jnp.float32), 'edge_index': jax.random.randint(ks[6], (2, N_EDGES), 0, B * N, jnp.int32)}
    _L0_ffn_all = _L0_ffn_setup()
    _L0_ffn_in = {k: v for k, v in _L0_ffn_all.items() if k in ('W_gat', 'att_src', 'att_dst', 'b_gat', 'ln_gamma', 'ln_beta', 'W1', 'b1', 'W2', 'b2', 'edge_index')}
    del _L0_ffn_all

    def _L1_gnn_setup():
        import jax, jax.numpy as jnp
        import numpy as np
        N, E, D = (10000, 10000, 256)

        def _add_self_loops(src, dst, n):
            loop = jnp.arange(n, dtype=src.dtype)
            return (jnp.concatenate([src, loop]), jnp.concatenate([dst, loop]))

        def _gcn_conv(x, W, b, src, dst, n):
            xw = x @ W
            deg = jax.ops.segment_sum(jnp.ones(src.shape[0], x.dtype), dst, num_segments=n)
            dinv = jnp.where(deg > 0, jax.lax.rsqrt(deg), 0.0)
            norm = dinv[src] * dinv[dst]
            agg = jax.ops.segment_sum(xw[src] * norm[:, None], dst, num_segments=n)
            return agg + b

        def _gat_conv(x, W, a_src, a_dst, b, src, dst, n):
            xw = x @ W
            e = jax.nn.leaky_relu((xw @ a_src)[src] + (xw @ a_dst)[dst], 0.2)
            m = jax.ops.segment_max(e, dst, num_segments=n)
            ex = jnp.exp(e - m[dst])
            s = jax.ops.segment_sum(ex, dst, num_segments=n)
            alpha = ex / (s[dst] + 1e-16)
            agg = jax.ops.segment_sum(alpha[:, None] * xw[src], dst, num_segments=n)
            return agg + b
        key = jax.random.key(seed)
        ks = jax.random.split(key, 6)
        return {'event_emb': jax.random.normal(ks[0], (N, D), jnp.float32), 'edge_index': jax.random.randint(ks[1], (2, E), 0, N), 'W1': jax.random.normal(ks[2], (D, D), jnp.float32) / np.sqrt(D).astype(np.float32), 'b1': jnp.zeros((D,), jnp.float32), 'W2': jax.random.normal(ks[3], (D, D), jnp.float32) / np.sqrt(D).astype(np.float32), 'att_src': jax.random.normal(ks[4], (D,), jnp.float32) / np.sqrt(D).astype(np.float32), 'att_dst': jax.random.normal(ks[5], (D,), jnp.float32) / np.sqrt(D).astype(np.float32), 'b2': jnp.zeros((D,), jnp.float32)}
    _L1_gnn_all = _L1_gnn_setup()
    _L1_gnn_in = {k: v for k, v in _L1_gnn_all.items() if k in ('W1', 'b1', 'W2', 'att_src', 'att_dst', 'b2')}
    del _L1_gnn_all

    def _L1_ffn_setup():
        import jax, jax.numpy as jnp
        import numpy as np
        BN_EPS = 0.001

        def _bn(h, g, b, m, v):
            return g * (h - m) * jax.lax.rsqrt(v + BN_EPS) + b
        key = jax.random.key(seed)
        ks = jax.random.split(key, 8)
        B, F, Df = (256, 64, 256)
        E, H, D = (8, 256, 256)
        s1 = 1.0 / np.sqrt(Df)
        s2 = 1.0 / np.sqrt(H)
        return {'x': jax.random.normal(ks[0], (B, F, Df), jnp.float32), 'Wr': jax.random.normal(ks[1], (Df, E), jnp.float32) * s1, 'br': jnp.zeros((E,), jnp.float32), 'W1': jax.random.normal(ks[2], (E, Df, H), jnp.float32) * s1, 'b1': jnp.zeros((E, H), jnp.float32), 'g1': jnp.ones((E, H), jnp.float32), 'be1': jnp.zeros((E, H), jnp.float32), 'm1': jnp.zeros((E, H), jnp.float32), 'v1': jnp.ones((E, H), jnp.float32), 'W2': jax.random.normal(ks[3], (E, H, H), jnp.float32) * s2, 'b2': jnp.zeros((E, H), jnp.float32), 'g2': jnp.ones((E, H), jnp.float32), 'be2': jnp.zeros((E, H), jnp.float32), 'm2': jnp.zeros((E, H), jnp.float32), 'v2': jnp.ones((E, H), jnp.float32), 'Wo': jax.random.normal(ks[4], (E, H, D), jnp.float32) * s2, 'bo': jnp.zeros((E, D), jnp.float32)}
    _L1_ffn_all = _L1_ffn_setup()
    _L1_ffn_in = {k: v for k, v in _L1_ffn_all.items() if k in ('Wr', 'br', 'W1', 'b1', 'g1', 'be1', 'm1', 'v1', 'W2', 'b2', 'g2', 'be2', 'm2', 'v2', 'Wo', 'bo')}
    del _L1_ffn_all

    def _L2_gnn_setup():
        import jax, jax.numpy as jnp
        import numpy as np
        N, E = (50000, 25000)
        IN, HID, HEADS, OUT = (256, 64, 4, 256)
        FIRST_OUT = HID * HEADS

        def gat_conv(x, src, dst, W, a_src, a_dst, b, concat):
            n = x.shape[0]
            H, C = a_src.shape
            h = (x @ W).reshape(n, H, C)
            es = jnp.einsum('nhc,hc->nh', h, a_src)[src]
            ed = jnp.einsum('nhc,hc->nh', h, a_dst)[dst]
            e = jax.nn.leaky_relu(es + ed, negative_slope=0.2)
            m = jax.ops.segment_max(e, dst, num_segments=n)
            p = jnp.exp(e - m[dst])
            z = jax.ops.segment_sum(p, dst, num_segments=n)
            alpha = p / z[dst]
            out = jax.ops.segment_sum(h[src] * alpha[:, :, None], dst, num_segments=n)
            out = out.reshape(n, H * C) if concat else out.mean(axis=1)
            return out + b

        def batchnorm(x, gamma, beta, eps=1e-05):
            mu = x.mean(axis=0)
            var = ((x - mu) ** 2).mean(axis=0)
            return gamma * (x - mu) / jnp.sqrt(var + eps) + beta
        key = jax.random.key(seed)
        ks = jax.random.split(key, 10)
        s = 0.05
        return {'x': jax.random.normal(ks[0], (N, IN), jnp.float32), 'edge_index': jax.random.randint(ks[1], (2, E), 0, N, dtype=jnp.int64), 'W0': jax.random.normal(ks[2], (IN, HEADS * HID), jnp.float32) * s, 'a_src0': jax.random.normal(ks[3], (HEADS, HID), jnp.float32) * s, 'a_dst0': jax.random.normal(ks[4], (HEADS, HID), jnp.float32) * s, 'b0': jnp.zeros((HEADS * HID,), jnp.float32), 'gamma0': jnp.ones((FIRST_OUT,), jnp.float32), 'beta0': jnp.zeros((FIRST_OUT,), jnp.float32), 'W1': jax.random.normal(ks[5], (FIRST_OUT, OUT), jnp.float32) * s, 'a_src1': jax.random.normal(ks[6], (1, OUT), jnp.float32) * s, 'a_dst1': jax.random.normal(ks[7], (1, OUT), jnp.float32) * s, 'b1': jnp.zeros((OUT,), jnp.float32)}
    _L2_gnn_all = _L2_gnn_setup()
    _L2_gnn_in = {k: v for k, v in _L2_gnn_all.items() if k in ('W0', 'a_src0', 'a_dst0', 'b0', 'gamma0', 'beta0', 'W1', 'a_src1', 'a_dst1', 'b1')}
    del _L2_gnn_all

    def _L2_ffn_setup():
        import math
        import jax, jax.numpy as jnp
        import numpy as np
        CAPACITY_FACTOR = 1.25
        key = jax.random.key(seed)
        ks = jax.random.split(key, 5)
        B, L, D, F, E = (8, 256, 256, 1024, 8)
        h = jax.random.normal(ks[0], (B, L, D), dtype=jnp.float32)
        gate_w = jax.random.normal(ks[1], (D, E), dtype=jnp.float32) * 0.02
        gate_b = jnp.zeros((E,), dtype=jnp.float32)
        w1 = jax.random.normal(ks[2], (E, D, F), dtype=jnp.float32) * (1.0 / math.sqrt(D))
        b1 = jnp.zeros((E, F), dtype=jnp.float32)
        w2 = jax.random.normal(ks[3], (E, F, D), dtype=jnp.float32) * (1.0 / math.sqrt(F))
        b2 = jnp.zeros((E, D), dtype=jnp.float32)
        return {'h': h, 'gate_w': gate_w, 'gate_b': gate_b, 'w1': w1, 'b1': b1, 'w2': w2, 'b2': b2}
    _L2_ffn_all = _L2_ffn_setup()
    _L2_ffn_in = {k: v for k, v in _L2_ffn_all.items() if k in ('gate_w', 'gate_b', 'w1', 'b1', 'w2', 'b2')}
    del _L2_ffn_all

    def _L3_gnn_setup():
        import jax, jax.numpy as jnp
        import numpy as np
        N, E, H = (3125, 50000, 256)
        BN_EPS = 1e-05

        def _bn(h, g, b):
            mu = h.mean(axis=0)
            var = h.var(axis=0)
            return (h - mu) * jax.lax.rsqrt(var + BN_EPS) * g + b

        def _lin_bn_relu(h, W, b, g, be):
            return jax.nn.relu(_bn(h @ W + b, g, be))
        key = jax.random.key(seed)
        ks = jax.random.split(key, 10)

        def lin_w(k, fan_in, fan_out):
            bound = 1.0 / np.sqrt(fan_in)
            return jax.random.uniform(k, (fan_in, fan_out), jnp.float32, -bound, bound)
        x = jax.random.normal(ks[0], (N, H), jnp.float32)
        edge_index = jax.random.randint(ks[1], (2, E), 0, N, jnp.int32)
        inp = {'x': x, 'edge_index': edge_index}
        dims = {'1': (H, H), '2': (H, H), '3': (2 * H, H), '4': (H, H), '5': (H, H)}
        for i, (name, (fi, fo)) in enumerate(dims.items()):
            inp[f'W{name}'] = lin_w(ks[2 + i], fi, fo)
            inp[f'b{name}'] = jnp.zeros((fo,), jnp.float32)
            inp[f'g{name}'] = jnp.ones((fo,), jnp.float32)
            inp[f'be{name}'] = jnp.zeros((fo,), jnp.float32)
        return inp
    _L3_gnn_all = _L3_gnn_setup()
    _L3_gnn_in = {k: v for k, v in _L3_gnn_all.items() if k in ('W1', 'b1', 'g1', 'be1', 'W2', 'b2', 'g2', 'be2', 'W3', 'b3', 'g3', 'be3', 'W4', 'b4', 'g4', 'be4', 'W5', 'b5', 'g5', 'be5')}
    del _L3_gnn_all

    def _L3_ffn_setup():
        import jax, jax.numpy as jnp
        import numpy as np
        E, D, H, TOP_K = (6, 256, 256, 2)
        ROUTER_H = D // 2
        key = jax.random.key(seed)
        ks = jax.random.split(key, 12)
        s = 1.0 / np.sqrt(D)
        sh = 1.0 / np.sqrt(H)
        sr = 1.0 / np.sqrt(ROUTER_H)
        return {'features': jax.random.normal(ks[0], (8, 128, D), dtype=jnp.float32), 'router_w1': jax.random.uniform(ks[1], (D, ROUTER_H), jnp.float32, -s, s), 'router_b1': jnp.zeros((ROUTER_H,), jnp.float32), 'router_w2': jax.random.uniform(ks[2], (ROUTER_H, E), jnp.float32, -sr, sr), 'router_b2': jnp.zeros((E,), jnp.float32), 'expert_w1': jax.random.uniform(ks[3], (E, D, H), jnp.float32, -s, s), 'expert_b1': jnp.zeros((E, H), jnp.float32), 'expert_w2': jax.random.uniform(ks[4], (E, H, H), jnp.float32, -sh, sh), 'expert_b2': jnp.zeros((E, H), jnp.float32), 'expert_w3': jax.random.uniform(ks[5], (E, H, D), jnp.float32, -sh, sh), 'expert_b3': jnp.zeros((E, D), jnp.float32)}
    _L3_ffn_all = _L3_ffn_setup()
    _L3_ffn_in = {k: v for k, v in _L3_ffn_all.items() if k in ('router_w1', 'router_b1', 'router_w2', 'router_b2', 'expert_w1', 'expert_b1', 'expert_w2', 'expert_b2', 'expert_w3', 'expert_b3')}
    del _L3_ffn_all
    return {'x': x, 'src': src, 'dst': dst, 'L0_gnn_W_gcn': _L0_gnn_in['W_gcn'], 'L0_gnn_b_gcn': _L0_gnn_in['b_gcn'], 'L0_gnn_W_V': _L0_gnn_in['W_V'], 'L0_ffn_W_gat': _L0_ffn_in['W_gat'], 'L0_ffn_att_src': _L0_ffn_in['att_src'], 'L0_ffn_att_dst': _L0_ffn_in['att_dst'], 'L0_ffn_b_gat': _L0_ffn_in['b_gat'], 'L0_ffn_ln_gamma': _L0_ffn_in['ln_gamma'], 'L0_ffn_ln_beta': _L0_ffn_in['ln_beta'], 'L0_ffn_W1': _L0_ffn_in['W1'], 'L0_ffn_b1': _L0_ffn_in['b1'], 'L0_ffn_W2': _L0_ffn_in['W2'], 'L0_ffn_b2': _L0_ffn_in['b2'], 'L0_ffn_edge_index': _L0_ffn_in['edge_index'], 'L1_gnn_W1': _L1_gnn_in['W1'], 'L1_gnn_b1': _L1_gnn_in['b1'], 'L1_gnn_W2': _L1_gnn_in['W2'], 'L1_gnn_att_src': _L1_gnn_in['att_src'], 'L1_gnn_att_dst': _L1_gnn_in['att_dst'], 'L1_gnn_b2': _L1_gnn_in['b2'], 'L1_ffn_Wr': _L1_ffn_in['Wr'], 'L1_ffn_br': _L1_ffn_in['br'], 'L1_ffn_W1': _L1_ffn_in['W1'], 'L1_ffn_b1': _L1_ffn_in['b1'], 'L1_ffn_g1': _L1_ffn_in['g1'], 'L1_ffn_be1': _L1_ffn_in['be1'], 'L1_ffn_m1': _L1_ffn_in['m1'], 'L1_ffn_v1': _L1_ffn_in['v1'], 'L1_ffn_W2': _L1_ffn_in['W2'], 'L1_ffn_b2': _L1_ffn_in['b2'], 'L1_ffn_g2': _L1_ffn_in['g2'], 'L1_ffn_be2': _L1_ffn_in['be2'], 'L1_ffn_m2': _L1_ffn_in['m2'], 'L1_ffn_v2': _L1_ffn_in['v2'], 'L1_ffn_Wo': _L1_ffn_in['Wo'], 'L1_ffn_bo': _L1_ffn_in['bo'], 'L2_gnn_W0': _L2_gnn_in['W0'], 'L2_gnn_a_src0': _L2_gnn_in['a_src0'], 'L2_gnn_a_dst0': _L2_gnn_in['a_dst0'], 'L2_gnn_b0': _L2_gnn_in['b0'], 'L2_gnn_gamma0': _L2_gnn_in['gamma0'], 'L2_gnn_beta0': _L2_gnn_in['beta0'], 'L2_gnn_W1': _L2_gnn_in['W1'], 'L2_gnn_a_src1': _L2_gnn_in['a_src1'], 'L2_gnn_a_dst1': _L2_gnn_in['a_dst1'], 'L2_gnn_b1': _L2_gnn_in['b1'], 'L2_ffn_gate_w': _L2_ffn_in['gate_w'], 'L2_ffn_gate_b': _L2_ffn_in['gate_b'], 'L2_ffn_w1': _L2_ffn_in['w1'], 'L2_ffn_b1': _L2_ffn_in['b1'], 'L2_ffn_w2': _L2_ffn_in['w2'], 'L2_ffn_b2': _L2_ffn_in['b2'], 'L3_gnn_W1': _L3_gnn_in['W1'], 'L3_gnn_b1': _L3_gnn_in['b1'], 'L3_gnn_g1': _L3_gnn_in['g1'], 'L3_gnn_be1': _L3_gnn_in['be1'], 'L3_gnn_W2': _L3_gnn_in['W2'], 'L3_gnn_b2': _L3_gnn_in['b2'], 'L3_gnn_g2': _L3_gnn_in['g2'], 'L3_gnn_be2': _L3_gnn_in['be2'], 'L3_gnn_W3': _L3_gnn_in['W3'], 'L3_gnn_b3': _L3_gnn_in['b3'], 'L3_gnn_g3': _L3_gnn_in['g3'], 'L3_gnn_be3': _L3_gnn_in['be3'], 'L3_gnn_W4': _L3_gnn_in['W4'], 'L3_gnn_b4': _L3_gnn_in['b4'], 'L3_gnn_g4': _L3_gnn_in['g4'], 'L3_gnn_be4': _L3_gnn_in['be4'], 'L3_gnn_W5': _L3_gnn_in['W5'], 'L3_gnn_b5': _L3_gnn_in['b5'], 'L3_gnn_g5': _L3_gnn_in['g5'], 'L3_gnn_be5': _L3_gnn_in['be5'], 'L3_ffn_router_w1': _L3_ffn_in['router_w1'], 'L3_ffn_router_b1': _L3_ffn_in['router_b1'], 'L3_ffn_router_w2': _L3_ffn_in['router_w2'], 'L3_ffn_router_b2': _L3_ffn_in['router_b2'], 'L3_ffn_expert_w1': _L3_ffn_in['expert_w1'], 'L3_ffn_expert_b1': _L3_ffn_in['expert_b1'], 'L3_ffn_expert_w2': _L3_ffn_in['expert_w2'], 'L3_ffn_expert_b2': _L3_ffn_in['expert_b2'], 'L3_ffn_expert_w3': _L3_ffn_in['expert_w3'], 'L3_ffn_expert_b3': _L3_ffn_in['expert_b3']}

def reference(x, src, dst, L0_gnn_W_gcn, L0_gnn_b_gcn, L0_gnn_W_V, L0_ffn_W_gat, L0_ffn_att_src, L0_ffn_att_dst, L0_ffn_b_gat, L0_ffn_ln_gamma, L0_ffn_ln_beta, L0_ffn_W1, L0_ffn_b1, L0_ffn_W2, L0_ffn_b2, L0_ffn_edge_index, L1_gnn_W1, L1_gnn_b1, L1_gnn_W2, L1_gnn_att_src, L1_gnn_att_dst, L1_gnn_b2, L1_ffn_Wr, L1_ffn_br, L1_ffn_W1, L1_ffn_b1, L1_ffn_g1, L1_ffn_be1, L1_ffn_m1, L1_ffn_v1, L1_ffn_W2, L1_ffn_b2, L1_ffn_g2, L1_ffn_be2, L1_ffn_m2, L1_ffn_v2, L1_ffn_Wo, L1_ffn_bo, L2_gnn_W0, L2_gnn_a_src0, L2_gnn_a_dst0, L2_gnn_b0, L2_gnn_gamma0, L2_gnn_beta0, L2_gnn_W1, L2_gnn_a_src1, L2_gnn_a_dst1, L2_gnn_b1, L2_ffn_gate_w, L2_ffn_gate_b, L2_ffn_w1, L2_ffn_b1, L2_ffn_w2, L2_ffn_b2, L3_gnn_W1, L3_gnn_b1, L3_gnn_g1, L3_gnn_be1, L3_gnn_W2, L3_gnn_b2, L3_gnn_g2, L3_gnn_be2, L3_gnn_W3, L3_gnn_b3, L3_gnn_g3, L3_gnn_be3, L3_gnn_W4, L3_gnn_b4, L3_gnn_g4, L3_gnn_be4, L3_gnn_W5, L3_gnn_b5, L3_gnn_g5, L3_gnn_be5, L3_ffn_router_w1, L3_ffn_router_b1, L3_ffn_router_w2, L3_ffn_router_b2, L3_ffn_expert_w1, L3_ffn_expert_b1, L3_ffn_expert_w2, L3_ffn_expert_b2, L3_ffn_expert_w3, L3_ffn_expert_b3):
    import jax
    import jax.numpy as jnp

    def _L0_gnn_ref(x, edge_index, W_gcn, b_gcn, W_V):
        import jax, jax.numpy as jnp
        import numpy as np
        EPS = 1e-12

        def l2_normalize_rows(x):
            nrm = jnp.sqrt(jnp.sum(x * x, axis=1, keepdims=True))
            return x / jnp.maximum(nrm, EPS)
        n = x.shape[0]
        beta = 0.1
        H = l2_normalize_rows(x)
        XW = H @ W_gcn
        loop = jnp.arange(n, dtype=edge_index.dtype)
        src = jnp.concatenate([edge_index[0], loop])
        dst = jnp.concatenate([edge_index[1], loop])
        deg = jax.ops.segment_sum(jnp.ones_like(dst, dtype=XW.dtype), dst, num_segments=n)
        dinv = jax.lax.rsqrt(jnp.maximum(deg, 1e-30))
        norm = dinv[src] * dinv[dst]
        msg = XW[src] * norm[:, None]
        z_local = jax.ops.segment_sum(msg, dst, num_segments=n) + b_gcn
        HtH = H.T @ H
        z_global = beta / n * (H @ HtH @ W_V)
        out = jax.nn.relu(z_local + z_global)
        return l2_normalize_rows(out)

    def _L0_ffn_ref(x, W_gat, att_src, att_dst, b_gat, ln_gamma, ln_beta, W1, b1, W2, b2, edge_index):
        import jax, jax.numpy as jnp
        import numpy as np
        B, N, D = (16, 128, 256)
        NUM_EXPERTS, TOP_K, HEADS = (4, 2, 4)
        N_EDGES = 32768
        LN_EPS = 1e-05

        def _layernorm(x, g, b):
            mu = x.mean(-1, keepdims=True)
            var = ((x - mu) ** 2).mean(-1, keepdims=True)
            return (x - mu) * jax.lax.rsqrt(var + LN_EPS) * g + b

        def _forward(x, edge_index, W_gat, att_src, att_dst, b_gat, ln_gamma, ln_beta, W1, b1, W2, b2):
            Bc, Nc, Dc = x.shape
            M = Bc * Nc
            x_flat = x.reshape(M, Dc)
            h = (x_flat @ W_gat).reshape(M, HEADS, NUM_EXPERTS)
            loops = jnp.arange(M, dtype=edge_index.dtype)
            src = jnp.concatenate([edge_index[0], loops])
            dst = jnp.concatenate([edge_index[1], loops])
            a_src = (h * att_src).sum(-1)
            a_dst = (h * att_dst).sum(-1)
            e = jax.nn.leaky_relu(a_src[src] + a_dst[dst], negative_slope=0.2)
            e_max = jax.ops.segment_max(e, dst, num_segments=M)
            ee = jnp.exp(e - e_max[dst])
            denom = jax.ops.segment_sum(ee, dst, num_segments=M)
            alpha = ee / (denom[dst] + 1e-16)
            msg = h[src] * alpha[:, :, None]
            agg = jax.ops.segment_sum(msg, dst, num_segments=M).reshape(M, HEADS * NUM_EXPERTS) + b_gat
            scores = _layernorm(agg, ln_gamma, ln_beta).reshape(M, HEADS, NUM_EXPERTS).mean(1)
            scores = scores.reshape(Bc, Nc, NUM_EXPERTS)
            topk_s, topk_i = jax.lax.top_k(scores, TOP_K)
            w = jax.nn.softmax(topk_s, axis=-1)
            out = jnp.zeros_like(x)
            for ei in range(NUM_EXPERTS):
                g = jnp.where(topk_i == ei, w, 0.0).sum(-1)
                hh = jax.nn.gelu(x @ W1[ei] + b1[ei], approximate=False)
                out = out + g[..., None] * (hh @ W2[ei] + b2[ei])
            return out
        return _forward(x, edge_index, W_gat, att_src, att_dst, b_gat, ln_gamma, ln_beta, W1, b1, W2, b2)

    def _L1_gnn_ref(event_emb, edge_index, W1, b1, W2, att_src, att_dst, b2):
        import jax, jax.numpy as jnp
        import numpy as np
        N, E, D = (10000, 10000, 256)

        def _add_self_loops(src, dst, n):
            loop = jnp.arange(n, dtype=src.dtype)
            return (jnp.concatenate([src, loop]), jnp.concatenate([dst, loop]))

        def _gcn_conv(x, W, b, src, dst, n):
            xw = x @ W
            deg = jax.ops.segment_sum(jnp.ones(src.shape[0], x.dtype), dst, num_segments=n)
            dinv = jnp.where(deg > 0, jax.lax.rsqrt(deg), 0.0)
            norm = dinv[src] * dinv[dst]
            agg = jax.ops.segment_sum(xw[src] * norm[:, None], dst, num_segments=n)
            return agg + b

        def _gat_conv(x, W, a_src, a_dst, b, src, dst, n):
            xw = x @ W
            e = jax.nn.leaky_relu((xw @ a_src)[src] + (xw @ a_dst)[dst], 0.2)
            m = jax.ops.segment_max(e, dst, num_segments=n)
            ex = jnp.exp(e - m[dst])
            s = jax.ops.segment_sum(ex, dst, num_segments=n)
            alpha = ex / (s[dst] + 1e-16)
            agg = jax.ops.segment_sum(alpha[:, None] * xw[src], dst, num_segments=n)
            return agg + b
        n = event_emb.shape[0]
        src, dst = _add_self_loops(edge_index[0], edge_index[1], n)
        x = jax.nn.relu(_gcn_conv(event_emb, W1, b1, src, dst, n))
        x = jax.nn.relu(_gat_conv(x, W2, att_src, att_dst, b2, src, dst, n))
        return x

    def _L1_ffn_ref(x, Wr, br, W1, b1, g1, be1, m1, v1, W2, b2, g2, be2, m2, v2, Wo, bo):
        import jax, jax.numpy as jnp
        import numpy as np
        BN_EPS = 0.001

        def _bn(h, g, b, m, v):
            return g * (h - m) * jax.lax.rsqrt(v + BN_EPS) + b
        feat = jnp.mean(x, axis=0)
        w = jax.nn.softmax(feat @ Wr + br, axis=-1)
        h = jnp.einsum('bfd,edh->bfeh', x, W1) + b1
        h = jax.nn.relu(_bn(h, g1, be1, m1, v1))
        h = jnp.einsum('bfeh,ehk->bfek', h, W2) + b2
        h = jax.nn.relu(_bn(h, g2, be2, m2, v2))
        y = jnp.einsum('bfeh,ehd->bfed', h, Wo) + bo
        return jnp.einsum('bfed,fe->bfd', y, w)

    def _L2_gnn_ref(x, edge_index, W0, a_src0, a_dst0, b0, gamma0, beta0, W1, a_src1, a_dst1, b1):
        import jax, jax.numpy as jnp
        import numpy as np
        N, E = (50000, 25000)
        IN, HID, HEADS, OUT = (256, 64, 4, 256)
        FIRST_OUT = HID * HEADS

        def gat_conv(x, src, dst, W, a_src, a_dst, b, concat):
            n = x.shape[0]
            H, C = a_src.shape
            h = (x @ W).reshape(n, H, C)
            es = jnp.einsum('nhc,hc->nh', h, a_src)[src]
            ed = jnp.einsum('nhc,hc->nh', h, a_dst)[dst]
            e = jax.nn.leaky_relu(es + ed, negative_slope=0.2)
            m = jax.ops.segment_max(e, dst, num_segments=n)
            p = jnp.exp(e - m[dst])
            z = jax.ops.segment_sum(p, dst, num_segments=n)
            alpha = p / z[dst]
            out = jax.ops.segment_sum(h[src] * alpha[:, :, None], dst, num_segments=n)
            out = out.reshape(n, H * C) if concat else out.mean(axis=1)
            return out + b

        def batchnorm(x, gamma, beta, eps=1e-05):
            mu = x.mean(axis=0)
            var = ((x - mu) ** 2).mean(axis=0)
            return gamma * (x - mu) / jnp.sqrt(var + eps) + beta
        n = x.shape[0]
        loops = jnp.arange(n, dtype=edge_index.dtype)
        src = jnp.concatenate([edge_index[0], loops])
        dst = jnp.concatenate([edge_index[1], loops])
        h = gat_conv(x, src, dst, W0, a_src0, a_dst0, b0, concat=True)
        h = batchnorm(h, gamma0, beta0)
        h = jax.nn.elu(h)
        h = gat_conv(h, src, dst, W1, a_src1, a_dst1, b1, concat=False)
        norm = jnp.maximum(jnp.linalg.norm(h, axis=-1, keepdims=True), 1e-12)
        return h / norm

    def _L2_ffn_ref(h, gate_w, gate_b, w1, b1, w2, b2):
        import math
        import jax, jax.numpy as jnp
        import numpy as np
        CAPACITY_FACTOR = 1.25
        B, L, D = h.shape
        E = gate_w.shape[1]
        T = B * L
        C = max(1, math.ceil(CAPACITY_FACTOR * T / E))
        x = h.reshape(T, D)
        logits = x @ gate_w + gate_b
        probs = jax.nn.softmax(logits, axis=-1)
        idx = jnp.argmax(probs, axis=-1)
        prb = jnp.take_along_axis(probs, idx[:, None], axis=1)[:, 0]
        one_hot = jax.nn.one_hot(idx, E, dtype=jnp.float32)
        pos = (jnp.cumsum(one_hot, axis=0) * one_hot).sum(-1).astype(jnp.int32) - 1
        kept = pos < C
        pos_safe = jnp.where(kept, pos, C)
        buf = jnp.zeros((E, C, D), dtype=h.dtype).at[idx, pos_safe].set(x, mode='drop')
        hmid = jax.nn.relu(jnp.einsum('ecd,edf->ecf', buf, w1) + b1[:, None, :])
        ybuf = jnp.einsum('ecf,efd->ecd', hmid, w2) + b2[:, None, :]
        pos_g = jnp.minimum(pos, C - 1)
        y_tok = ybuf[idx, pos_g] * (prb * kept)[:, None]
        y = y_tok.reshape(B, L, D)
        y = jnp.nan_to_num(y, nan=0.0, posinf=10000.0, neginf=-10000.0)
        return y

    def _L3_gnn_ref(x, edge_index, W1, b1, g1, be1, W2, b2, g2, be2, W3, b3, g3, be3, W4, b4, g4, be4, W5, b5, g5, be5):
        import jax, jax.numpy as jnp
        import numpy as np
        N, E, H = (3125, 50000, 256)
        BN_EPS = 1e-05

        def _bn(h, g, b):
            mu = h.mean(axis=0)
            var = h.var(axis=0)
            return (h - mu) * jax.lax.rsqrt(var + BN_EPS) * g + b

        def _lin_bn_relu(h, W, b, g, be):
            return jax.nn.relu(_bn(h @ W + b, g, be))
        src, dst = (edge_index[0], edge_index[1])
        n = x.shape[0]
        agg = jax.ops.segment_sum(x[src], dst, num_segments=n)
        h = x + agg
        h = _lin_bn_relu(h, W1, b1, g1, be1)
        h = _lin_bn_relu(h, W2, b2, g2, be2)
        xc = jnp.concatenate([x, h], axis=1)
        agg2 = jax.ops.segment_sum(xc[src], dst, num_segments=n)
        h2 = xc + agg2
        h2 = _lin_bn_relu(h2, W3, b3, g3, be3)
        h2 = _lin_bn_relu(h2, W4, b4, g4, be4)
        out = _lin_bn_relu(h2, W5, b5, g5, be5)
        return out

    def _L3_ffn_ref(features, router_w1, router_b1, router_w2, router_b2, expert_w1, expert_b1, expert_w2, expert_b2, expert_w3, expert_b3):
        import jax, jax.numpy as jnp
        import numpy as np
        E, D, H, TOP_K = (6, 256, 256, 2)
        ROUTER_H = D // 2
        rh = jax.nn.relu(features @ router_w1 + router_b1)
        expert_logits = jax.nn.softmax(rh @ router_w2 + router_b2, axis=-1)
        top_w, top_i = jax.lax.top_k(expert_logits, TOP_K)
        routing_weights = jax.nn.softmax(top_w, axis=-1)
        h1 = jax.nn.relu(jnp.einsum('bsd,edh->bseh', features, expert_w1) + expert_b1)
        h2 = jax.nn.relu(jnp.einsum('bseh,ehf->bsef', h1, expert_w2) + expert_b2)
        expert_out = jnp.einsum('bsef,efo->bseo', h2, expert_w3) + expert_b3
        sel = jnp.take_along_axis(expert_out, top_i[:, :, :, None], axis=2)
        combined = jnp.sum(sel * routing_weights[..., None], axis=2)
        return combined
    edge_index = jnp.stack([src, dst])
    x = x + _L0_gnn_ref(_layernorm(x, axis=-1), edge_index, L0_gnn_W_gcn, L0_gnn_b_gcn, L0_gnn_W_V)
    x = x + _L0_ffn_ref(_layernorm(x, axis=-1)[None], L0_ffn_W_gat, L0_ffn_att_src, L0_ffn_att_dst, L0_ffn_b_gat, L0_ffn_ln_gamma, L0_ffn_ln_beta, L0_ffn_W1, L0_ffn_b1, L0_ffn_W2, L0_ffn_b2, L0_ffn_edge_index)[0]
    x = x + _L1_gnn_ref(_layernorm(x, axis=-1), edge_index, L1_gnn_W1, L1_gnn_b1, L1_gnn_W2, L1_gnn_att_src, L1_gnn_att_dst, L1_gnn_b2)
    x = x + _L1_ffn_ref(_layernorm(x, axis=-1)[None], L1_ffn_Wr, L1_ffn_br, L1_ffn_W1, L1_ffn_b1, L1_ffn_g1, L1_ffn_be1, L1_ffn_m1, L1_ffn_v1, L1_ffn_W2, L1_ffn_b2, L1_ffn_g2, L1_ffn_be2, L1_ffn_m2, L1_ffn_v2, L1_ffn_Wo, L1_ffn_bo)[0]
    x = x + _L2_gnn_ref(_layernorm(x, axis=-1), edge_index, L2_gnn_W0, L2_gnn_a_src0, L2_gnn_a_dst0, L2_gnn_b0, L2_gnn_gamma0, L2_gnn_beta0, L2_gnn_W1, L2_gnn_a_src1, L2_gnn_a_dst1, L2_gnn_b1)
    x = x + _L2_ffn_ref(_layernorm(x, axis=-1)[None], L2_ffn_gate_w, L2_ffn_gate_b, L2_ffn_w1, L2_ffn_b1, L2_ffn_w2, L2_ffn_b2)[0]
    x = x + _L3_gnn_ref(_layernorm(x, axis=-1), edge_index, L3_gnn_W1, L3_gnn_b1, L3_gnn_g1, L3_gnn_be1, L3_gnn_W2, L3_gnn_b2, L3_gnn_g2, L3_gnn_be2, L3_gnn_W3, L3_gnn_b3, L3_gnn_g3, L3_gnn_be3, L3_gnn_W4, L3_gnn_b4, L3_gnn_g4, L3_gnn_be4, L3_gnn_W5, L3_gnn_b5, L3_gnn_g5, L3_gnn_be5)
    x = x + _L3_ffn_ref(_layernorm(x, axis=-1)[None], L3_ffn_router_w1, L3_ffn_router_b1, L3_ffn_router_w2, L3_ffn_router_b2, L3_ffn_expert_w1, L3_ffn_expert_b1, L3_ffn_expert_w2, L3_ffn_expert_b2, L3_ffn_expert_w3, L3_ffn_expert_b3)[0]
    return x

_drawn_inputs = setup_inputs


def setup_inputs(seed=0):
    import zlib

    import numpy as np

    out = dict(_drawn_inputs(seed))
    spreads = {'L0_gnn_b_gcn': (0.0, 0.1),
     'L0_ffn_b_gat': (0.0, 0.1),
     'L0_ffn_ln_gamma': (1.0, 0.2),
     'L0_ffn_ln_beta': (0.0, 0.1),
     'L0_ffn_b1': (0.0, 0.1),
     'L0_ffn_b2': (0.0, 0.1),
     'L1_gnn_b1': (0.0, 0.1),
     'L1_gnn_b2': (0.0, 0.1),
     'L1_ffn_br': (0.0, 0.3),
     'L1_ffn_b1': (0.0, 0.1),
     'L1_ffn_g1': (1.0, 0.2),
     'L1_ffn_be1': (0.0, 0.1),
     'L1_ffn_m1': (0.0, 0.1),
     'L1_ffn_v1': (1.0, 0.2),
     'L1_ffn_b2': (0.0, 0.1),
     'L1_ffn_g2': (1.0, 0.2),
     'L1_ffn_be2': (0.0, 0.1),
     'L1_ffn_m2': (0.0, 0.1),
     'L1_ffn_v2': (1.0, 0.2),
     'L1_ffn_bo': (0.0, 0.1),
     'L2_gnn_b0': (0.0, 2.0),
     'L2_gnn_gamma0': (1.0, 0.6),
     'L2_gnn_beta0': (0.0, 0.322),
     'L2_gnn_b1': (0.0, 0.293),
     'L2_ffn_gate_b': (0.0, 0.1),
     'L2_ffn_b1': (0.0, 0.546),
     'L2_ffn_b2': (0.0, 0.386),
     'L3_gnn_b1': (0.0, 2.0),
     'L3_gnn_g1': (1.0, 0.2),
     'L3_gnn_be1': (0.0, 0.1),
     'L3_gnn_b2': (0.0, 2.0),
     'L3_gnn_g2': (1.0, 0.2),
     'L3_gnn_be2': (0.0, 0.1),
     'L3_gnn_b3': (0.0, 2.0),
     'L3_gnn_g3': (1.0, 0.2),
     'L3_gnn_be3': (0.0, 0.1),
     'L3_gnn_b4': (0.0, 2.0),
     'L3_gnn_g4': (1.0, 0.2),
     'L3_gnn_be4': (0.0, 0.1),
     'L3_gnn_b5': (0.0, 2.0),
     'L3_gnn_g5': (1.0, 0.2),
     'L3_gnn_be5': (0.0, 0.1),
     'L3_ffn_router_b1': (0.0, 0.1),
     'L3_ffn_router_b2': (0.0, 0.1),
     'L3_ffn_expert_b1': (0.0, 0.8),
     'L3_ffn_expert_b2': (0.0, 0.403),
     'L3_ffn_expert_b3': (0.0, 0.1)}
    factors = {'L0_gnn_W_V': 200.0,
     'L1_gnn_att_src': 8.0,
     'L1_gnn_att_dst': 74.969,
     'L2_gnn_a_src0': 3.04,
     'L2_gnn_a_dst0': 6.739,
     'L2_gnn_a_dst1': 21.329,
     'L2_gnn_a_src1': 2.72}
    for name, (base, spread) in spreads.items():
        noise = np.random.default_rng([zlib.crc32(name.encode()), seed]).standard_normal(out[name].shape)
        drawn = base * np.exp(spread * noise) if base else spread * noise
        out[name] = jnp.asarray(drawn.astype(out[name].dtype))
    for name, factor in factors.items():
        out[name] = (out[name] * factor).astype(out[name].dtype)
    return out
```

```python
from contextlib import ExitStack, contextmanager

import concourse.bass as bass
from concourse import mybir

F32 = mybir.dt.float32
I32 = mybir.dt.int32
U32 = mybir.dt.uint32
U8 = mybir.dt.uint8
BF16 = mybir.dt.bfloat16
ALU = mybir.AluOpType
ACT = mybir.ActivationFunctionType
AX = mybir.AxisListType.X
ds = bass.ds

P = 128
N = 3125
T = -(-N // P)
NP = T * P
D = 256
KD = D // P
G1 = 5
N2 = 2048
T2 = N2 // P
G2 = 4
W = 8
E1 = 53125
NCH1 = 2 * W * -(-E1 // (2 * W * P))
E2 = 32768
NCH2 = E2 // P
FAR = -1e30
SLOPE = 0.2
SEM0 = 150


@contextmanager
def stage(nc, name, *names):
    with ExitStack() as cx:
        sems = [cx.enter_context(nc.semaphore(f"{name}_{s}", num=SEM0 + i)) for i, s in enumerate(names)]
        with nc.Block() as block:
            yield (block, *sems)
        nc.all_engine_barrier(sems_to_clear=range(SEM0, SEM0 + len(names)))


class Link:

    def __init__(self, eng, sem):
        self.eng, self.sem, self.n = eng, sem, 0

    def __call__(self, ins):
        self.n += 1
        ins.then_inc(self.sem, 1)
        self.eng.wait_ge(self.sem, self.n)


class Scope:

    def __init__(self, nc, tag):
        self.nc, self.tag, self.cx = nc, tag, ExitStack()

    def __enter__(self):
        return self

    def __exit__(self, *a):
        return self.cx.__exit__(*a)

    def sb(self, name, shape, dt=F32):
        return self.cx.enter_context(self.nc.sbuf_tensor(f"{self.tag}_{name}", shape, dt))

    def ps(self, name, shape, dt=F32):
        return self.cx.enter_context(self.nc.psum_tensor(f"{self.tag}_{name}", shape, dt))


def across(vec, n):
    return vec.rearrange("(o n) -> o n", o=1).to_broadcast([P, n])


def over_last(ap, n):
    a, t = ap.shape
    return ap.rearrange("p (t o) -> p t o", o=1).to_broadcast([a, t, n])


def over_mid(ap, t):
    a, n = ap.shape
    return ap.rearrange("p (o n) -> p o n", o=1).to_broadcast([a, t, n])



def count_edges(nc, tag, src, dst, nch, n_pad, table, key_rows, landed):
    nt = n_pad // P
    with Scope(nc, tag) as s:
        ids = s.sb("ids", [P, 2, nch], I32)
        key = s.sb("key", [P, nch])
        eye_rows = s.sb("eye_rows", [P, 2 * n_pad])
        keys = s.sb("keys", [P, 2, W * P])
        before = s.sb("before", [P, 2 * W * P], BF16)
        junk = s.sb("junk", [P, W * P], BF16)
        count = s.sb("count", [P, 2, W])
        early = s.sb("early", [P, W])
        move = s.sb("move", [P, W])
        spare = s.sb("spare", [P, W])
        cell = s.sb("cell", [P, 2, W], U32)
        with stage(nc, tag, "ids_in", "consts", "table_set", "keyed", "keys_out", "keys_in0", "keys_in1",
                   "keys_free", "cells_ready", "cells_free", "begun", "step") as (
                block, ids_in, consts, table_set, keyed, keys_out, keys_in0, keys_in1,
                keys_free, cells_ready, cells_free, begun, step):
            keys_in = [keys_in0, keys_in1]

            @block.sync
            def _(sp):
                with nc.allow_non_contiguous_dma(reason="one edge per partition"):
                    sp.dma_start(ids[:, 0, :], src.rearrange("(c p) -> p c", p=P)).then_inc(ids_in, 16)
                    sp.dma_start(ids[:, 1, :], dst.rearrange("(c p) -> p c", p=P)).then_inc(ids_in, 16)
                    sp.wait_ge(keyed, 1)
                    sp.dma_start(key_rows.rearrange("(c p) -> p c", p=P), key[:]).then_inc(keys_out, 16)
                sp.wait_ge(keys_out, 16)
                sp.sem_inc(keys_free, 2)
                with sp.Fori(0, nch // W // 2) as i:
                    for b in range(2):
                        sp.wait_ge(keys_free, 2 * i + b + 1)
                        sp.dma_start(keys[:, b, :], key_rows.rearrange("(o n) -> o n", o=1)[
                            :, ds((2 * i + b) * (W * P), W * P)].to_broadcast([P, W * P])).then_inc(keys_in[b], 16)

            @block.scalar
            def _(act):
                act.wait_ge(consts, 5)
                for t in range(nt):
                    act.dma_start(table[0:n_pad * n_pad, 0].rearrange("(r n) -> r n", n=n_pad)[t * P:(t + 1) * P, :],
                                  eye_rows[:, n_pad - t * P:2 * n_pad - t * P]).then_inc(table_set, 16)

            @block.gpsimd
            def _(pool):
                pool.memset(eye_rows[:], 0.0).then_inc(consts, 1)
                pool.memset(before[:], 1.0).then_inc(consts, 1)
                pool.iota(spare[:], pattern=[[P, W]], base=n_pad * n_pad, channel_multiplier=1,
                          allow_small_or_imprecise_dtypes=True).then_inc(consts, 1)
                pool.wait_ge(consts, 3)
                pool.affine_select(out=eye_rows[:], in_=eye_rows[:], compare_op=ALU.not_equal, fill=1.0,
                                   base=-n_pad, pattern=[[1, 2 * n_pad]], channel_multiplier=-1).then_inc(consts, 1)
                pool.affine_select(out=before[:], in_=before[:], compare_op=ALU.is_gt, fill=0.0, base=W * P,
                                   pattern=[[-1, 2 * W * P]], channel_multiplier=1).then_inc(consts, 1)
                pool.wait_ge(table_set, 16 * nt)
                pool.sem_inc(cells_free, 2)
                with pool.Fori(0, nch // W // 2) as i:
                    for b in range(2):
                        pool.wait_ge(cells_ready, 2 * i + b + 1)
                        pool.sem_inc(begun, 1)
                        for j in range(W):
                            pool.indirect_dma_start(
                                table, bass.IndirectOffsetOnAxis(ap=cell[:, b, j:j + 1], axis=0),
                                count[:, b, j:j + 1], None, compute_op=ALU.add,
                                bounds_check=n_pad * n_pad + W * P - 1, oob_is_err=True).then_inc(landed, 16)
                        pool.wait_ge(landed, (2 * i + b + 1) * (16 * W))
                        pool.sem_inc(cells_free, 1)

            @block.vector
            def _(dve):
                dve.wait_ge(ids_in, 32)
                dve.wait_ge(consts, 5)
                dve.scalar_tensor_tensor(out=key[:], in0=ids[:, 0, :], scalar=float(n_pad), in1=ids[:, 1, :],
                                         op0=ALU.mult, op1=ALU.add).then_inc(keyed, 1)
                dve.wait_ge(keyed, 1)
                dve.sem_inc(step, 1)
                steps = 2 * W + 4
                with dve.Fori(0, nch // W // 2) as i:
                    for b in range(2):
                        w = 2 * i + b
                        n = 1
                        dve.wait_ge(keys_in[b], (i + 1) * 16)
                        dve.wait_ge(cells_free, w + 1)
                        for j in range(W):
                            own = key[:, ds(w * W + j, 1)]
                            dve.wait_ge(step, w * steps + n)
                            dve.tensor_scalar(junk[:, 0:(W - j) * P], keys[:, b, j * P:W * P], own, 0.0,
                                              ALU.is_equal, ALU.add, accum_out=count[:, b, j:j + 1]).then_inc(step, 1)
                            dve.wait_ge(step, w * steps + n + 1)
                            dve.scalar_tensor_tensor(out=junk[:, 0:(j + 1) * P], in0=keys[:, b, 0:(j + 1) * P],
                                                     scalar=own, in1=before[:, (W - j) * P:(W + 1) * P],
                                                     op0=ALU.is_equal, op1=ALU.mult,
                                                     accum_out=early[:, j:j + 1]).then_inc(step, 1)
                            n += 2
                        dve.wait_ge(step, w * steps + n)
                        dve.sem_inc(keys_free, 1)
                        dve.tensor_scalar(early[:], early[:], 1.0, None, ALU.min).then_inc(step, 1)
                        dve.tensor_tensor(move[:], spare[:], key[:, ds(w * W, W)], ALU.subtract).then_inc(step, 1)
                        dve.wait_ge(step, w * steps + n + 2)
                        dve.tensor_tensor(move[:], move[:], early[:], ALU.mult).then_inc(step, 1)
                        dve.wait_ge(step, w * steps + n + 3)
                        dve.tensor_tensor(cell[:, b, :], move[:], key[:, ds(w * W, W)], ALU.add).then_inc(step, 1)
                        dve.wait_ge(step, w * steps + n + 4)
                        dve.sem_inc(cells_ready, 1)


def mask_and_degrees(nc, tag, table, nt, gt, far, ident, degree):
    n_pad = nt * P
    ngr = -(-nt // 4)
    table2 = table[0:n_pad * n_pad, 0].rearrange("(r n) -> r n", n=n_pad)
    with Scope(nc, tag) as s:
        panel = s.sb("panel", [P, gt, nt, P])
        turned = s.sb("turned", [P, ngr, 4 * P])
        mask = s.sb("mask", [P, gt, n_pad], BF16)
        part = s.sb("part", [P, nt, ngr])
        pt = s.ps("pt", [P, ngr, 4 * P])
        with stage(nc, tag, *[f"panel_in{u}" for u in range(gt)], *[f"mask_out{u}" for u in range(gt)],
                   "panel_free", "turned_ps", "copied", "masked", "summed") as (block, *sems):
            panel_in, mask_out = sems[:gt], sems[gt:2 * gt]
            panel_free, turned_ps, copied, masked, summed = sems[2 * gt:]

            @block.sync
            def _(sp):
                def load_panel(k, u):
                    sp.wait_ge(panel_free, k * gt + u + 1)
                    sp.dma_start(panel[:, u], table2[:, ds((k * gt + u) * P, P)].rearrange("(t p) d -> p t d", p=P)
                                 ).then_inc(panel_in[u], 16)

                def store_mask(k, u):
                    sp.wait_ge(masked, (k * gt + u + 2) * ngr)
                    sp.dma_start(far[ds((k * gt + u) * P, P), :], mask[:, u, :]).then_inc(mask_out[u], 16)

                for u in range(gt):
                    sp.sem_inc(mask_out[u], 16)
                    load_panel(0, u)
                with sp.Fori(1, nt // gt) as k:
                    for u in range(gt):
                        load_panel(k, u)
                        store_mask(k - 1, u)
                for u in range(gt):
                    store_mask(nt // gt - 1, u)
                for u in range(gt):
                    sp.wait_ge(mask_out[u], (nt // gt + 1) * 16)

            @block.tensor
            def _(pe):
                pe.sem_inc(panel_free, gt)
                with pe.Fori(0, nt // gt) as k:
                    for u in range(gt):
                        j = k * gt + u
                        pe.wait_ge(panel_in[u], (k + 1) * 16)
                        for q in range(ngr):
                            pe.wait_ge(copied, j * ngr + q + 1)
                            for t in range(4 * q, min(4 * q + 4, nt)):
                                last = pe.transpose(pt[:, q, (t - 4 * q) * P:(t - 4 * q + 1) * P], panel[:, u, t, :],
                                                    ident[:])
                            last.then_inc(turned_ps, 1)
                        pe.wait_ge(turned_ps, j * ngr + ngr)
                        pe.sem_inc(panel_free, 1)

            @block.scalar
            def _(act):
                act.sem_inc(copied, ngr)
                act.sem_inc(masked, ngr)
                with act.Fori(0, nt // gt) as k:
                    for u in range(gt):
                        j = k * gt + u
                        for q in range(ngr):
                            n = (min(4 * q + 4, nt) - 4 * q) * P
                            act.wait_ge(turned_ps, j * ngr + q + 1)
                            act.wait_ge(masked, j * ngr + q + 1)
                            act.activation(turned[:, q, 0:n], pt[:, q, 0:n], ACT.Copy,
                                           accum_out=part[:, ds(j, 1), q]).then_inc(copied, 1)

            @block.vector
            def _(dve):
                with dve.Fori(0, nt // gt) as k:
                    for u in range(gt):
                        j = k * gt + u
                        dve.wait_ge(mask_out[u], (k + 1) * 16)
                        for q in range(ngr):
                            n = (min(4 * q + 4, nt) - 4 * q) * P
                            dve.wait_ge(copied, j * ngr + q + 1 + ngr)
                            dve.tensor_scalar(mask[:, u, 4 * q * P:4 * q * P + n], turned[:, q, 0:n], 0.5, FAR,
                                              ALU.is_lt, ALU.mult).then_inc(masked, 1)
                dve.wait_ge(copied, (nt + 1) * ngr)
                if degree is not None:
                    dve.tensor_reduce(degree[:, 0:nt], part[:], AX, ALU.add).then_inc(summed, 1)



def layernorm(nc, tag, x, xn, unit=False):
    with Scope(nc, tag) as s:
        stats = s.sb("stats", [P, T, 6])
        mv = s.sb("mv", [P, T, 2])
        rstd = s.sb("rstd", [P, T])
        size = s.sb("size", [P, T])
        with stage(nc, tag, "stat", "agg", "eps", "root", "step", "done") as (block, stat, agg, eps, root, step, done):
            @block.vector
            def _(dve):
                link = Link(dve, step)
                with dve.Fori(0, T) as t:
                    dve.bn_stats(stats[:, ds(t, 1), :].rearrange("p a b -> p (a b)"),
                                 x[:, ds(t, 1), :].rearrange("p a b -> p (a b)")).then_inc(stat, 1)
                dve.wait_ge(stat, T)
                for t in range(T):
                    dve.bn_aggr(mv[:, t, :], stats[:, t, :]).then_inc(agg, 1)
                dve.wait_ge(agg, T)
                if unit:
                    dve.tensor_scalar(size[:], mv[:, :, 1], float(D), None, ALU.mult).then_inc(eps, 1)
                dve.tensor_scalar(rstd[:], mv[:, :, 1], 1e-5, None, ALU.add).then_inc(eps, 1)
                dve.wait_ge(root, 2 if unit else 1)
                link(dve.reciprocal(rstd[:], rstd[:]))
                if unit:
                    link(dve.tensor_tensor(size[:], size[:], rstd[:], ALU.mult))
                    link(dve.tensor_scalar(size[:], size[:], 1e-12, None, ALU.max))
                    link(dve.reciprocal(size[:], size[:]))
                    link(dve.tensor_tensor(rstd[:], rstd[:], size[:], ALU.mult))
                with dve.Fori(0, T) as t:
                    dve.tensor_scalar(xn[:, ds(t, 1), :].rearrange("p a b -> p (a b)"),
                                      x[:, ds(t, 1), :].rearrange("p a b -> p (a b)"),
                                      mv[:, ds(t, 1), 0], rstd[:, ds(t, 1)],
                                      ALU.subtract, ALU.mult).then_inc(done, 1)

            @block.scalar
            def _(act):
                if unit:
                    act.wait_ge(eps, 1)
                    act.activation(size[:], size[:], ACT.Sqrt).then_inc(root, 1)
                act.wait_ge(eps, 2 if unit else 1)
                act.activation(rstd[:], rstd[:], ACT.Sqrt).then_inc(root, 1)


def turn(nc, tag, nm, fm, ident, bias=None, func=ACT.Identity):
    with Scope(nc, tag) as s:
        pt = s.ps("pt", [P, 4, KD, 2 * P])
        with stage(nc, tag, "turned", "out") as (block, turned, out):
            pairs = [(t, min(2, T - t)) for t in range(0, T, 2)]

            @block.tensor
            def _(pe):
                for i, (t, n) in enumerate(pairs):
                    if i >= 4:
                        pe.wait_ge(out, i - 3)
                    for j in range(n):
                        for k in range(KD):
                            last = pe.transpose(pt[:, i % 4, k, j * P:(j + 1) * P], nm[:, t + j, k * P:(k + 1) * P],
                                                ident[:])
                    last.then_inc(turned, 1)

            @block.scalar
            def _(act):
                for i, (t, n) in enumerate(pairs):
                    act.wait_ge(turned, i + 1)
                    if bias is None:
                        last = act.activation(fm[:, :, t * P:(t + n) * P], pt[:, i % 4, :, 0:n * P], func)
                    else:
                        for k in range(KD):
                            last = act.activation(fm[:, k, t * P:(t + n) * P], pt[:, i % 4, k, 0:n * P], func,
                                                  bias=bias[:, k:k + 1])
                    last.then_inc(out, 1)


def product_nm(nc, tag, fm, w, width, store):
    kk = w.shape[1]
    with Scope(nc, tag) as s:
        acc = s.ps("acc", [P, 8, 512])
        with stage(nc, tag, "done", "stored") as (block, done, stored):
            @block.tensor
            def _(pe):
                for t in range(T):
                    if t >= 8:
                        pe.wait_ge(stored, t - 7)
                    for k in range(kk):
                        last = pe.matmul(acc[:, t % 8, 0:width], fm[:, k, t * P:(t + 1) * P], w[:, k, :],
                                         start=(k == 0), stop=(k == kk - 1))
                    last.then_inc(done, 1)

            @block.vector
            def _(dve):
                for t in range(T):
                    dve.wait_ge(done, t + 1)
                    store(dve, t, acc[:, t % 8, 0:width]).then_inc(stored, 1)


def product_fm(nc, tag, srcs, w, dst, func, bias):
    kk, m_all = w.shape[1], w.shape[2]
    mm = m_all // P
    n = 400
    with Scope(nc, tag) as s:
        acc = s.ps("acc", [P, 2, mm, 512])
        with stage(nc, tag, "done", "stored") as (block, done, stored):
            @block.tensor
            def _(pe):
                pe.sem_inc(stored, 2 * mm)
                with pe.Fori(0, NP // n // 2) as i:
                    for b in range(2):
                        for m in range(mm):
                            pe.wait_ge(stored, (2 * i + b) * mm + m + 1)
                            for k in range(kk):
                                last = pe.matmul(acc[:, b, m, 0:n], w[:, k, m * P:(m + 1) * P],
                                                 srcs[k][:, ds((2 * i + b) * n, n)], start=(k == 0), stop=(k == kk - 1))
                            last.then_inc(done, 1)

            @block.scalar
            def _(act):
                with act.Fori(0, NP // n // 2) as i:
                    for b in range(2):
                        for m in range(mm):
                            act.wait_ge(done, (2 * i + b) * mm + m + 1)
                            act.activation(dst[:, m, ds((2 * i + b) * n, n)], acc[:, b, m, 0:n], func,
                                           bias=bias[:, m:m + 1]).then_inc(stored, 1)


def load(nc, tag, *pairs):
    with stage(nc, tag, "loaded") as (block, loaded):
        @block.sync
        def _(sp):
            with nc.allow_non_contiguous_dma(reason="short vectors by columns"):
                for dst, src in pairs:
                    sp.dma_start(dst, src).then_inc(loaded, 16)
            sp.wait_ge(loaded, 16 * len(pairs))


def columns_to_rows(nc, tag, cols, n, ident, dram, rows):
    with Scope(nc, tag) as s:
        pt = s.ps("pt", [P, P])
        flat = s.sb("flat", [P, P])
        with stage(nc, tag, "turned", "copied", "moved") as (block, turned, copied, moved):
            @block.tensor
            def _(pe):
                pe.transpose(pt[0:n, :], cols, ident[:]).then_inc(turned, 1)

            @block.vector
            def _(dve):
                dve.wait_ge(turned, 1)
                dve.tensor_copy(flat[0:n, :], pt[0:n, :]).then_inc(copied, 1)

            @block.sync
            def _(sp):
                sp.wait_ge(copied, 1)
                sp.dma_start(dram[0:n * P].rearrange("(q p) -> q p", p=P), flat[0:n, :]).then_inc(moved, 16)
                sp.wait_ge(moved, 16)
                sp.dma_start(rows, across(dram[0:n * P], n * P)).then_inc(moved, 16)
                sp.wait_ge(moved, 32)



def aggregate(nc, tag, c, table, nt, gt, rhs, width, out, scale=None, attention=None, eps=0.0):
    n_pad = nt * P
    ng = nt // gt
    cols = gt * P
    table2 = table[0:n_pad * n_pad, 0].rearrange("(r n) -> r n", n=n_pad)
    with Scope(nc, tag) as s:
        counts = s.sb("counts", [P, gt, cols])
        narrow = width <= P
        acc = s.ps("acc", [P, 2 if narrow else gt, 512])
        if narrow:
            half = cols // 2
            flat = s.sb("flat", [width, cols])
            back = s.ps("back", [P, gt, width])
        if attention:
            rows, es, es2 = attention
            p = s.sb("p", [P, gt, cols])
            total = s.sb("total", [P, gt])
            warm = s.sb("warm", [P, 1])
        with stage(nc, tag, *[f"counts_in{u}" for u in range(gt)], "counts_free", "sums_ready", "sums_free",
                   "low_ready", "score_ready", "exp_ready", "clamped", "weighted_dve", "weighted_pool", "step",
                   "flat_ready", "back_ready", "begun", "begun_pe") as (
                block, *sems):
            counts_in = sems[:gt]
            (counts_free, sums_ready, sums_free, low_ready, score_ready, exp_ready, clamped, weighted_dve,
             weighted_pool, step, flat_ready, back_ready,
             begun, begun_pe) = sems[gt:]
            weighted = [weighted_dve, weighted_pool]
            pool_slots = (0,)

            def by_pool(u):
                return u in pool_slots

            def nth(u, round_):
                mine = [v for v in range(gt) if by_pool(v) == by_pool(u)]
                return round_ * len(mine) + mine.index(u)

            @block.sync
            def _(sp):
                with sp.Fori(0, ng) as g:
                    with sp.Fori(0, ng) as k:
                        for u in range(gt):
                            sp.wait_ge(counts_free, (g * ng + k) * gt + u + 1)
                            sp.dma_start(counts[:, u, :], table2[ds((k * gt + u) * P, P), ds(g * cols, cols)]
                                         ).then_inc(counts_in[u], 16)

            def narrow_group(pe, g):
                for t in range(nt):
                    u = t % gt
                    pe.wait_ge(weighted[by_pool(u)], nth(u, g * ng + t // gt + 1) + 1)
                    for j in range(2):
                        last = pe.matmul(acc[0:width, j, 0:half], rhs(t), counts[:, u, j * half:(j + 1) * half],
                                         start=(t == 0), stop=(t == nt - 1), skip_group_check=True)
                    last.then_inc(counts_free, 1)
                pe.wait_ge(counts_free, (g + 1) * nt + gt)
                pe.sem_inc(sums_ready, 1)
                pe.wait_ge(flat_ready, g + 1)
                pe.sem_inc(begun_pe, 1)
                for j in range(gt):
                    last = pe.transpose(back[:, j, :], flat[:, j * P:(j + 1) * P], c.ident[0:width, 0:width])
                last.then_inc(back_ready, 1)

            def wide_group(pe, g):
                for j in range(gt):
                    pe.matmul(acc[:, j, 0:width], c.zero[0:1, 0:P], c.zero[0:1, 0:width], start=True, stop=False,
                              skip_group_check=True)
                with pe.Fori(0, ng) as k:
                    for u in range(gt):
                        if attention:
                            pe.wait_ge(weighted[by_pool(u)], nth(u, g * ng + k + 1) + 1)
                        else:
                            pe.wait_ge(counts_in[u], (g * ng + k + 1) * 16)
                        for j in range(gt):
                            last = pe.matmul(acc[:, j, 0:width], counts[:, u, j * P:(j + 1) * P],
                                             rhs(k * gt + u), start=False, stop=False, skip_group_check=True)
                        last.then_inc(counts_free, 1)
                for j in range(gt):
                    last = pe.matmul(acc[:, j, 0:width], c.zero[0:1, 0:P], c.zero[0:1, 0:width], start=False,
                                     stop=True, skip_group_check=True)
                last.then_inc(sums_ready, 1)

            @block.tensor
            def _(pe):
                pe.sem_inc(counts_free, gt)
                pe.sem_inc(sums_free, 1)
                if attention:
                    pe.sem_inc(weighted_pool, len(pool_slots))
                    pe.sem_inc(weighted_dve, gt - len(pool_slots))
                with pe.Fori(0, ng) as g:
                    pe.wait_ge(sums_free, g + 1)
                    (narrow_group if narrow else wide_group)(pe, g)

            if attention:
                @block.gpsimd
                def _(pool):
                    with pool.Fori(0, ng) as g:
                        with pool.Fori(0, ng) as k:
                            for u in pool_slots:
                                pool.wait_ge(exp_ready, (g * ng + k) * gt + u + 1)
                                pool.sem_inc(begun, 1)
                                pool.tensor_scalar(p[:, u, :], p[:, u, :], 1.0, None, ALU.min).then_inc(clamped, 1)
                                pool.wait_ge(counts_in[u], (g * ng + k + 1) * 16)
                                pool.wait_ge(clamped, nth(u, g * ng + k) + 1)
                                pool.tensor_tensor(counts[:, u, :], p[:, u, :], counts[:, u, :], ALU.mult
                                                   ).then_inc(weighted_pool, 1)

                @block.scalar
                def _(act):
                    act.activation(warm[:], c.ident[:, 0:1], ACT.Exp)
                    with act.Fori(0, ng) as g:
                        with act.Fori(0, ng) as k:
                            at = (g * ng + k) * gt
                            for u in range(gt):
                                act.wait_ge(weighted[by_pool(u)], nth(u, g * ng + k) + 1)
                                act.activation(p[:, u, :], rows[:, 1, ds(g * cols, cols)], ACT.Identity,
                                               bias=es2[:, ds(k * gt + u, 1)]).then_inc(low_ready, 1)
                            for u in range(gt):
                                act.wait_ge(score_ready, at + u + 1)
                                act.activation(p[:, u, :], p[:, u, :], ACT.Exp).then_inc(exp_ready, 1)

            @block.vector
            def _(dve):
                dve.sem_inc(step, 1)
                with dve.Fori(0, ng) as g:
                    if attention:
                        with dve.Fori(0, ng) as k:
                            at = (g * ng + k) * gt
                            for u in range(gt):
                                dve.wait_ge(low_ready, at + u + 1)
                                dve.scalar_tensor_tensor(out=p[:, u, :], in0=rows[:, 0, ds(g * cols, cols)],
                                                         scalar=es[:, ds(k * gt + u, 1)], in1=p[:, u, :],
                                                         op0=ALU.add, op1=ALU.max).then_inc(score_ready, 1)
                            for u in range(gt):
                                if by_pool(u):
                                    continue
                                dve.wait_ge(exp_ready, at + u + 1)
                                dve.wait_ge(counts_in[u], (g * ng + k + 1) * 16)
                                dve.scalar_tensor_tensor(out=counts[:, u, :], in0=p[:, u, :], scalar=1.0,
                                                         in1=counts[:, u, :], op0=ALU.min, op1=ALU.mult
                                                         ).then_inc(weighted_dve, 1)
                    dve.wait_ge(sums_ready, g + 1)
                    sums = acc
                    if narrow:
                        dve.tensor_copy(flat[:].rearrange("w (j n) -> w j n", j=2), acc[0:width, :, 0:half]
                                        ).then_inc(flat_ready, 1)
                        dve.wait_ge(back_ready, g + 1)
                        sums = back
                    if attention:
                        f = width - 1
                        dve.tensor_scalar(total[:], sums[:, :, f], eps, None, ALU.add).then_inc(step, 1)
                        dve.wait_ge(step, 2 * g + 2)
                        dve.reciprocal(total[:], total[:]).then_inc(step, 1)
                        dve.wait_ge(step, 2 * g + 3)
                        for j in range(gt):
                            last = dve.tensor_scalar(out(g * gt + j), sums[:, j, 0:f], total[:, j:j + 1], None, ALU.mult)
                    else:
                        for j in range(gt):
                            if scale is None:
                                last = dve.tensor_copy(out(g * gt + j), acc[:, j, 0:width])
                            else:
                                last = dve.tensor_scalar(out(g * gt + j), acc[:, j, 0:width],
                                                         scale[:, ds(g * gt + j, 1)], None, ALU.mult)
                    last.then_inc(sums_free, 1)


def neighbour_max(nc, tag, far, nt, gt, heads, es_rows, smax):
    n_pad = nt * P
    with Scope(nc, tag) as s:
        mask = s.sb("mask", [P, gt, n_pad], BF16)
        junk = s.sb("junk", [P, n_pad], BF16)
        with stage(nc, tag, *[f"mask_in{u}" for u in range(gt)], "seen") as (block, *sems):
            mask_in, seen = sems[:gt], sems[gt]

            @block.sync
            def _(sp):
                for t in range(nt):
                    if t >= gt:
                        sp.wait_ge(seen, (t - gt + 1) * heads)
                    sp.dma_start(mask[:, t % gt, :], far[t * P:(t + 1) * P, :]).then_inc(mask_in[t % gt], 16)

            @block.vector
            def _(dve):
                link = Link(dve, seen)
                for t in range(nt):
                    dve.wait_ge(mask_in[t % gt], (t // gt + 1) * 16)
                    for h in range(heads):
                        link(dve.tensor_tensor_reduce(junk[:], es_rows[:, h, :], mask[:, t % gt, :], 1.0, -3e38,
                                                      ALU.add, ALU.max, smax[:, h, t:t + 1]))


def gat(nc, tag, c, fm, w, w_cols, a_src, a_dst, heads, table, far, nt, gt, dram, out_tile, eps, tail=None):
    ch = w_cols // heads
    n_pad = nt * P
    with Scope(nc, tag) as s:
        h = s.sb("h", [P, T, heads, ch + 1])
        ec = s.sb("ec", [P, 2 * heads, nt])
        smax = s.sb("smax", [P, heads, nt])
        es2 = s.sb("es2", [P, heads, nt])
        shift = s.sb("shift", [P, heads, 2, nt])
        with Scope(nc, tag + "w") as q:
            wx = q.sb("wx", [P, KD, w_cols + 2 * heads])
            att = q.sb("att", [P, 2, w_cols])
            prod = q.sb("prod", [P, KD, 2, w_cols])
            load(nc, tag + "_load", (wx[:, :, 0:w_cols], w.rearrange("(k p) n -> p k n", p=P)),
                 (att[:, 0, :], across(a_src, w_cols)), (att[:, 1, :], across(a_dst, w_cols)))
            with stage(nc, tag + "_wa", "mul", "red") as (block, mul, red):
                @block.vector
                def _(dve):
                    for k in range(KD):
                        for a in range(2):
                            dve.tensor_tensor(prod[:, k, a, :], wx[:, k, 0:w_cols], att[:, a, :], ALU.mult).then_inc(mul, 1)
                    dve.wait_ge(mul, 2 * KD)
                    for k in range(KD):
                        for a in range(2):
                            dve.tensor_reduce(wx[:, k, w_cols + a * heads:w_cols + (a + 1) * heads],
                                              prod[:, k, a, :].rearrange("p (h c) -> p h c", h=heads), AX, ALU.add
                                              ).then_inc(red, 1)
                    dve.memset(h[:, :, :, ch:ch + 1], 1.0)

            def store(dve, t, ps):
                if t < nt:
                    dve.tensor_copy(ec[:, :, t], ps[:, w_cols:w_cols + 2 * heads])
                if t >= nt and tail is not None:
                    dve.tensor_copy(tail(t), ps[:, 0:w_cols])
                return dve.tensor_copy(h[:, t, :, 0:ch], ps[:, 0:w_cols].rearrange("p (h c) -> p h c", h=heads))

            product_nm(nc, tag + "_h", fm, wx, w_cols + 2 * heads, store)
        with Scope(nc, tag + "m") as q:
            es_rows = q.sb("es_rows", [P, heads, n_pad])
            columns_to_rows(nc, tag + "_es", ec[:, 0:heads, :].rearrange("p h t -> p (h t)"), heads * nt, c.ident, dram,
                            es_rows[:].rearrange("p h n -> p (h n)"))
            neighbour_max(nc, tag + "_max", far, nt, gt, heads, es_rows, smax)
        with stage(nc, tag + "_shift", "step") as (block, step):
            @block.vector
            def _(dve):
                link = Link(dve, step)
                ed = ec[:, heads:2 * heads, :]
                link(dve.tensor_tensor(smax[:], smax[:], ed, ALU.add))
                link(dve.scalar_tensor_tensor(out=smax[:], in0=smax[:], scalar=SLOPE, in1=smax[:], op0=ALU.mult, op1=ALU.max))
                link(dve.tensor_tensor(shift[:, :, 0, :], ed, smax[:], ALU.subtract))
                link(dve.scalar_tensor_tensor(out=shift[:, :, 1, :], in0=ed, scalar=SLOPE, in1=smax[:], op0=ALU.mult,
                                              op1=ALU.subtract))
                link(dve.tensor_scalar(es2[:], ec[:, 0:heads, :], SLOPE, None, ALU.mult))
        with Scope(nc, tag + "r") as q:
            rows = q.sb("rows", [P, 2, n_pad])
            for i in range(heads):
                columns_to_rows(nc, f"{tag}_rows{i}", shift[:, i, :, :].rearrange("p a t -> p (a t)"), 2 * nt, c.ident,
                                dram, rows[:].rearrange("p a n -> p (a n)"))
                aggregate(nc, f"{tag}_agg{i}", c, table, nt, gt,
                          lambda t, i=i: h[:, ds(t, 1), i, :].rearrange("p a c -> p (a c)"), ch + 1,
                          lambda t, i=i: out_tile(t, i), attention=(rows, ec[:, i, :], es2[:, i, :]), eps=eps)



def first_max(dve, link, s, n, prio, top, onehot, tmp):
    link(dve.tensor_reduce(top[:], s[:], AX, ALU.max))
    link(dve.tensor_tensor(onehot[:], s[:], over_last(top[:], n), ALU.is_equal))
    link(dve.tensor_tensor(onehot[:], onehot[:], over_mid(prio[:, 0:n], T), ALU.mult))
    link(dve.tensor_reduce(tmp[:], onehot[:], AX, ALU.max))
    link(dve.tensor_tensor(onehot[:], onehot[:], over_last(tmp[:], n), ALU.is_equal))


def top2_gates(nc, tag, c, score, n, gate):
    with Scope(nc, tag) as s:
        prio = s.sb("prio", [P, n])
        top = s.sb("top", [P, T])
        top_b = s.sb("top_b", [P, T])
        one = s.sb("one", [P, T, n])
        tmp = s.sb("tmp", [P, T])
        ratio = s.sb("ratio", [P, T])
        with stage(nc, tag, "prio_set", "step", "diff", "expd") as (block, prio_set, step, diff, expd):
            @block.gpsimd
            def _(pool):
                pool.iota(prio[:], pattern=[[-1, n]], base=n, channel_multiplier=0,
                          allow_small_or_imprecise_dtypes=True).then_inc(prio_set, 1)

            @block.vector
            def _(dve):
                link = Link(dve, step)
                dve.wait_ge(prio_set, 1)
                first_max(dve, link, score, n, prio, top, gate, tmp)
                link(dve.scalar_tensor_tensor(out=score[:], in0=gate[:], scalar=-3e38, in1=score[:], op0=ALU.mult,
                                              op1=ALU.add))
                first_max(dve, link, score, n, prio, top_b, one, tmp)
                link(dve.tensor_tensor(ratio[:], top_b[:], top[:], ALU.subtract))
                dve.sem_inc(diff, 1)
                dve.wait_ge(expd, 1)
                link(dve.tensor_scalar(tmp[:], ratio[:], 1.0, None, ALU.add))
                link(dve.reciprocal(tmp[:], tmp[:]))
                link(dve.tensor_tensor(ratio[:], ratio[:], tmp[:], ALU.mult))
                link(dve.tensor_tensor(gate[:], gate[:], over_last(tmp[:], n), ALU.mult))
                link(dve.tensor_tensor(one[:], one[:], over_last(ratio[:], n), ALU.mult))
                link(dve.tensor_tensor(gate[:], gate[:], one[:], ALU.add))

            @block.scalar
            def _(act):
                act.wait_ge(diff, 1)
                act.activation(ratio[:], ratio[:], ACT.Exp).then_inc(expd, 1)


def softmax(nc, tag, logit, n, bias):
    with Scope(nc, tag) as s:
        top = s.sb("top", [P, T])
        with stage(nc, tag, "step", "shifted", "expd") as (block, step, shifted, expd):
            @block.vector
            def _(dve):
                link = Link(dve, step)
                link(dve.tensor_tensor(logit[:], logit[:], over_mid(bias[:], T), ALU.add))
                link(dve.tensor_reduce(top[:], logit[:], AX, ALU.max))
                dve.tensor_tensor(logit[:], logit[:], over_last(top[:], n), ALU.subtract).then_inc(shifted, 1)
                dve.wait_ge(expd, 1)
                link(dve.tensor_reduce(top[:], logit[:], AX, ALU.add))
                link(dve.reciprocal(top[:], top[:]))
                link(dve.tensor_tensor(logit[:], logit[:], over_last(top[:], n), ALU.mult))

            @block.scalar
            def _(act):
                act.wait_ge(shifted, 1)
                act.activation(logit[:], logit[:], ACT.Exp).then_inc(expd, 1)


def turn_gates(nc, tag, c, gate, n, gate_fm):
    with Scope(nc, tag) as s:
        pt = s.ps("pt", [n, 4, 4 * P])
        with stage(nc, tag, "turned", "out") as (block, turned, out):
            quads = [(t, min(4, T - t)) for t in range(0, T, 4)]

            @block.tensor
            def _(pe):
                for i, (t, m) in enumerate(quads):
                    if i >= 4:
                        pe.wait_ge(out, i - 3)
                    for j in range(m):
                        last = pe.transpose(pt[:, i % 4, j * P:(j + 1) * P], gate[:, t + j, :], c.ident[:])
                    last.then_inc(turned, 1)

            @block.vector
            def _(dve):
                for i, (t, m) in enumerate(quads):
                    dve.wait_ge(turned, i + 1)
                    dve.tensor_copy(gate_fm[:, t * P:(t + m) * P], pt[:, i % 4, 0:m * P]).then_inc(out, 1)


def experts(nc, tag, c, fm, x, gate, n_e, layers, last_w, last_bias):
    half = G1 * P // 2
    chunk = G1 * P
    nh = [2 if i == 0 else 1 for i in range(len(layers))]
    blocks = sum(m for _, _, m, _, _, _ in layers)
    k_last = layers[-1][2]
    with Scope(nc, tag) as s:
        gate_fm = s.sb("gate_fm", [n_e, NP])
        turn_gates(nc, tag + "_gt", c, gate, n_e, gate_fm)
        gate_c = s.sb("gate_c", [n_e, 2, chunk])
        hid = [s.sb(f"hid{i}", [P, nh[i], m, chunk]) for i, (_, _, m, _, _, _) in enumerate(layers)]
        ph = s.ps("ph", [P, 2, 2, 512])
        py = s.ps("py", [P, 4, 512])
        with stage(nc, tag, "gate_in", "gate_free", "hid_ready", "hid_read", *[f"act{i}" for i in range(len(layers))],
                   *[f"used{i}" for i in range(len(layers))], "y_ready", "y_free") as (block, *sems):
            gate_in, gate_free, hid_ready, hid_read = sems[:4]
            nl = len(layers)
            acted, used = sems[4:4 + nl], sems[4 + nl:4 + 2 * nl]
            y_ready, y_free = sems[4 + 2 * nl:]

            order = [(0, 0)]
            for e in range(n_e):
                order += [(i, e) for i in range(1, min(2, nl))]
                order += [(0, e + 1)] * (e + 1 < n_e)
                order += [(i, e) for i in range(2, nl)] + [("y", e)]

            @block.gpsimd
            def _(pool):
                with pool.Fori(0, T // G1) as g:
                    pool.wait_ge(gate_free, g + 1)
                    pool.tensor_copy(gate_c[:, 0, :], gate_fm[:, ds(g * chunk, chunk)]).then_inc(gate_in, 1)

            @block.tensor
            def _(pe):
                pe.sem_inc(hid_read, 2)
                pe.sem_inc(y_free, 5)
                pe.sem_inc(gate_free, 1)
                for i in range(nl):
                    pe.sem_inc(used[i], nh[i])
                with pe.Fori(0, T // G1) as g:
                    pe.wait_ge(gate_in, g + 1)
                    for tt in range(G1):
                        pe.wait_ge(y_free, g * (G1 * (n_e + 1)) + max(tt + 2, 5))
                        last = pe.matmul(py[:, tt % 4, 0:D], gate_c[:, 0, tt * P:(tt + 1) * P], last_bias[:],
                                         start=True, stop=True)
                        last.then_inc(y_ready, 1)
                    pe.wait_ge(y_ready, g * (G1 * (n_e + 1)) + G1)
                    pe.sem_inc(gate_free, 1)
                    nb, ny = 0, G1
                    for kind, e in order:
                        if kind == "y":
                            pe.wait_ge(acted[-1], g * (n_e * k_last) + (e + 1) * k_last)
                            for tt in range(G1):
                                pe.wait_ge(y_free, g * (G1 * (n_e + 1)) + ny + 2)
                                for k in range(k_last):
                                    last = pe.matmul(py[:, ny % 4, 0:D], hid[-1][:, e % nh[-1], k, tt * P:(tt + 1) * P],
                                                     last_w[:, e, k, :], start=(k == 0), stop=(k == k_last - 1))
                                last.then_inc(y_ready, 1)
                                ny += 1
                            pe.wait_ge(y_ready, g * (G1 * (n_e + 1)) + ny)
                            pe.sem_inc(used[-1], 1)
                            continue
                        w, kk, mm, _, _, _ = layers[kind]
                        if kind:
                            km = layers[kind - 1][2]
                            pe.wait_ge(acted[kind - 1], g * (n_e * km) + (e + 1) * km)
                        for m in range(mm):
                            pe.wait_ge(hid_read, g * (blocks * n_e) + nb + 1)
                            for j in range(2):
                                for k in range(kk):
                                    rhs = (fm[:, k, ds(g * chunk + j * half, half)] if kind == 0 else
                                           hid[kind - 1][:, e % nh[kind - 1], k, j * half:(j + 1) * half])
                                    last = pe.matmul(ph[:, nb % 2, j, 0:half], w[:, e, k, m * P:(m + 1) * P], rhs,
                                                     start=(k == 0), stop=(k == kk - 1))
                            last.then_inc(hid_ready, 1)
                            nb += 1
                        if kind:
                            pe.wait_ge(hid_ready, g * (blocks * n_e) + nb)
                            pe.sem_inc(used[kind - 1], 1)

            @block.scalar
            def _(act):
                with act.Fori(0, T // G1) as g:
                    nb = 0
                    for kind, e in order:
                        if kind == "y":
                            continue
                        _, _, mm, func, scale, bias = layers[kind]
                        act.wait_ge(used[kind], g * n_e + e + 1)
                        for m in range(mm):
                            act.wait_ge(hid_ready, g * (blocks * n_e) + nb + 1)
                            act.activation(hid[kind][:, e % nh[kind], m, :].rearrange("p (j n) -> p j n", j=2),
                                           ph[:, nb % 2, :, 0:half], func, bias=bias[:, e, m:m + 1],
                                           scale=1.0 if scale is None else scale[:, e, m:m + 1]
                                           ).then_inc(acted[kind], 1)
                            act.wait_ge(acted[kind], g * (n_e * mm) + e * mm + m + 1)
                            act.sem_inc(hid_read, 1)
                            nb += 1

            @block.vector
            def _(dve):
                with dve.Fori(0, T // G1) as g:
                    ny = 0
                    for e in range(-1, n_e):
                        for tt in range(G1):
                            xt = x[:, ds(g * G1 + tt, 1), :].rearrange("p a d -> p (a d)")
                            at = g * (G1 * (n_e + 1)) + ny
                            dve.wait_ge(y_ready, at + 1)
                            dve.wait_ge(y_free, at + 1)
                            if e < 0:
                                ins = dve.tensor_tensor(xt, py[:, ny % 4, 0:D], xt, ALU.add)
                            else:
                                ins = dve.scalar_tensor_tensor(
                                    out=xt, in0=py[:, ny % 4, 0:D], scalar=gate[:, ds(g * G1 + tt, 1), e], in1=xt,
                                    op0=ALU.mult, op1=ALU.add)
                            ins.then_inc(y_free, 1)
                            ny += 1



def finish_rows(nc, tag, x, a, bias, relu, unit):
    with Scope(nc, tag) as s:
        sq = s.sb("sq", [P, 2, D])
        ss = s.sb("ss", [P, T])
        with stage(nc, tag, "biased", "squared", "root", "step", "added") as (block, biased, squared, root, step, added):
            @block.vector
            def _(dve):
                link = Link(dve, step)
                if bias is not None:
                    link(dve.tensor_tensor(a[:], a[:], over_mid(bias[:], T), ALU.add))
                if relu:
                    link(dve.tensor_scalar(a[:], a[:], 0.0, None, ALU.max))
                dve.sem_inc(biased, 1)
                if not unit:
                    link(dve.tensor_tensor(x[:], x[:], a[:], ALU.add))
                    return
                dve.wait_ge(root, 1)
                link(dve.tensor_scalar(ss[:], ss[:], 1e-12, None, ALU.max))
                link(dve.reciprocal(ss[:], ss[:]))
                with dve.Fori(0, T) as t:
                    xt = x[:, ds(t, 1), :].rearrange("p a d -> p (a d)")
                    dve.scalar_tensor_tensor(out=xt, in0=a[:, ds(t, 1), :].rearrange("p a d -> p (a d)"),
                                             scalar=ss[:, ds(t, 1)], in1=xt, op0=ALU.mult, op1=ALU.add).then_inc(added, 1)

            if unit:
                @block.scalar
                def _(act):
                    act.wait_ge(biased, 1)
                    for t in range(T):
                        if t >= 2:
                            act.wait_ge(squared, t - 1)
                        act.activation(sq[:, t % 2, :], a[:, t, :], ACT.Square, accum_out=ss[:, t:t + 1]).then_inc(squared, 1)
                    act.wait_ge(squared, T)
                    act.activation(ss[:], ss[:], ACT.Sqrt).then_inc(root, 1)


def batchnorm_columns(nc, tag, fm, gamma, beta, scale, shift):
    n = 500
    nb = -(-N // n)
    with Scope(nc, tag) as s:
        stats = s.sb("stats", [P, KD, nb, 6])
        mv = s.sb("mv", [P, KD, 2])
        with stage(nc, tag, "stat", "eps", "root", "step") as (block, stat, eps, root, step):
            @block.vector
            def _(dve):
                link = Link(dve, step)
                for k in range(KD):
                    for b in range(nb):
                        dve.bn_stats(stats[:, k, b, :], fm[:, k, b * n:min((b + 1) * n, N)]).then_inc(stat, 1)
                dve.wait_ge(stat, KD * nb)
                for k in range(KD):
                    link(dve.bn_aggr(mv[:, k, :], stats[:, k].rearrange("p b s -> p (b s)")))
                dve.tensor_scalar(scale[:], mv[:, :, 1], 1e-5, None, ALU.add).then_inc(eps, 1)
                dve.wait_ge(root, 1)
                link(dve.reciprocal(scale[:], scale[:]))
                link(dve.tensor_tensor(scale[:], scale[:], gamma[:], ALU.mult))
                link(dve.tensor_tensor(shift[:], mv[:, :, 0], scale[:], ALU.mult))
                link(dve.tensor_tensor(shift[:], beta[:], shift[:], ALU.subtract))

            @block.scalar
            def _(act):
                act.wait_ge(eps, 1)
                act.activation(scale[:], scale[:], ACT.Sqrt).then_inc(root, 1)


def scale_relu(nc, tag, fm, scale, shift):
    with stage(nc, tag, "done") as (block, done):
        @block.scalar
        def _(act):
            act.activation(fm[:, 0, :], fm[:, 0, :], ACT.Relu, bias=shift[:, 0:1], scale=scale[:, 0:1]).then_inc(done, 1)

        @block.vector
        def _(dve):
            dve.tensor_scalar(fm[:, 1, :], fm[:, 1, :], scale[:, 1:2], shift[:, 1:2], ALU.mult, ALU.add).then_inc(done, 1)
            dve.wait_ge(done, 1)
            dve.wait_ge(done, 2)
            dve.tensor_scalar(fm[:, 1, :], fm[:, 1, :], 0.0, None, ALU.max)


class Consts:
    pass


def vec_cols(v):
    return v.rearrange("(m p) -> p m", p=P)


def build(nc, a, out):
    size1, size2 = NP * NP + W * P, N2 * N2 + W * P
    table1 = nc.dram_tensor("table1", (size1, 1), F32, kind="Internal").ap()
    table2 = nc.dram_tensor("table2", (size2, 1), F32, kind="Internal").ap()
    far1 = nc.dram_tensor("far1", (NP, NP), BF16, kind="Internal").ap()
    far2 = nc.dram_tensor("far2", (N2, N2), BF16, kind="Internal").ap()
    keys1 = nc.dram_tensor("keys1", (NCH1 * P,), F32, kind="Internal").ap()
    keys2 = nc.dram_tensor("keys2", (NCH2 * P,), F32, kind="Internal").ap()
    dram = nc.dram_tensor("row_scratch", (P * P,), F32, kind="Internal").ap()
    with Scope(nc, "all") as top:
        c = Consts()
        c.ident = top.sb("ident", [P, P])
        c.zero = top.sb("zero", [1, 512], BF16)
        degree = top.sb("degree", [P, T])
        x = top.sb("x", [P, T, D])
        full = N // P
        rest = N - full * P
        with stage(nc, "start", "set", "pad", "xin") as (block, set_, pad, xin):
            @block.gpsimd
            def _(pool):
                pool.memset(x[:, T - 1, :], 0.0).then_inc(pad, 1)
                pool.memset(c.ident[:], 0.0).then_inc(set_, 1)
                pool.memset(c.zero[:], 0.0).then_inc(set_, 1)
                pool.wait_ge(set_, 1)
                pool.wait_ge(set_, 2)
                pool.affine_select(out=c.ident[:], in_=c.ident[:], compare_op=ALU.not_equal, fill=1.0, base=0,
                                   pattern=[[-1, P]], channel_multiplier=1).then_inc(set_, 1)

            @block.sync
            def _(sp):
                sp.dma_start(x[:, 0:full, :], a["x"][0:full * P, :].rearrange("(t p) d -> p t d", p=P)).then_inc(xin, 16)
                sp.wait_ge(pad, 1)
                sp.dma_start(x[0:rest, full, :], a["x"][full * P:N, :]).then_inc(xin, 16)
                sp.wait_ge(xin, 32)
        landed = [top.cx.enter_context(nc.semaphore(f"edges{i}_landed")) for i in (1, 2)]
        count_edges(nc, "g1", a["src"], a["dst"], NCH1, NP, table1, keys1,
                    landed[0])
        count_edges(nc, "g2", a["L0_ffn_edge_index"][0, :], a["L0_ffn_edge_index"][1, :], NCH2, N2, table2, keys2,
                    landed[1])
        mask_and_degrees(nc, "m1", table1, T, G1, far1, c.ident, degree)
        mask_and_degrees(nc, "m2", table2, T2, G2, far2, c.ident, None)
        dinv = top.sb("dinv", [P, T])
        with stage(nc, "dinv", "clamped", "root") as (block, clamped, root):
            @block.vector
            def _(dve):
                dve.tensor_scalar(dinv[:], degree[:], 1e-30, None, ALU.max).then_inc(clamped, 1)
                dve.wait_ge(root, 1)
                dve.reciprocal(dinv[:], dinv[:])

            @block.scalar
            def _(act):
                act.wait_ge(clamped, 1)
                act.activation(dinv[:], dinv[:], ACT.Sqrt).then_inc(root, 1)

        for name, part in PARTS:
            part(nc, c, a, x, (table1, far1, table2, far2), dinv, dram)

        with stage(nc, "end", "out") as (block, out_sem):
            @block.sync
            def _(sp):
                sp.dma_start(out[0:full * P, :].rearrange("(t p) d -> p t d", p=P), x[:, 0:full, :]).then_inc(out_sem, 16)
                sp.dma_start(out[full * P:N, :], x[0:rest, full, :]).then_inc(out_sem, 16)
                sp.wait_ge(out_sem, 32)


def l0_gnn(nc, c, a, x, tables, dinv, dram):
    with Scope(nc, "l0g") as s:
        xn = s.sb("xn", [P, T, D])
        xt = s.sb("xt", [P, KD, NP])
        h = s.sb("h", [P, T, D])
        w = s.sb("w", [P, 2, KD, D])
        gram = s.sb("gram", [P, KD, D])
        gw = s.sb("gw", [P, KD, D])
        bias = s.sb("bias", [P, D])
        load(nc, "l0g_load", (w[:, 0], a["L0_gnn_W_gcn"].rearrange("(k p) n -> p k n", p=P)),
             (w[:, 1], a["L0_gnn_W_V"].rearrange("(k p) n -> p k n", p=P)), (bias[:], across(a["L0_gnn_b_gcn"], D)))
        layernorm(nc, "l0g_ln", x, xn, unit=True)
        turn(nc, "l0g_t", xn, xt, c.ident)
        product_nm(nc, "l0g_w", xt, w[:, 0], D,
                   lambda dve, t, ps: dve.tensor_scalar(h[:, t, :], ps, dinv[:, t:t + 1], None, ALU.mult))
        with Scope(nc, "l0gg") as q:
            pg = q.ps("pg", [P, 2, KD, 512])
            with stage(nc, "l0g_gram", "gram_ps", "gram_sb", "gw_ps") as (block, gram_ps, gram_sb, gw_ps):
                @block.tensor
                def _(pe):
                    for m in range(KD):
                        for t in range(T):
                            last = pe.matmul(pg[:, 0, m, 0:D], xn[:, t, m * P:(m + 1) * P], xn[:, t, :],
                                             start=(t == 0), stop=(t == T - 1))
                    last.then_inc(gram_ps, 1)
                    pe.wait_ge(gram_sb, 1)
                    for m in range(KD):
                        for k in range(KD):
                            last = pe.matmul(pg[:, 1, m, 0:D], gram[:, k, m * P:(m + 1) * P], w[:, 1, k, :],
                                             start=(k == 0), stop=(k == KD - 1))
                    last.then_inc(gw_ps, 1)

                @block.vector
                def _(dve):
                    dve.wait_ge(gram_ps, 1)
                    dve.tensor_copy(gram[:], pg[:, 0, :, 0:D]).then_inc(gram_sb, 1)
                    dve.wait_ge(gw_ps, 1)
                    dve.tensor_copy(gw[:], pg[:, 1, :, 0:D])
        agg = xn
        aggregate(nc, "l0g_agg", c, tables[0], T, G1, lambda t: h[:, ds(t, 1), :].rearrange("p a d -> p (a d)"), D,
                  lambda t: agg[:, ds(t, 1), :].rearrange("p a d -> p (a d)"), scale=dinv)
        product_nm(nc, "l0g_z", xt, gw, D, lambda dve, t, ps: dve.scalar_tensor_tensor(
            out=agg[:, t, :], in0=ps, scalar=0.1 / N, in1=agg[:, t, :], op0=ALU.mult, op1=ALU.add))
        finish_rows(nc, "l0g_end", x, agg, bias, True, True)


def l0_ffn(nc, c, a, x, tables, dinv, dram):
    hd, ne = 4, 4
    with Scope(nc, "l0f") as s:
        xt = s.sb("xt", [P, KD, NP])
        gate = s.sb("gate", [P, T, ne])
        with Scope(nc, "l0fa") as q:
            xn = q.sb("xn", [P, T, D])
            layernorm(nc, "l0f_ln", x, xn)
            turn(nc, "l0f_t", xn, xt, c.ident)
        with Scope(nc, "l0fb") as q:
            agg = q.sb("agg", [P, T, hd * ne])
            rows = q.sb("rows", [P, 3, hd * ne])
            gat(nc, "l0f_gat", c, xt, a["L0_ffn_W_gat"], hd * ne, a["L0_ffn_att_src"].rearrange("h c -> (h c)"),
                a["L0_ffn_att_dst"].rearrange("h c -> (h c)"), hd, tables[2], tables[3], T2, G2, dram,
                lambda t, i: agg[:, ds(t, 1), i * ne:(i + 1) * ne].rearrange("p a d -> p (a d)"), 1e-16,
                tail=lambda t: agg[:, t, :])
            load(nc, "l0f_vec", (rows[:, 0], across(a["L0_ffn_b_gat"], hd * ne)),
                 (rows[:, 1], across(a["L0_ffn_ln_gamma"], hd * ne)), (rows[:, 2], across(a["L0_ffn_ln_beta"], hd * ne)))
            score = q.sb("score", [P, T, ne])
            sq = q.sb("sq", [P, T, hd * ne])
            m = q.sb("m", [P, T])
            v = q.sb("v", [P, T])
            with stage(nc, "l0f_score", "step", "ready", "root") as (block, step, ready, root):
                @block.vector
                def _(dve):
                    link = Link(dve, step)
                    n = hd * ne
                    link(dve.tensor_tensor(agg[:], agg[:], over_mid(rows[:, 0, :], T), ALU.add))
                    link(dve.tensor_reduce(m[:], agg[:], AX, ALU.add))
                    link(dve.tensor_scalar(m[:], m[:], 1.0 / n, None, ALU.mult))
                    link(dve.tensor_tensor(agg[:], agg[:], over_last(m[:], n), ALU.subtract))
                    link(dve.tensor_tensor(sq[:], agg[:], agg[:], ALU.mult))
                    link(dve.tensor_reduce(v[:], sq[:], AX, ALU.add))
                    dve.tensor_scalar(v[:], v[:], 1.0 / n, 1e-5, ALU.mult, ALU.add).then_inc(ready, 1)
                    dve.wait_ge(root, 1)
                    link(dve.reciprocal(v[:], v[:]))
                    link(dve.tensor_tensor(agg[:], agg[:], over_last(v[:], n), ALU.mult))
                    link(dve.tensor_tensor(agg[:], agg[:], over_mid(rows[:, 1, :], T), ALU.mult))
                    link(dve.tensor_tensor(agg[:], agg[:], over_mid(rows[:, 2, :], T), ALU.add))
                    link(dve.tensor_tensor(score[:], agg[:, :, 0:ne], agg[:, :, ne:2 * ne], ALU.add))
                    for i in range(2, hd):
                        link(dve.tensor_tensor(score[:], score[:], agg[:, :, i * ne:(i + 1) * ne], ALU.add))
                    link(dve.tensor_scalar(score[:], score[:], 1.0 / hd, None, ALU.mult))

                @block.scalar
                def _(act):
                    act.wait_ge(ready, 1)
                    act.activation(v[:], v[:], ACT.Sqrt).then_inc(root, 1)
            top2_gates(nc, "l0f_top", c, score, ne, gate)
        w1 = s.sb("w1", [P, ne, KD, 2 * D])
        b1 = s.sb("b1", [P, ne, 2 * KD])
        w2 = s.sb("w2", [P, ne, 2 * KD, D])
        b2 = s.sb("b2", [ne, D])
        load(nc, "l0f_load", *[(w1[:, e], a["L0_ffn_W1"][e].rearrange("(k p) n -> p k n", p=P)) for e in range(ne)],
             *[(w2[:, e], a["L0_ffn_W2"][e].rearrange("(k p) n -> p k n", p=P)) for e in range(ne)],
             *[(b1[:, e], vec_cols(a["L0_ffn_b1"][e])) for e in range(ne)], (b2[:], a["L0_ffn_b2"]))
        experts(nc, "l0f_moe", c, xt, x, gate, ne, [(w1, KD, 2 * KD, ACT.Gelu, None, b1)], w2, b2)


def l1_gnn(nc, c, a, x, tables, dinv, dram):
    with Scope(nc, "l1g") as s:
        xt = s.sb("xt", [P, KD, NP])
        agg = s.sb("agg", [P, T, D])
        bias = s.sb("bias", [P, KD])
        bias2 = s.sb("bias2", [P, D])
        with Scope(nc, "l1ga") as q:
            h = q.sb("h", [P, T, D])
            w = q.sb("w", [P, KD, D])
            load(nc, "l1g_load", (w[:], a["L1_gnn_W1"].rearrange("(k p) n -> p k n", p=P)),
                 (bias[:], vec_cols(a["L1_gnn_b1"])), (bias2[:], across(a["L1_gnn_b2"], D)))
            layernorm(nc, "l1g_ln", x, h)
            turn(nc, "l1g_t", h, xt, c.ident)
            product_nm(nc, "l1g_w", xt, w, D,
                       lambda dve, t, ps: dve.tensor_scalar(h[:, t, :], ps, dinv[:, t:t + 1], None, ALU.mult))
            aggregate(nc, "l1g_agg", c, tables[0], T, G1, lambda t: h[:, ds(t, 1), :].rearrange("p a d -> p (a d)"), D,
                      lambda t: agg[:, ds(t, 1), :].rearrange("p a d -> p (a d)"), scale=dinv)
        turn(nc, "l1g_t2", agg, xt, c.ident, bias=bias, func=ACT.Relu)
        gat(nc, "l1g_gat", c, xt, a["L1_gnn_W2"], D, a["L1_gnn_att_src"], a["L1_gnn_att_dst"], 1, tables[0], tables[1],
            T, G1, dram, lambda t, i: agg[:, ds(t, 1), :].rearrange("p a d -> p (a d)"), 1e-16)
        finish_rows(nc, "l1g_end", x, agg, bias2, True, False)


def normal_input(nc, tag, c, x, xt):
    with Scope(nc, tag + "n") as q:
        xn = q.sb("xn", [P, T, D])
        layernorm(nc, tag + "_ln", x, xn)
        turn(nc, tag + "_t", xn, xt, c.ident)


def l1_ffn(nc, c, a, x, tables, dinv, dram):
    ne = 8
    f = "L1_ffn_"
    with Scope(nc, "l1f") as s:
        xt = s.sb("xt", [P, KD, NP])
        gate = s.sb("gate", [P, T, ne])
        normal_input(nc, "l1f", c, x, xt)
        wr = s.sb("wr", [P, KD, ne])
        br = s.sb("br", [P, ne])
        ws = [s.sb(f"w{i}", [P, ne, KD, D]) for i in range(3)]
        vec = s.sb("vec", [P, 2, 5, ne, KD])
        bo = s.sb("bo", [ne, D])
        names = [["b1", "g1", "be1", "m1", "v1"], ["b2", "g2", "be2", "m2", "v2"]]
        load(nc, "l1f_load", (wr[:], a[f + "Wr"].rearrange("(k p) n -> p k n", p=P)), (br[:], across(a[f + "br"], ne)),
             *[(ws[i][:, e], a[f + n][e].rearrange("(k p) n -> p k n", p=P)) for i, n in enumerate(["W1", "W2", "Wo"])
               for e in range(ne)],
             *[(vec[:, i, j, e], vec_cols(a[f + names[i][j]][e])) for i in range(2) for j in range(5) for e in range(ne)],
             (bo[:], a[f + "bo"]))
        with stage(nc, "l1f_bn", "step", "ready", "root") as (block, step, ready, root):
            @block.vector
            def _(dve):
                link = Link(dve, step)
                dve.tensor_scalar(vec[:, :, 4], vec[:, :, 4], 1e-3, None, ALU.add).then_inc(ready, 1)
                dve.wait_ge(root, 1)
                link(dve.reciprocal(vec[:, :, 4], vec[:, :, 4]))
                link(dve.tensor_tensor(vec[:, :, 1], vec[:, :, 1], vec[:, :, 4], ALU.mult))
                link(dve.tensor_tensor(vec[:, :, 0], vec[:, :, 0], vec[:, :, 3], ALU.subtract))
                link(dve.tensor_tensor(vec[:, :, 0], vec[:, :, 0], vec[:, :, 1], ALU.mult))
                link(dve.tensor_tensor(vec[:, :, 0], vec[:, :, 0], vec[:, :, 2], ALU.add))

            @block.scalar
            def _(act):
                act.wait_ge(ready, 1)
                act.activation(vec[:, :, 4], vec[:, :, 4], ACT.Sqrt).then_inc(root, 1)
        product_nm(nc, "l1f_r", xt, wr, ne, lambda dve, t, ps: dve.tensor_copy(gate[:, t, :], ps))
        softmax(nc, "l1f_sm", gate, ne, br)
        experts(nc, "l1f_moe", c, xt, x, gate, ne,
                [(ws[i], KD, KD, ACT.Relu, vec[:, i, 1], vec[:, i, 0]) for i in range(2)], ws[2], bo)


def l2_gnn(nc, c, a, x, tables, dinv, dram):
    f = "L2_gnn_"
    with Scope(nc, "l2g") as s:
        xt = s.sb("xt", [P, KD, NP])
        agg = s.sb("agg", [P, T, D])
        vec = s.sb("vec", [P, 3, KD])
        bias = s.sb("bias", [P, D])
        scale = s.sb("scale", [P, KD])
        shift = s.sb("shift", [P, KD])
        normal_input(nc, "l2g", c, x, xt)
        load(nc, "l2g_load", (vec[:, 0], vec_cols(a[f + "b0"])), (vec[:, 1], vec_cols(a[f + "gamma0"])),
             (vec[:, 2], vec_cols(a[f + "beta0"])), (bias[:], across(a[f + "b1"], D)))
        gat(nc, "l2g_a", c, xt, a[f + "W0"], D, a[f + "a_src0"].rearrange("h c -> (h c)"),
            a[f + "a_dst0"].rearrange("h c -> (h c)"), 4, tables[0], tables[1], T, G1, dram,
            lambda t, i: agg[:, ds(t, 1), i * 64:(i + 1) * 64].rearrange("p a d -> p (a d)"), 0.0)
        turn(nc, "l2g_t2", agg, xt, c.ident, bias=vec[:, 0])
        batchnorm_columns(nc, "l2g_bn", xt, vec[:, 1], vec[:, 2], scale, shift)
        with Scope(nc, "l2e") as q:
            low = q.sb("low", [P, KD, NP])
            with stage(nc, "l2g_elu", "step", "ready", "expd") as (block, step, ready, expd):
                @block.vector
                def _(dve):
                    for k in range(KD):
                        dve.tensor_scalar(xt[:, k, :], xt[:, k, :], scale[:, k:k + 1], shift[:, k:k + 1],
                                          ALU.mult, ALU.add).then_inc(step, 1)
                        dve.wait_ge(step, 2 * k + 1)
                        dve.tensor_scalar(low[:, k, :], xt[:, k, :], 0.0, None, ALU.min).then_inc(ready, 1)
                        dve.tensor_scalar(xt[:, k, :], xt[:, k, :], 0.0, -1.0, ALU.max, ALU.add).then_inc(step, 1)
                        dve.wait_ge(step, 2 * k + 2)
                    for k in range(KD):
                        dve.wait_ge(expd, k + 1)
                        dve.tensor_tensor(xt[:, k, :], xt[:, k, :], low[:, k, :], ALU.add)

                @block.scalar
                def _(act):
                    for k in range(KD):
                        act.wait_ge(ready, k + 1)
                        act.activation(low[:, k, :], low[:, k, :], ACT.Exp).then_inc(expd, 1)
        gat(nc, "l2g_b", c, xt, a[f + "W1"], D, a[f + "a_src1"].rearrange("h c -> (h c)"),
            a[f + "a_dst1"].rearrange("h c -> (h c)"), 1, tables[0], tables[1], T, G1, dram,
            lambda t, i: agg[:, ds(t, 1), :].rearrange("p a d -> p (a d)"), 0.0)
        finish_rows(nc, "l2g_end", x, agg, bias, False, True)


def l2_ffn(nc, c, a, x, tables, dinv, dram):
    ne, fh = 8, 1024
    cap = -(-5 * N // (4 * ne))
    f = "L2_ffn_"
    with Scope(nc, "l2f") as s:
        xt = s.sb("xt", [P, KD, NP])
        gate = s.sb("gate", [P, T, ne])
        normal_input(nc, "l2f", c, x, xt)
        with Scope(nc, "l2fr") as q:
            wr = q.sb("wr", [P, KD, ne])
            br = q.sb("br", [P, ne])
            prio = q.sb("prio", [P, ne])
            upto = q.sb("upto", [P, P])
            ones = q.sb("ones", [P, P])
            prob = q.sb("prob", [P, T])
            tmp = q.sb("tmp", [P, T])
            one = q.sb("one", [P, T, ne])
            pos = q.sb("pos", [P, T, ne])
            tot = q.sb("tot", [P, T + 1, ne])
            load(nc, "l2f_loadr", (wr[:], a[f + "gate_w"].rearrange("(k p) n -> p k n", p=P)),
                 (br[:], across(a[f + "gate_b"], ne)))
            product_nm(nc, "l2f_r", xt, wr, ne, lambda dve, t, ps: dve.tensor_copy(gate[:, t, :], ps))
            softmax(nc, "l2f_sm", gate, ne, br)
            pp = q.ps("pp", [P, 2, 512])
            with stage(nc, "l2f_pos", "sets", "step", "chosen", "summed") as (block, sets, step, chosen, summed):
                @block.gpsimd
                def _(pool):
                    pool.iota(prio[:], pattern=[[-1, ne]], base=ne, channel_multiplier=0,
                              allow_small_or_imprecise_dtypes=True).then_inc(sets, 1)
                    pool.memset(ones[:], 1.0).then_inc(sets, 1)
                    pool.memset(upto[:], 1.0).then_inc(sets, 1)
                    pool.wait_ge(sets, 3)
                    pool.affine_select(out=upto[:], in_=upto[:], compare_op=ALU.is_ge, fill=0.0, base=0,
                                       pattern=[[1, P]], channel_multiplier=-1).then_inc(sets, 1)

                @block.vector
                def _(dve):
                    link = Link(dve, step)
                    dve.wait_ge(sets, 4)
                    first_max(dve, link, gate, ne, prio, prob, one, tmp)
                    dve.sem_inc(chosen, 1)
                    link(dve.memset(tot[:], 0.0))
                    dve.wait_ge(summed, 1)
                    link(dve.tensor_copy(pos[:].rearrange("p t e -> p (t e)"), pp[:, 1, 0:T * ne]))
                    for t in range(1, T):
                        link(dve.tensor_tensor(tot[:, t, :], tot[:, t - 1, :], pos[:, t - 1, :], ALU.add))
                    link(dve.tensor_tensor(pos[:].rearrange("p t e -> p (t e)"), pp[:, 0, 0:T * ne],
                                           tot[:, 0:T, :].rearrange("p t e -> p (t e)"), ALU.add))
                    link(dve.tensor_scalar(pos[:], pos[:], cap + 0.5, None, ALU.is_lt))
                    link(dve.tensor_tensor(gate[:], one[:], pos[:], ALU.mult))
                    link(dve.tensor_tensor(gate[:], gate[:], over_last(prob[:], ne), ALU.mult))

                @block.tensor
                def _(pe):
                    pe.wait_ge(chosen, 1)
                    pe.matmul(pp[:, 0, 0:T * ne], upto[:], one[:].rearrange("p t e -> p (t e)"), start=True, stop=True)
                    pe.matmul(pp[:, 1, 0:T * ne], ones[:], one[:].rearrange("p t e -> p (t e)"), start=True, stop=True
                              ).then_inc(summed, 1)
        y_all = s.sb("y_all", [P, T, D])
        with stage(nc, "l2f_zero", "z") as (block, z):
            @block.vector
            def _(dve):
                dve.memset(y_all[:], 0.0)
        part = 4
        w1 = s.sb("w1", [P, part, KD, fh])
        w2 = s.sb("w2", [P, part, fh // P, D])
        b1 = s.sb("b1", [P, part, fh // P])
        b2 = s.sb("b2", [part, D])
        gp = s.sb("gp", [P, T, part])
        for e0 in range(0, ne, part):
            load(nc, f"l2f_load{e0}",
                 *[(w1[:, e], a[f + "w1"][e0 + e].rearrange("(k p) n -> p k n", p=P)) for e in range(part)],
                 *[(w2[:, e], a[f + "w2"][e0 + e].rearrange("(k p) n -> p k n", p=P)) for e in range(part)],
                 *[(b1[:, e], vec_cols(a[f + "b1"][e0 + e])) for e in range(part)], (b2[:], a[f + "b2"][e0:e0 + part]))
            with stage(nc, f"l2f_g{e0}", "z") as (block, z):
                @block.vector
                def _(dve):
                    dve.tensor_copy(gp[:], gate[:, :, e0:e0 + part])
            experts(nc, f"l2f_moe{e0}", c, xt, y_all, gp, part, [(w1, KD, fh // P, ACT.Relu, None, b1)], w2, b2)
        with Scope(nc, "l2n") as q:
            flag = q.sb("flag", [P, G1, D], U8)
            fill = q.sb("fill", [P, 3, D])
            with stage(nc, "l2f_num", "filled", "step") as (block, filled, step):
                @block.gpsimd
                def _(pool):
                    for i, v in enumerate((0.0, 10000.0, -10000.0)):
                        pool.memset(fill[:, i, :], v).then_inc(filled, 1)

                @block.vector
                def _(dve):
                    link = Link(dve, step)
                    dve.wait_ge(filled, 3)
                    for g in range(T // G1):
                        y = y_all[:, g * G1:(g + 1) * G1, :]
                        xs = x[:, g * G1:(g + 1) * G1, :]
                        link(dve.tensor_tensor(flag[:], y, y, ALU.not_equal))
                        link(dve.copy_predicated(y, flag[:], over_mid(fill[:, 0, :], G1)))
                        link(dve.tensor_scalar(flag[:], y, 3.4028235e38, None, ALU.is_gt))
                        link(dve.copy_predicated(y, flag[:], over_mid(fill[:, 1, :], G1)))
                        link(dve.tensor_scalar(flag[:], y, -3.4028235e38, None, ALU.is_lt))
                        link(dve.copy_predicated(y, flag[:], over_mid(fill[:, 2, :], G1)))
                        link(dve.tensor_tensor(xs, xs, y, ALU.add))


def l3_gnn(nc, c, a, x, tables, dinv, dram):
    f = "L3_gnn_"
    with Scope(nc, "l3g") as s:
        vec = s.sb("vec", [P, 5, 3, KD])
        w = s.sb("w", [P, 6, KD, D])
        scale = s.sb("scale", [P, KD])
        shift = s.sb("shift", [P, KD])
        rows = s.sb("rows", [P, T, D])
        agg_x = s.sb("agg_x", [P, KD, NP])
        h_fm = s.sb("h_fm", [P, KD, NP])
        agg_h = s.sb("agg_h", [P, KD, NP])

        def slot(i):
            return (0, 1, 2, 4, 5)[i]
        load(nc, "l3g_load",
             *[(w[:, slot(i)], a[f + f"W{i + 1}"].rearrange("(k p) n -> p k n", p=P)) for i in (0, 1, 3, 4)],
             (w[:, 2:4].rearrange("p a k n -> p (a k) n"), a[f + "W3"].rearrange("(k p) n -> p k n", p=P)),
             *[(vec[:, i, j], vec_cols(a[f + n + str(i + 1)])) for i in range(5) for j, n in enumerate(["b", "g", "be"])])

        def lin_bn_relu(i, srcs, dst):
            wi = w[:, 2:4].rearrange("p a k n -> p (a k) n") if i == 2 else w[:, slot(i)]
            product_fm(nc, f"l3g_w{i}", srcs, wi, dst, ACT.Identity, vec[:, i, 0])
            batchnorm_columns(nc, f"l3g_bn{i}", dst, vec[:, i, 1], vec[:, i, 2], scale, shift)
            scale_relu(nc, f"l3g_relu{i}", dst, scale, shift)

        def halves(t):
            return [t[:, k] for k in range(KD)]

        with Scope(nc, "l3ga") as q:
            agg = q.sb("agg", [P, T, D])
            layernorm(nc, "l3g_ln", x, rows)
            aggregate(nc, "l3g_agg", c, tables[0], T, G1, lambda t: rows[:, ds(t, 1), :].rearrange("p a d -> p (a d)"),
                      D, lambda t: agg[:, ds(t, 1), :].rearrange("p a d -> p (a d)"))
            turn(nc, "l3g_t", agg, agg_x, c.ident)
            lin_bn_relu(0, halves(agg_x), h_fm)
            lin_bn_relu(1, halves(h_fm), agg_h)
            unturn(nc, "l3g_u", agg_h, rows, c.ident)
            aggregate(nc, "l3g_agg2", c, tables[0], T, G1, lambda t: rows[:, ds(t, 1), :].rearrange("p a d -> p (a d)"),
                      D, lambda t: agg[:, ds(t, 1), :].rearrange("p a d -> p (a d)"))
            turn(nc, "l3g_t2", agg, agg_h, c.ident)
        lin_bn_relu(2, halves(agg_x) + halves(agg_h), h_fm)
        lin_bn_relu(3, halves(h_fm), agg_x)
        lin_bn_relu(4, halves(agg_x), h_fm)
        unturn(nc, "l3g_u2", h_fm, x, c.ident, add=True)


def unturn(nc, tag, fm, nm, ident, add=False):
    with Scope(nc, tag) as s:
        pt = s.ps("pt", [P, 8, 512])
        with stage(nc, tag, "turned", "out") as (block, turned, out):
            @block.tensor
            def _(pe):
                for t in range(T):
                    if t >= 8:
                        pe.wait_ge(out, t - 7)
                    for k in range(KD):
                        last = pe.transpose(pt[:, t % 8, k * P:(k + 1) * P], fm[:, k, t * P:(t + 1) * P], ident[:])
                    last.then_inc(turned, 1)

            @block.vector
            def _(dve):
                for t in range(T):
                    dve.wait_ge(turned, t + 1)
                    if add:
                        dve.tensor_tensor(nm[:, t, :], pt[:, t % 8, 0:D], nm[:, t, :], ALU.add).then_inc(out, 1)
                    else:
                        dve.tensor_copy(nm[:, t, :], pt[:, t % 8, 0:D]).then_inc(out, 1)


def l3_ffn(nc, c, a, x, tables, dinv, dram):
    ne = 6
    f = "L3_ffn_"
    with Scope(nc, "l3f") as s:
        xt = s.sb("xt", [P, KD, NP])
        gate = s.sb("gate", [P, T, ne])
        normal_input(nc, "l3f", c, x, xt)
        with Scope(nc, "l3fr") as q:
            w1 = q.sb("w1", [P, KD, P])
            b1 = q.sb("b1", [P, 1])
            w2 = q.sb("w2", [P, 1, ne])
            br = q.sb("br", [P, ne])
            rh = q.sb("rh", [P, 1, NP])
            score = q.sb("score", [P, T, ne])
            load(nc, "l3f_loadr", (w1[:], a[f + "router_w1"].rearrange("(k p) n -> p k n", p=P)),
                 (b1[:], vec_cols(a[f + "router_b1"])), (w2[:, 0], a[f + "router_w2"]), (br[:], across(a[f + "router_b2"], ne)))
            product_fm(nc, "l3f_r1", [xt[:, k] for k in range(KD)], w1, rh, ACT.Relu, b1)
            product_nm(nc, "l3f_r2", rh, w2, ne, lambda dve, t, ps: dve.tensor_copy(score[:, t, :], ps))
            softmax(nc, "l3f_sm", score, ne, br)
            top2_gates(nc, "l3f_top", c, score, ne, gate)
        ws = [s.sb(f"w{i}", [P, ne, KD, D]) for i in range(3)]
        b = s.sb("b", [P, 2, ne, KD])
        b3 = s.sb("b3", [ne, D])
        load(nc, "l3f_load",
             *[(ws[i][:, e], a[f + f"expert_w{i + 1}"][e].rearrange("(k p) n -> p k n", p=P)) for i in range(3)
               for e in range(ne)],
             *[(b[:, i, e], vec_cols(a[f + f"expert_b{i + 1}"][e])) for i in range(2) for e in range(ne)],
             (b3[:], a[f + "expert_b3"]))
        experts(nc, "l3f_moe", c, xt, x, gate, ne, [(ws[i], KD, KD, ACT.Relu, None, b[:, i]) for i in range(2)], ws[2], b3)


PARTS = [("l0_gnn", l0_gnn), ("l0_ffn", l0_ffn), ("l1_gnn", l1_gnn), ("l1_ffn", l1_ffn), ("l2_gnn", l2_gnn),
         ("l2_ffn", l2_ffn), ("l3_gnn", l3_gnn), ("l3_ffn", l3_ffn)]
_INS = "x src dst".split() + """L0_gnn_W_gcn L0_gnn_b_gcn L0_gnn_W_V
L0_ffn_W_gat L0_ffn_att_src L0_ffn_att_dst L0_ffn_b_gat L0_ffn_ln_gamma L0_ffn_ln_beta L0_ffn_W1 L0_ffn_b1 L0_ffn_W2
L0_ffn_b2 L0_ffn_edge_index L1_gnn_W1 L1_gnn_b1 L1_gnn_W2 L1_gnn_att_src L1_gnn_att_dst L1_gnn_b2 L1_ffn_Wr L1_ffn_br
L1_ffn_W1 L1_ffn_b1 L1_ffn_g1 L1_ffn_be1 L1_ffn_m1 L1_ffn_v1 L1_ffn_W2 L1_ffn_b2 L1_ffn_g2 L1_ffn_be2 L1_ffn_m2
L1_ffn_v2 L1_ffn_Wo L1_ffn_bo L2_gnn_W0 L2_gnn_a_src0 L2_gnn_a_dst0 L2_gnn_b0 L2_gnn_gamma0 L2_gnn_beta0 L2_gnn_W1
L2_gnn_a_src1 L2_gnn_a_dst1 L2_gnn_b1 L2_ffn_gate_w L2_ffn_gate_b L2_ffn_w1 L2_ffn_b1 L2_ffn_w2 L2_ffn_b2""".split() + [
    f"L3_gnn_{v}{i}" for i in range(1, 6) for v in ("W", "b", "g", "be")] + [
    "L3_ffn_router_w1", "L3_ffn_router_b1", "L3_ffn_router_w2", "L3_ffn_router_b2"] + [
    f"L3_ffn_expert_{v}{i}" for i in range(1, 4) for v in ("w", "b")]


def kernel(**inputs):
    import concourse.bacc as bacc
    import numpy as np
    from concourse.bass_utils import run_bass_kernel_spmd

    nc = bacc.Bacc("TRN2", target_bir_lowering=False, num_devices=1)
    arrays, args = {}, {}
    for name in _INS:
        v = np.ascontiguousarray(inputs[name])
        if name in ("src", "dst"):
            v = np.concatenate([v, np.full(NCH1 * P - E1, NP - 1, v.dtype)])
        arrays["in_" + name] = v
        args[name] = nc.dram_tensor("in_" + name, v.shape, mybir.dt.from_np(v.dtype), kind="ExternalInput").ap()
    out = nc.dram_tensor("out_x", (N, D), F32, kind="ExternalOutput").ap()
    build(nc, args, out)
    r = run_bass_kernel_spmd(nc, [arrays], core_ids=[0])
    return r.results[0]["out_x"]
```

```python
from contextlib import ExitStack, contextmanager

import concourse.bass as bass
from concourse import mybir

F32 = mybir.dt.float32
I32 = mybir.dt.int32
U32 = mybir.dt.uint32
U8 = mybir.dt.uint8
BF16 = mybir.dt.bfloat16
ALU = mybir.AluOpType
ACT = mybir.ActivationFunctionType
AX = mybir.AxisListType.X
ds = bass.ds

P = 128
N = 3125
T = -(-N // P)
NP = T * P
D = 256
KD = D // P
G1 = 5
N2 = 2048
T2 = N2 // P
G2 = 4
W = 8
E1 = 53125
NCH1 = 2 * W * -(-E1 // (2 * W * P))
E2 = 32768
NCH2 = E2 // P
FAR = -1e30
SLOPE = 0.2
ROUTED = 8 * 512
SEM0 = 150


@contextmanager
def stage(nc, name, *names):
    with ExitStack() as cx:
        sems = [cx.enter_context(nc.semaphore(f"{name}_{s}", num=SEM0 + i)) for i, s in enumerate(names)]
        with nc.Block() as block:
            yield (block, *sems)
        nc.all_engine_barrier(sems_to_clear=range(SEM0, SEM0 + len(names)))


class Link:

    def __init__(self, eng, sem):
        self.eng, self.sem, self.n = eng, sem, 0

    def __call__(self, ins):
        self.n += 1
        ins.then_inc(self.sem, 1)
        self.eng.wait_ge(self.sem, self.n)


class Scope:

    def __init__(self, nc, tag):
        self.nc, self.tag, self.cx = nc, tag, ExitStack()

    def __enter__(self):
        return self

    def __exit__(self, *a):
        return self.cx.__exit__(*a)

    def sb(self, name, shape, dt=F32):
        return self.cx.enter_context(self.nc.sbuf_tensor(f"{self.tag}_{name}", shape, dt))

    def ps(self, name, shape, dt=F32):
        return self.cx.enter_context(self.nc.psum_tensor(f"{self.tag}_{name}", shape, dt))


def across(vec, n):
    return vec.rearrange("(o n) -> o n", o=1).to_broadcast([P, n])


def over_last(ap, n):
    a, t = ap.shape
    return ap.rearrange("p (t o) -> p t o", o=1).to_broadcast([a, t, n])


def over_mid(ap, t):
    a, n = ap.shape
    return ap.rearrange("p (o n) -> p o n", o=1).to_broadcast([a, t, n])



def count_edges(nc, graphs, key_rows, ident, landed):
    n_win = [nch // W for _, _, nch, _, _ in graphs]
    alone = n_win[0] // 4 * 2
    turns = n_win[0] - alone
    n_all = graphs[0][2] + graphs[1][2]
    first = [0, graphs[0][2]]
    span = (W + 1) * P
    blocks = [(at, min(P, n_all - at)) for at in range(0, n_all, P)]
    with Scope(nc, "count") as s:
        ids = s.sb("ids", [P, 2, n_all], I32)
        key = s.sb("key", [P, n_all])
        apart = s.sb("apart", [P, n_all])
        key_turned = s.sb("key_turned", [P, len(blocks), P])
        eye_rows = s.sb("eye_rows", [P, 2 * NP])
        keys = s.sb("keys", [P, 2, W * P])
        same = s.sb("same", [P, 2, W, span], BF16)
        same_own = s.sb("same_own", [P, 2, W, P], BF16)
        below = s.sb("below", [P, P], BF16)
        picks = s.sb("picks", [P, 4], BF16)
        sign = s.sb("sign", [P, 2, W])
        count = s.sb("count", [P, 2, W])
        cell = s.sb("cell", [P, 2, W], U32)
        sums = s.ps("sums", [P, 2, 512])
        turned = s.ps("turned", [P, len(blocks), 512])
        with stage(nc, "count", "ids_in", "eye", "consts", "table_set0", "table_set1", "keyed", "keys_turned",
                   "turned_out", "keys_out", "keys_in0", "keys_in1", "compared", "own_ready", "counted",
                   "sums_read", "cells_ready", "cells_free", "begun", "clear") as (
                block, ids_in, eye, consts, table_set0, table_set1, keyed, keys_turned,
                turned_out, keys_out, keys_in0, keys_in1, compared, own_ready, counted,
                sums_read, cells_ready, cells_free, begun, clear):
            keys_in = [keys_in0, keys_in1]
            table_set = [table_set0, table_set1]

            def windows(eng, body):
                start = alone // 2
                with eng.Fori(0, start) as i:
                    for b in range(2):
                        body(b, 0, 2 * i + b, 2 * i + b, i)
                with eng.Fori(start, start + turns) as i:
                    body(0, 0, i + (alone - start), 2 * i, i)
                    body(1, 1, i - start, 2 * i + 1, i)
                with eng.Fori(start + turns, sum(n_win) // 2) as i:
                    for b in range(2):
                        body(b, 1, 2 * i + (b - n_win[0]), 2 * i + b, i)

            @block.sync
            def _(sp):
                for g, (src, dst, nch, _, _) in enumerate(graphs):
                    for i, ends in enumerate((src, dst)):
                        sp.dma_start(ids[:, i, first[g]:first[g] + nch], ends.rearrange("(p c) -> p c", p=P)
                                     ).then_inc(ids_in, 16)
                sp.wait_ge(turned_out, len(blocks))
                for i, (at, m) in enumerate(blocks):
                    sp.dma_start(key_rows[at * P:(at + m) * P].rearrange("(c p) -> c p", p=P), key_turned[0:m, i, :]
                                 ).then_inc(keys_out, 16)
                sp.wait_ge(keys_out, 16 * len(blocks))

                def body(b, g, w, n, i):
                    sp.wait_ge(compared, n * W + W)
                    sp.dma_start(keys[:, b, :], key_rows.rearrange("(o n) -> o n", o=1)[
                        :, ds(w * (W * P) + first[g] * P, W * P)].to_broadcast([P, W * P])).then_inc(keys_in[b], 16)
                windows(sp, body)

            @block.vector
            def _(dve):
                dve.wait_ge(ids_in, 64)
                for g, (_, _, nch, n_pad, _) in enumerate(graphs):
                    own = slice(first[g], first[g] + nch)
                    dve.scalar_tensor_tensor(out=key[:, own], in0=ids[:, 0, own], scalar=float(n_pad),
                                             in1=ids[:, 1, own], op0=ALU.mult, op1=ALU.add).then_inc(keyed, 1)
                for i, (at, m) in enumerate(blocks):
                    dve.wait_ge(keys_turned, i + 1)
                    dve.tensor_copy(key_turned[0:m, i, :], turned[0:m, i, 0:P]).then_inc(turned_out, 1)
                dve.wait_ge(consts, 7)
                dve.wait_ge(keyed, 2)
                dve.tensor_tensor(apart[:], apart[:], key[:], ALU.subtract).then_inc(keyed, 2)
                dve.sem_inc(compared, 2 * W)
                dve.sem_inc(counted, 2)

                def body(b, g, w, n, i):
                    dve.wait_ge(keys_in[b], (i + 1) * 16)
                    dve.wait_ge(counted, n + 1)
                    for j in range(W):
                        dve.tensor_scalar(same[:, b].rearrange("p j s -> p (j s)")[:, j * W * P:(j + 1) * W * P],
                                          keys[:, b, :], key[:, ds(w * W + (first[g] + j), 1)], None, ALU.is_equal
                                          ).then_inc(compared, 1)
                    dve.wait_ge(compared, n * W + 3 * W)
                    dve.tensor_tensor(same_own[:, b], same[:, b, :, 0:P], over_mid(below[:], W), ALU.mult
                                      ).then_inc(own_ready, 1)
                windows(dve, body)

            @block.tensor
            def _(pe):
                pe.wait_ge(keyed, 2)
                for i, (at, m) in enumerate(blocks):
                    pe.transpose(turned[0:m, i, 0:P], key[:, at:at + m], ident[:]).then_inc(keys_turned, 1)
                pe.wait_ge(consts, 7)
                pe.sem_inc(sums_read, 4)

                def body(b, g, w, n, i):
                    pe.wait_ge(own_ready, n + 1)
                    pe.wait_ge(sums_read, 2 * n + 2)
                    flat = same[:, b].rearrange("p j s -> p (j s)")
                    for k in range(W):
                        for j in range(W):
                            at = (j * W + k) * P
                            pe.matmul(sums[:, b, 2 * k:2 * k + 2], flat[:, at:at + P],
                                      picks[:, 0:2] if j < k else picks[:, 1:3], start=(j == 0), stop=False)
                        last = pe.matmul(sums[:, b, 2 * k:2 * k + 2], same_own[:, b, k, :], picks[:, 2:4],
                                         start=False, stop=True)
                    last.then_inc(counted, 1)
                windows(pe, body)

            @block.scalar
            def _(act):
                for g, (_, _, _, n_pad, table) in enumerate(graphs):
                    act.wait_ge(eye, 1)
                    for t in range(n_pad // P):
                        act.dma_start(table[0:n_pad * n_pad, 0].rearrange("(r n) -> r n", n=n_pad)[t * P:(t + 1) * P, :],
                                      eye_rows[:, NP - t * P:NP - t * P + n_pad]).then_inc(table_set[g], 16)

                act.wait_ge(keyed, 4)

                def body(b, g, w, n, i):
                    act.wait_ge(cells_free, n + 1)
                    act.wait_ge(counted, n + 3)
                    both_sums = sums[:, b, 0:2 * W].rearrange("p (k a) -> p k a", a=2)
                    act.activation(sign[:, b, :], both_sums[:, :, 1], ACT.Sign).then_inc(sums_read, 1)
                    act.activation(count[:, b, :], both_sums[:, :, 0], ACT.Copy).then_inc(sums_read, 1)
                    act.wait_ge(sums_read, 2 * n + 6)
                    for j in range(W):
                        at = w * W + (first[g] + j)
                        last = act.activation(cell[:, b, j:j + 1], sign[:, b, j:j + 1], ACT.Identity,
                                              scale=apart[:, ds(at, 1)], bias=key[:, ds(at, 1)])
                        last.then_inc(cells_ready, 1)
                windows(act, body)

            @block.gpsimd
            def _(pool):
                pool.memset(eye_rows[:], 0.0).then_inc(clear, 1)
                pool.memset(below[:], 1.0).then_inc(clear, 1)
                pool.memset(picks[:], 1.0).then_inc(clear, 1)
                pool.wait_ge(clear, 3)
                pool.affine_select(out=eye_rows[:], in_=eye_rows[:], compare_op=ALU.not_equal, fill=1.0,
                                   base=-NP, pattern=[[1, 2 * NP]], channel_multiplier=-1).then_inc(eye, 1)
                pool.memset(picks[:, 2:3], 0.0).then_inc(consts, 1)
                pool.affine_select(out=below[:], in_=below[:], compare_op=ALU.is_gt, fill=0.0, base=0,
                                   pattern=[[1, P]], channel_multiplier=-1).then_inc(consts, 1)
                for g, (_, _, nch, n_pad, _) in enumerate(graphs):
                    pool.iota(apart[:, first[g]:first[g] + nch], pattern=[[0, nch // W], [P, W]], base=n_pad * n_pad,
                              channel_multiplier=1, allow_small_or_imprecise_dtypes=True).then_inc(consts, 1)
                pool.wait_ge(consts, 4)
                pool.sem_inc(consts, 3)
                def add_window(b, g):
                    n_pad, table = graphs[g][3:]
                    pool.sem_inc(begun, 1)
                    for j in range(W):
                        pool.indirect_dma_start(
                            table, bass.IndirectOffsetOnAxis(ap=cell[:, b, j:j + 1], axis=0),
                            count[:, b, j:j + 1], None, compute_op=ALU.add,
                            bounds_check=n_pad * n_pad + W * P - 1, oob_is_err=True).then_inc(landed[g], 16)

                def land_own(g, w):
                    pool.wait_ge(landed[g], w * (16 * W))

                def window_alone(b, g, w, n):
                    land_own(g, w - 1)
                    pool.sem_inc(cells_free, 1)
                    pool.wait_ge(cells_ready, n * W + W)
                    land_own(g, w)
                    add_window(b, g)

                pool.wait_ge(table_set[0], 16 * (graphs[0][3] // P))
                pool.sem_inc(cells_free, 2)
                pool.wait_ge(cells_ready, W)
                add_window(0, 0)
                pool.wait_ge(cells_ready, 2 * W)
                land_own(0, 1)
                add_window(1, 0)
                start = alone // 2
                with pool.Fori(1, start) as i:
                    for b in range(2):
                        window_alone(b, 0, 2 * i + b, 2 * i + b)
                pool.wait_ge(table_set[1], 16 * (graphs[1][3] // P))

                def turn_of(g, w, n):
                    if w is not None:
                        land_own(g, w)
                    pool.sem_inc(cells_free, 1)
                    pool.wait_ge(cells_ready, n * W + W)
                    add_window(g, g)

                turn_of(0, alone, alone)
                turn_of(1, None, alone + 1)
                with pool.Fori(start + 1, start + turns) as i:
                    turn_of(0, i + (alone - start), 2 * i)
                    turn_of(1, i - start, 2 * i + 1)
                land_own(0, n_win[0])
                with pool.Fori(start + turns, sum(n_win) // 2) as i:
                    for b in range(2):
                        window_alone(b, 1, 2 * i + (b - n_win[0]), 2 * i + b)
                land_own(1, n_win[1])


def mask_and_degrees(nc, tag, table, nt, gt, far, ident, degree):
    n_pad = nt * P
    ngr = -(-nt // 4)
    table2 = table[0:n_pad * n_pad, 0].rearrange("(r n) -> r n", n=n_pad)
    with Scope(nc, tag) as s:
        panel = s.sb("panel", [P, gt, nt, P])
        turned = s.sb("turned", [P, ngr, 4 * P])
        mask = s.sb("mask", [P, gt, n_pad], BF16)
        part = s.sb("part", [P, nt, ngr])
        pt = s.ps("pt", [P, ngr, 4 * P])
        with stage(nc, tag, *[f"panel_in{u}" for u in range(gt)], *[f"mask_out{u}" for u in range(gt)],
                   "panel_free", "turned_ps", "copied", "masked", "summed") as (block, *sems):
            panel_in, mask_out = sems[:gt], sems[gt:2 * gt]
            panel_free, turned_ps, copied, masked, summed = sems[2 * gt:]

            @block.sync
            def _(sp):
                def load_panel(k, u):
                    sp.wait_ge(panel_free, k * gt + u + 1)
                    sp.dma_start(panel[:, u], table2[:, ds((k * gt + u) * P, P)].rearrange("(t p) d -> p t d", p=P)
                                 ).then_inc(panel_in[u], 16)

                def store_mask(k, u):
                    sp.wait_ge(masked, (k * gt + u + 2) * ngr)
                    sp.dma_start(far[ds((k * gt + u) * P, P), :], mask[:, u, :]).then_inc(mask_out[u], 16)

                for u in range(gt):
                    sp.sem_inc(mask_out[u], 16)
                    load_panel(0, u)
                with sp.Fori(1, nt // gt) as k:
                    for u in range(gt):
                        load_panel(k, u)
                        store_mask(k - 1, u)
                for u in range(gt):
                    store_mask(nt // gt - 1, u)
                for u in range(gt):
                    sp.wait_ge(mask_out[u], (nt // gt + 1) * 16)

            @block.tensor
            def _(pe):
                pe.sem_inc(panel_free, gt)
                with pe.Fori(0, nt // gt) as k:
                    for u in range(gt):
                        j = k * gt + u
                        pe.wait_ge(panel_in[u], (k + 1) * 16)
                        for q in range(ngr):
                            pe.wait_ge(copied, j * ngr + q + 1)
                            for t in range(4 * q, min(4 * q + 4, nt)):
                                last = pe.transpose(pt[:, q, (t - 4 * q) * P:(t - 4 * q + 1) * P], panel[:, u, t, :],
                                                    ident[:])
                            last.then_inc(turned_ps, 1)
                        pe.wait_ge(turned_ps, j * ngr + ngr)
                        pe.sem_inc(panel_free, 1)

            @block.scalar
            def _(act):
                act.sem_inc(copied, ngr)
                act.sem_inc(masked, ngr)
                with act.Fori(0, nt // gt) as k:
                    for u in range(gt):
                        j = k * gt + u
                        for q in range(ngr):
                            n = (min(4 * q + 4, nt) - 4 * q) * P
                            act.wait_ge(turned_ps, j * ngr + q + 1)
                            act.wait_ge(masked, j * ngr + q + 1)
                            act.activation(turned[:, q, 0:n], pt[:, q, 0:n], ACT.Copy,
                                           accum_out=part[:, ds(j, 1), q]).then_inc(copied, 1)

            @block.vector
            def _(dve):
                with dve.Fori(0, nt // gt) as k:
                    for u in range(gt):
                        j = k * gt + u
                        dve.wait_ge(mask_out[u], (k + 1) * 16)
                        for q in range(ngr):
                            n = (min(4 * q + 4, nt) - 4 * q) * P
                            dve.wait_ge(copied, j * ngr + q + 1 + ngr)
                            dve.tensor_scalar(mask[:, u, 4 * q * P:4 * q * P + n], turned[:, q, 0:n], 0.5, FAR,
                                              ALU.is_lt, ALU.mult).then_inc(masked, 1)
                dve.wait_ge(copied, (nt + 1) * ngr)
                if degree is not None:
                    dve.tensor_reduce(degree[:, 0:nt], part[:], AX, ALU.add).then_inc(summed, 1)



def layernorm(nc, tag, x, xn, unit=False):
    with Scope(nc, tag) as s:
        stats = s.sb("stats", [P, T, 6])
        mv = s.sb("mv", [P, T, 2])
        rstd = s.sb("rstd", [P, T])
        size = s.sb("size", [P, T])
        with stage(nc, tag, "stat", "agg", "eps", "root", "step", "done") as (block, stat, agg, eps, root, step, done):
            @block.vector
            def _(dve):
                link = Link(dve, step)
                with dve.Fori(0, T) as t:
                    dve.bn_stats(stats[:, ds(t, 1), :].rearrange("p a b -> p (a b)"),
                                 x[:, ds(t, 1), :].rearrange("p a b -> p (a b)")).then_inc(stat, 1)
                dve.wait_ge(stat, T)
                for t in range(T):
                    dve.bn_aggr(mv[:, t, :], stats[:, t, :]).then_inc(agg, 1)
                dve.wait_ge(agg, T)
                if unit:
                    dve.tensor_scalar(size[:], mv[:, :, 1], float(D), None, ALU.mult).then_inc(eps, 1)
                dve.tensor_scalar(rstd[:], mv[:, :, 1], 1e-5, None, ALU.add).then_inc(eps, 1)
                dve.wait_ge(root, 2 if unit else 1)
                link(dve.reciprocal(rstd[:], rstd[:]))
                if unit:
                    link(dve.tensor_tensor(size[:], size[:], rstd[:], ALU.mult))
                    link(dve.tensor_scalar(size[:], size[:], 1e-12, None, ALU.max))
                    link(dve.reciprocal(size[:], size[:]))
                    link(dve.tensor_tensor(rstd[:], rstd[:], size[:], ALU.mult))
                with dve.Fori(0, T) as t:
                    dve.tensor_scalar(xn[:, ds(t, 1), :].rearrange("p a b -> p (a b)"),
                                      x[:, ds(t, 1), :].rearrange("p a b -> p (a b)"),
                                      mv[:, ds(t, 1), 0], rstd[:, ds(t, 1)],
                                      ALU.subtract, ALU.mult).then_inc(done, 1)

            @block.scalar
            def _(act):
                if unit:
                    act.wait_ge(eps, 1)
                    act.activation(size[:], size[:], ACT.Sqrt).then_inc(root, 1)
                act.wait_ge(eps, 2 if unit else 1)
                act.activation(rstd[:], rstd[:], ACT.Sqrt).then_inc(root, 1)


def turn(nc, tag, nm, fm, ident, bias=None, func=ACT.Identity):
    with Scope(nc, tag) as s:
        pt = s.ps("pt", [P, 4, KD, 2 * P])
        with stage(nc, tag, "turned", "out") as (block, turned, out):
            pairs = [(t, min(2, T - t)) for t in range(0, T, 2)]

            @block.tensor
            def _(pe):
                for i, (t, n) in enumerate(pairs):
                    if i >= 4:
                        pe.wait_ge(out, i - 3)
                    for j in range(n):
                        for k in range(KD):
                            last = pe.transpose(pt[:, i % 4, k, j * P:(j + 1) * P], nm[:, t + j, k * P:(k + 1) * P],
                                                ident[:])
                    last.then_inc(turned, 1)

            @block.scalar
            def _(act):
                for i, (t, n) in enumerate(pairs):
                    act.wait_ge(turned, i + 1)
                    if bias is None:
                        last = act.activation(fm[:, :, t * P:(t + n) * P], pt[:, i % 4, :, 0:n * P], func)
                    else:
                        for k in range(KD):
                            last = act.activation(fm[:, k, t * P:(t + n) * P], pt[:, i % 4, k, 0:n * P], func,
                                                  bias=bias[:, k:k + 1])
                    last.then_inc(out, 1)


def product_nm(nc, tag, fm, w, width, store):
    kk = w.shape[1]
    with Scope(nc, tag) as s:
        acc = s.ps("acc", [P, 8, 512])
        with stage(nc, tag, "done", "stored") as (block, done, stored):
            @block.tensor
            def _(pe):
                for t in range(T):
                    if t >= 8:
                        pe.wait_ge(stored, t - 7)
                    for k in range(kk):
                        last = pe.matmul(acc[:, t % 8, 0:width], fm[:, k, t * P:(t + 1) * P], w[:, k, :],
                                         start=(k == 0), stop=(k == kk - 1))
                    last.then_inc(done, 1)

            @block.vector
            def _(dve):
                for t in range(T):
                    dve.wait_ge(done, t + 1)
                    store(dve, t, acc[:, t % 8, 0:width]).then_inc(stored, 1)


def product_fm(nc, tag, srcs, w, dst, func, bias):
    kk, m_all = w.shape[1], w.shape[2]
    mm = m_all // P
    n = 400
    with Scope(nc, tag) as s:
        acc = s.ps("acc", [P, 2, mm, 512])
        with stage(nc, tag, "done", "stored") as (block, done, stored):
            @block.tensor
            def _(pe):
                pe.sem_inc(stored, 2 * mm)
                with pe.Fori(0, NP // n // 2) as i:
                    for b in range(2):
                        for m in range(mm):
                            pe.wait_ge(stored, (2 * i + b) * mm + m + 1)
                            for k in range(kk):
                                last = pe.matmul(acc[:, b, m, 0:n], w[:, k, m * P:(m + 1) * P],
                                                 srcs[k][:, ds((2 * i + b) * n, n)], start=(k == 0), stop=(k == kk - 1))
                            last.then_inc(done, 1)

            @block.scalar
            def _(act):
                with act.Fori(0, NP // n // 2) as i:
                    for b in range(2):
                        for m in range(mm):
                            act.wait_ge(done, (2 * i + b) * mm + m + 1)
                            act.activation(dst[:, m, ds((2 * i + b) * n, n)], acc[:, b, m, 0:n], func,
                                           bias=bias[:, m:m + 1]).then_inc(stored, 1)


def load(nc, tag, *pairs):
    with stage(nc, tag, "loaded") as (block, loaded):
        @block.sync
        def _(sp):
            with nc.allow_non_contiguous_dma(reason="short vectors by columns"):
                for dst, src in pairs:
                    sp.dma_start(dst, src).then_inc(loaded, 16)
            sp.wait_ge(loaded, 16 * len(pairs))


def columns_to_rows(nc, tag, cols, n, ident, dram, rows):
    with Scope(nc, tag) as s:
        pt = s.ps("pt", [P, P])
        flat = s.sb("flat", [P, P])
        with stage(nc, tag, "turned", "copied", "moved") as (block, turned, copied, moved):
            @block.tensor
            def _(pe):
                pe.transpose(pt[0:n, :], cols, ident[:]).then_inc(turned, 1)

            @block.vector
            def _(dve):
                dve.wait_ge(turned, 1)
                dve.tensor_copy(flat[0:n, :], pt[0:n, :]).then_inc(copied, 1)

            @block.sync
            def _(sp):
                sp.wait_ge(copied, 1)
                sp.dma_start(dram[0:n * P].rearrange("(q p) -> q p", p=P), flat[0:n, :]).then_inc(moved, 16)
                sp.wait_ge(moved, 16)
                sp.dma_start(rows, across(dram[0:n * P], n * P)).then_inc(moved, 16)
                sp.wait_ge(moved, 32)



def aggregate(nc, tag, c, table, nt, gt, rhs, width, out, scale=None, attention=None, eps=0.0):
    n_pad = nt * P
    ng = nt // gt
    cols = gt * P
    table2 = table[0:n_pad * n_pad, 0].rearrange("(r n) -> r n", n=n_pad)
    with Scope(nc, tag) as s:
        counts = s.sb("counts", [P, gt, cols])
        narrow = width <= P
        acc = s.ps("acc", [P, 2 if narrow else gt, 512])
        if narrow:
            half = cols // 2
            flat = s.sb("flat", [width, cols])
            back = s.ps("back", [P, gt, width])
        if attention:
            rows, es, es2 = attention
            p = s.sb("p", [P, gt, cols])
            total = s.sb("total", [P, gt])
            warm = s.sb("warm", [P, 1])
        with stage(nc, tag, *[f"counts_in{u}" for u in range(gt)], "counts_free", "sums_ready", "sums_free",
                   "low_ready", "score_ready", "exp_ready", "clamped", "weighted_dve", "weighted_pool", "step",
                   "flat_ready", "back_ready", "begun", "begun_pe") as (
                block, *sems):
            counts_in = sems[:gt]
            (counts_free, sums_ready, sums_free, low_ready, score_ready, exp_ready, clamped, weighted_dve,
             weighted_pool, step, flat_ready, back_ready,
             begun, begun_pe) = sems[gt:]
            weighted = [weighted_dve, weighted_pool]
            pool_slots = (0,)

            def by_pool(u):
                return u in pool_slots

            def nth(u, round_):
                mine = [v for v in range(gt) if by_pool(v) == by_pool(u)]
                return round_ * len(mine) + mine.index(u)

            @block.sync
            def _(sp):
                with sp.Fori(0, ng) as g:
                    with sp.Fori(0, ng) as k:
                        for u in range(gt):
                            sp.wait_ge(counts_free, (g * ng + k) * gt + u + 1)
                            sp.dma_start(counts[:, u, :], table2[ds((k * gt + u) * P, P), ds(g * cols, cols)]
                                         ).then_inc(counts_in[u], 16)

            def narrow_group(pe, g):
                for t in range(nt):
                    u = t % gt
                    pe.wait_ge(weighted[by_pool(u)], nth(u, g * ng + t // gt + 1) + 1)
                    for j in range(2):
                        last = pe.matmul(acc[0:width, j, 0:half], rhs(t), counts[:, u, j * half:(j + 1) * half],
                                         start=(t == 0), stop=(t == nt - 1), skip_group_check=True)
                    last.then_inc(counts_free, 1)
                pe.wait_ge(counts_free, (g + 1) * nt + gt)
                pe.sem_inc(sums_ready, 1)
                pe.wait_ge(flat_ready, g + 1)
                pe.sem_inc(begun_pe, 1)
                for j in range(gt):
                    last = pe.transpose(back[:, j, :], flat[:, j * P:(j + 1) * P], c.ident[0:width, 0:width])
                last.then_inc(back_ready, 1)

            def wide_group(pe, g):
                for j in range(gt):
                    pe.matmul(acc[:, j, 0:width], c.zero[0:1, 0:P], c.zero[0:1, 0:width], start=True, stop=False,
                              skip_group_check=True)
                with pe.Fori(0, ng) as k:
                    for u in range(gt):
                        if attention:
                            pe.wait_ge(weighted[by_pool(u)], nth(u, g * ng + k + 1) + 1)
                        else:
                            pe.wait_ge(counts_in[u], (g * ng + k + 1) * 16)
                        for j in range(gt):
                            last = pe.matmul(acc[:, j, 0:width], counts[:, u, j * P:(j + 1) * P],
                                             rhs(k * gt + u), start=False, stop=False, skip_group_check=True)
                        last.then_inc(counts_free, 1)
                for j in range(gt):
                    last = pe.matmul(acc[:, j, 0:width], c.zero[0:1, 0:P], c.zero[0:1, 0:width], start=False,
                                     stop=True, skip_group_check=True)
                last.then_inc(sums_ready, 1)

            @block.tensor
            def _(pe):
                pe.sem_inc(counts_free, gt)
                pe.sem_inc(sums_free, 1)
                if attention:
                    pe.sem_inc(weighted_pool, len(pool_slots))
                    pe.sem_inc(weighted_dve, gt - len(pool_slots))
                with pe.Fori(0, ng) as g:
                    pe.wait_ge(sums_free, g + 1)
                    (narrow_group if narrow else wide_group)(pe, g)

            if attention:
                @block.gpsimd
                def _(pool):
                    with pool.Fori(0, ng) as g:
                        with pool.Fori(0, ng) as k:
                            for u in pool_slots:
                                pool.wait_ge(exp_ready, (g * ng + k) * gt + u + 1)
                                pool.sem_inc(begun, 1)
                                pool.tensor_scalar(p[:, u, :], p[:, u, :], 1.0, None, ALU.min).then_inc(clamped, 1)
                                pool.wait_ge(counts_in[u], (g * ng + k + 1) * 16)
                                pool.wait_ge(clamped, nth(u, g * ng + k) + 1)
                                pool.tensor_tensor(counts[:, u, :], p[:, u, :], counts[:, u, :], ALU.mult
                                                   ).then_inc(weighted_pool, 1)

                @block.scalar
                def _(act):
                    act.activation(warm[:], c.ident[:, 0:1], ACT.Exp)
                    with act.Fori(0, ng) as g:
                        with act.Fori(0, ng) as k:
                            at = (g * ng + k) * gt
                            for u in range(gt):
                                act.wait_ge(weighted[by_pool(u)], nth(u, g * ng + k) + 1)
                                act.activation(p[:, u, :], rows[:, 1, ds(g * cols, cols)], ACT.Identity,
                                               bias=es2[:, ds(k * gt + u, 1)]).then_inc(low_ready, 1)
                            for u in range(gt):
                                act.wait_ge(score_ready, at + u + 1)
                                act.activation(p[:, u, :], p[:, u, :], ACT.Exp).then_inc(exp_ready, 1)

            @block.vector
            def _(dve):
                dve.sem_inc(step, 1)
                with dve.Fori(0, ng) as g:
                    if attention:
                        with dve.Fori(0, ng) as k:
                            at = (g * ng + k) * gt
                            for u in range(gt):
                                dve.wait_ge(low_ready, at + u + 1)
                                dve.scalar_tensor_tensor(out=p[:, u, :], in0=rows[:, 0, ds(g * cols, cols)],
                                                         scalar=es[:, ds(k * gt + u, 1)], in1=p[:, u, :],
                                                         op0=ALU.add, op1=ALU.max).then_inc(score_ready, 1)
                            for u in range(gt):
                                if by_pool(u):
                                    continue
                                dve.wait_ge(exp_ready, at + u + 1)
                                dve.wait_ge(counts_in[u], (g * ng + k + 1) * 16)
                                dve.scalar_tensor_tensor(out=counts[:, u, :], in0=p[:, u, :], scalar=1.0,
                                                         in1=counts[:, u, :], op0=ALU.min, op1=ALU.mult
                                                         ).then_inc(weighted_dve, 1)
                    dve.wait_ge(sums_ready, g + 1)
                    sums = acc
                    if narrow:
                        dve.tensor_copy(flat[:].rearrange("w (j n) -> w j n", j=2), acc[0:width, :, 0:half]
                                        ).then_inc(flat_ready, 1)
                        dve.wait_ge(back_ready, g + 1)
                        sums = back
                    if attention:
                        f = width - 1
                        dve.tensor_scalar(total[:], sums[:, :, f], eps, None, ALU.add).then_inc(step, 1)
                        dve.wait_ge(step, 2 * g + 2)
                        dve.reciprocal(total[:], total[:]).then_inc(step, 1)
                        dve.wait_ge(step, 2 * g + 3)
                        for j in range(gt):
                            last = dve.tensor_scalar(out(g * gt + j), sums[:, j, 0:f], total[:, j:j + 1], None, ALU.mult)
                    else:
                        for j in range(gt):
                            if scale is None:
                                last = dve.tensor_copy(out(g * gt + j), acc[:, j, 0:width])
                            else:
                                last = dve.tensor_scalar(out(g * gt + j), acc[:, j, 0:width],
                                                         scale[:, ds(g * gt + j, 1)], None, ALU.mult)
                    last.then_inc(sums_free, 1)


def neighbour_max(nc, tag, far, nt, gt, heads, es_rows, smax):
    n_pad = nt * P
    with Scope(nc, tag) as s:
        mask = s.sb("mask", [P, gt, n_pad], BF16)
        junk = s.sb("junk", [P, n_pad], BF16)
        with stage(nc, tag, *[f"mask_in{u}" for u in range(gt)], "seen") as (block, *sems):
            mask_in, seen = sems[:gt], sems[gt]

            @block.sync
            def _(sp):
                for t in range(nt):
                    if t >= gt:
                        sp.wait_ge(seen, (t - gt + 1) * heads)
                    sp.dma_start(mask[:, t % gt, :], far[t * P:(t + 1) * P, :]).then_inc(mask_in[t % gt], 16)

            @block.vector
            def _(dve):
                link = Link(dve, seen)
                for t in range(nt):
                    dve.wait_ge(mask_in[t % gt], (t // gt + 1) * 16)
                    for h in range(heads):
                        link(dve.tensor_tensor_reduce(junk[:], es_rows[:, h, :], mask[:, t % gt, :], 1.0, -3e38,
                                                      ALU.add, ALU.max, smax[:, h, t:t + 1]))


def gat(nc, tag, c, fm, w, w_cols, a_src, a_dst, heads, table, far, nt, gt, dram, out_tile, eps, tail=None):
    ch = w_cols // heads
    n_pad = nt * P
    with Scope(nc, tag) as s:
        h = s.sb("h", [P, T, heads, ch + 1])
        ec = s.sb("ec", [P, 2 * heads, nt])
        smax = s.sb("smax", [P, heads, nt])
        es2 = s.sb("es2", [P, heads, nt])
        shift = s.sb("shift", [P, heads, 2, nt])
        with Scope(nc, tag + "w") as q:
            wx = q.sb("wx", [P, KD, w_cols + 2 * heads])
            att = q.sb("att", [P, 2, w_cols])
            prod = q.sb("prod", [P, KD, 2, w_cols])
            load(nc, tag + "_load", (wx[:, :, 0:w_cols], w.rearrange("(k p) n -> p k n", p=P)),
                 (att[:, 0, :], across(a_src, w_cols)), (att[:, 1, :], across(a_dst, w_cols)))
            with stage(nc, tag + "_wa", "mul", "red") as (block, mul, red):
                @block.vector
                def _(dve):
                    for k in range(KD):
                        for a in range(2):
                            dve.tensor_tensor(prod[:, k, a, :], wx[:, k, 0:w_cols], att[:, a, :], ALU.mult).then_inc(mul, 1)
                    dve.wait_ge(mul, 2 * KD)
                    for k in range(KD):
                        for a in range(2):
                            dve.tensor_reduce(wx[:, k, w_cols + a * heads:w_cols + (a + 1) * heads],
                                              prod[:, k, a, :].rearrange("p (h c) -> p h c", h=heads), AX, ALU.add
                                              ).then_inc(red, 1)
                    dve.memset(h[:, :, :, ch:ch + 1], 1.0)

            def store(dve, t, ps):
                if t < nt:
                    dve.tensor_copy(ec[:, :, t], ps[:, w_cols:w_cols + 2 * heads])
                if t >= nt and tail is not None:
                    dve.tensor_copy(tail(t), ps[:, 0:w_cols])
                return dve.tensor_copy(h[:, t, :, 0:ch], ps[:, 0:w_cols].rearrange("p (h c) -> p h c", h=heads))

            product_nm(nc, tag + "_h", fm, wx, w_cols + 2 * heads, store)
        with Scope(nc, tag + "m") as q:
            es_rows = q.sb("es_rows", [P, heads, n_pad])
            columns_to_rows(nc, tag + "_es", ec[:, 0:heads, :].rearrange("p h t -> p (h t)"), heads * nt, c.ident, dram,
                            es_rows[:].rearrange("p h n -> p (h n)"))
            neighbour_max(nc, tag + "_max", far, nt, gt, heads, es_rows, smax)
        with stage(nc, tag + "_shift", "step") as (block, step):
            @block.vector
            def _(dve):
                link = Link(dve, step)
                ed = ec[:, heads:2 * heads, :]
                link(dve.tensor_tensor(smax[:], smax[:], ed, ALU.add))
                link(dve.scalar_tensor_tensor(out=smax[:], in0=smax[:], scalar=SLOPE, in1=smax[:], op0=ALU.mult, op1=ALU.max))
                link(dve.tensor_tensor(shift[:, :, 0, :], ed, smax[:], ALU.subtract))
                link(dve.scalar_tensor_tensor(out=shift[:, :, 1, :], in0=ed, scalar=SLOPE, in1=smax[:], op0=ALU.mult,
                                              op1=ALU.subtract))
                link(dve.tensor_scalar(es2[:], ec[:, 0:heads, :], SLOPE, None, ALU.mult))
        with Scope(nc, tag + "r") as q:
            rows = q.sb("rows", [P, 2, n_pad])
            for i in range(heads):
                columns_to_rows(nc, f"{tag}_rows{i}", shift[:, i, :, :].rearrange("p a t -> p (a t)"), 2 * nt, c.ident,
                                dram, rows[:].rearrange("p a n -> p (a n)"))
                aggregate(nc, f"{tag}_agg{i}", c, table, nt, gt,
                          lambda t, i=i: h[:, ds(t, 1), i, :].rearrange("p a c -> p (a c)"), ch + 1,
                          lambda t, i=i: out_tile(t, i), attention=(rows, ec[:, i, :], es2[:, i, :]), eps=eps)



def first_max(dve, link, s, n, prio, top, onehot, tmp):
    link(dve.tensor_reduce(top[:], s[:], AX, ALU.max))
    link(dve.tensor_tensor(onehot[:], s[:], over_last(top[:], n), ALU.is_equal))
    link(dve.tensor_tensor(onehot[:], onehot[:], over_mid(prio[:, 0:n], T), ALU.mult))
    link(dve.tensor_reduce(tmp[:], onehot[:], AX, ALU.max))
    link(dve.tensor_tensor(onehot[:], onehot[:], over_last(tmp[:], n), ALU.is_equal))


def top2_gates(nc, tag, c, score, n, gate):
    with Scope(nc, tag) as s:
        prio = s.sb("prio", [P, n])
        top = s.sb("top", [P, T])
        top_b = s.sb("top_b", [P, T])
        one = s.sb("one", [P, T, n])
        tmp = s.sb("tmp", [P, T])
        ratio = s.sb("ratio", [P, T])
        with stage(nc, tag, "prio_set", "step", "diff", "expd") as (block, prio_set, step, diff, expd):
            @block.gpsimd
            def _(pool):
                pool.iota(prio[:], pattern=[[-1, n]], base=n, channel_multiplier=0,
                          allow_small_or_imprecise_dtypes=True).then_inc(prio_set, 1)

            @block.vector
            def _(dve):
                link = Link(dve, step)
                dve.wait_ge(prio_set, 1)
                first_max(dve, link, score, n, prio, top, gate, tmp)
                link(dve.scalar_tensor_tensor(out=score[:], in0=gate[:], scalar=-3e38, in1=score[:], op0=ALU.mult,
                                              op1=ALU.add))
                first_max(dve, link, score, n, prio, top_b, one, tmp)
                link(dve.tensor_tensor(ratio[:], top_b[:], top[:], ALU.subtract))
                dve.sem_inc(diff, 1)
                dve.wait_ge(expd, 1)
                link(dve.tensor_scalar(tmp[:], ratio[:], 1.0, None, ALU.add))
                link(dve.reciprocal(tmp[:], tmp[:]))
                link(dve.tensor_tensor(ratio[:], ratio[:], tmp[:], ALU.mult))
                link(dve.tensor_tensor(gate[:], gate[:], over_last(tmp[:], n), ALU.mult))
                link(dve.tensor_tensor(one[:], one[:], over_last(ratio[:], n), ALU.mult))
                link(dve.tensor_tensor(gate[:], gate[:], one[:], ALU.add))

            @block.scalar
            def _(act):
                act.wait_ge(diff, 1)
                act.activation(ratio[:], ratio[:], ACT.Exp).then_inc(expd, 1)


def softmax(nc, tag, logit, n, bias):
    with Scope(nc, tag) as s:
        top = s.sb("top", [P, T])
        with stage(nc, tag, "step", "shifted", "expd") as (block, step, shifted, expd):
            @block.vector
            def _(dve):
                link = Link(dve, step)
                link(dve.tensor_tensor(logit[:], logit[:], over_mid(bias[:], T), ALU.add))
                link(dve.tensor_reduce(top[:], logit[:], AX, ALU.max))
                dve.tensor_tensor(logit[:], logit[:], over_last(top[:], n), ALU.subtract).then_inc(shifted, 1)
                dve.wait_ge(expd, 1)
                link(dve.tensor_reduce(top[:], logit[:], AX, ALU.add))
                link(dve.reciprocal(top[:], top[:]))
                link(dve.tensor_tensor(logit[:], logit[:], over_last(top[:], n), ALU.mult))

            @block.scalar
            def _(act):
                act.wait_ge(shifted, 1)
                act.activation(logit[:], logit[:], ACT.Exp).then_inc(expd, 1)


def turn_gates(nc, tag, c, gate, n, gate_fm):
    with Scope(nc, tag) as s:
        pt = s.ps("pt", [n, 4, 4 * P])
        with stage(nc, tag, "turned", "out") as (block, turned, out):
            quads = [(t, min(4, T - t)) for t in range(0, T, 4)]

            @block.tensor
            def _(pe):
                for i, (t, m) in enumerate(quads):
                    if i >= 4:
                        pe.wait_ge(out, i - 3)
                    for j in range(m):
                        last = pe.transpose(pt[:, i % 4, j * P:(j + 1) * P], gate[:, t + j, :], c.ident[:])
                    last.then_inc(turned, 1)

            @block.vector
            def _(dve):
                for i, (t, m) in enumerate(quads):
                    dve.wait_ge(turned, i + 1)
                    dve.tensor_copy(gate_fm[:, t * P:(t + m) * P], pt[:, i % 4, 0:m * P]).then_inc(out, 1)


def experts(nc, tag, c, fm, x, gate, n_e, layers, last_w, last_bias):
    half = G1 * P // 2
    chunk = G1 * P
    nh = [2 if i == 0 else 1 for i in range(len(layers))]
    blocks = sum(m for _, _, m, _, _, _ in layers)
    k_last = layers[-1][2]
    with Scope(nc, tag) as s:
        gate_fm = s.sb("gate_fm", [n_e, NP])
        turn_gates(nc, tag + "_gt", c, gate, n_e, gate_fm)
        gate_c = s.sb("gate_c", [n_e, 2, chunk])
        hid = [s.sb(f"hid{i}", [P, nh[i], m, chunk]) for i, (_, _, m, _, _, _) in enumerate(layers)]
        ph = s.ps("ph", [P, 2, 2, 512])
        py = s.ps("py", [P, 4, 512])
        with stage(nc, tag, "gate_in", "gate_free", "hid_ready", "hid_read", *[f"act{i}" for i in range(len(layers))],
                   *[f"used{i}" for i in range(len(layers))], "y_ready", "y_free") as (block, *sems):
            gate_in, gate_free, hid_ready, hid_read = sems[:4]
            nl = len(layers)
            acted, used = sems[4:4 + nl], sems[4 + nl:4 + 2 * nl]
            y_ready, y_free = sems[4 + 2 * nl:]

            order = [(0, 0)]
            for e in range(n_e):
                order += [(i, e) for i in range(1, min(2, nl))]
                order += [(0, e + 1)] * (e + 1 < n_e)
                order += [(i, e) for i in range(2, nl)] + [("y", e)]

            @block.gpsimd
            def _(pool):
                with pool.Fori(0, T // G1) as g:
                    pool.wait_ge(gate_free, g + 1)
                    pool.tensor_copy(gate_c[:, 0, :], gate_fm[:, ds(g * chunk, chunk)]).then_inc(gate_in, 1)

            @block.tensor
            def _(pe):
                pe.sem_inc(hid_read, 2)
                pe.sem_inc(y_free, 5)
                pe.sem_inc(gate_free, 1)
                for i in range(nl):
                    pe.sem_inc(used[i], nh[i])
                with pe.Fori(0, T // G1) as g:
                    pe.wait_ge(gate_in, g + 1)
                    for tt in range(G1):
                        pe.wait_ge(y_free, g * (G1 * (n_e + 1)) + max(tt + 2, 5))
                        last = pe.matmul(py[:, tt % 4, 0:D], gate_c[:, 0, tt * P:(tt + 1) * P], last_bias[:],
                                         start=True, stop=True)
                        last.then_inc(y_ready, 1)
                    pe.wait_ge(y_ready, g * (G1 * (n_e + 1)) + G1)
                    pe.sem_inc(gate_free, 1)
                    nb, ny = 0, G1
                    for kind, e in order:
                        if kind == "y":
                            pe.wait_ge(acted[-1], g * (n_e * k_last) + (e + 1) * k_last)
                            for tt in range(G1):
                                pe.wait_ge(y_free, g * (G1 * (n_e + 1)) + ny + 2)
                                for k in range(k_last):
                                    last = pe.matmul(py[:, ny % 4, 0:D], hid[-1][:, e % nh[-1], k, tt * P:(tt + 1) * P],
                                                     last_w[:, e, k, :], start=(k == 0), stop=(k == k_last - 1))
                                last.then_inc(y_ready, 1)
                                ny += 1
                            pe.wait_ge(y_ready, g * (G1 * (n_e + 1)) + ny)
                            pe.sem_inc(used[-1], 1)
                            continue
                        w, kk, mm, _, _, _ = layers[kind]
                        if kind:
                            km = layers[kind - 1][2]
                            pe.wait_ge(acted[kind - 1], g * (n_e * km) + (e + 1) * km)
                        for m in range(mm):
                            pe.wait_ge(hid_read, g * (blocks * n_e) + nb + 1)
                            for j in range(2):
                                for k in range(kk):
                                    rhs = (fm[:, k, ds(g * chunk + j * half, half)] if kind == 0 else
                                           hid[kind - 1][:, e % nh[kind - 1], k, j * half:(j + 1) * half])
                                    last = pe.matmul(ph[:, nb % 2, j, 0:half], w[:, e, k, m * P:(m + 1) * P], rhs,
                                                     start=(k == 0), stop=(k == kk - 1))
                            last.then_inc(hid_ready, 1)
                            nb += 1
                        if kind:
                            pe.wait_ge(hid_ready, g * (blocks * n_e) + nb)
                            pe.sem_inc(used[kind - 1], 1)

            @block.scalar
            def _(act):
                with act.Fori(0, T // G1) as g:
                    nb = 0
                    for kind, e in order:
                        if kind == "y":
                            continue
                        _, _, mm, func, scale, bias = layers[kind]
                        act.wait_ge(used[kind], g * n_e + e + 1)
                        for m in range(mm):
                            act.wait_ge(hid_ready, g * (blocks * n_e) + nb + 1)
                            act.activation(hid[kind][:, e % nh[kind], m, :].rearrange("p (j n) -> p j n", j=2),
                                           ph[:, nb % 2, :, 0:half], func, bias=bias[:, e, m:m + 1],
                                           scale=1.0 if scale is None else scale[:, e, m:m + 1]
                                           ).then_inc(acted[kind], 1)
                            act.wait_ge(acted[kind], g * (n_e * mm) + e * mm + m + 1)
                            act.sem_inc(hid_read, 1)
                            nb += 1

            @block.vector
            def _(dve):
                with dve.Fori(0, T // G1) as g:
                    ny = 0
                    for e in range(-1, n_e):
                        for tt in range(G1):
                            xt = x[:, ds(g * G1 + tt, 1), :].rearrange("p a d -> p (a d)")
                            at = g * (G1 * (n_e + 1)) + ny
                            dve.wait_ge(y_ready, at + 1)
                            dve.wait_ge(y_free, at + 1)
                            if e < 0:
                                ins = dve.tensor_tensor(xt, py[:, ny % 4, 0:D], xt, ALU.add)
                            else:
                                ins = dve.scalar_tensor_tensor(
                                    out=xt, in0=py[:, ny % 4, 0:D], scalar=gate[:, ds(g * G1 + tt, 1), e], in1=xt,
                                    op0=ALU.mult, op1=ALU.add)
                            ins.then_inc(y_free, 1)
                            ny += 1



def finish_rows(nc, tag, x, a, bias, relu, unit):
    with Scope(nc, tag) as s:
        sq = s.sb("sq", [P, 2, D])
        ss = s.sb("ss", [P, T])
        with stage(nc, tag, "biased", "squared", "root", "step", "added") as (block, biased, squared, root, step, added):
            @block.vector
            def _(dve):
                link = Link(dve, step)
                if bias is not None:
                    link(dve.tensor_tensor(a[:], a[:], over_mid(bias[:], T), ALU.add))
                if relu:
                    link(dve.tensor_scalar(a[:], a[:], 0.0, None, ALU.max))
                dve.sem_inc(biased, 1)
                if not unit:
                    link(dve.tensor_tensor(x[:], x[:], a[:], ALU.add))
                    return
                dve.wait_ge(root, 1)
                link(dve.tensor_scalar(ss[:], ss[:], 1e-12, None, ALU.max))
                link(dve.reciprocal(ss[:], ss[:]))
                with dve.Fori(0, T) as t:
                    xt = x[:, ds(t, 1), :].rearrange("p a d -> p (a d)")
                    dve.scalar_tensor_tensor(out=xt, in0=a[:, ds(t, 1), :].rearrange("p a d -> p (a d)"),
                                             scalar=ss[:, ds(t, 1)], in1=xt, op0=ALU.mult, op1=ALU.add).then_inc(added, 1)

            if unit:
                @block.scalar
                def _(act):
                    act.wait_ge(biased, 1)
                    for t in range(T):
                        if t >= 2:
                            act.wait_ge(squared, t - 1)
                        act.activation(sq[:, t % 2, :], a[:, t, :], ACT.Square, accum_out=ss[:, t:t + 1]).then_inc(squared, 1)
                    act.wait_ge(squared, T)
                    act.activation(ss[:], ss[:], ACT.Sqrt).then_inc(root, 1)


def batchnorm_columns(nc, tag, fm, gamma, beta, scale, shift):
    n = 500
    nb = -(-N // n)
    with Scope(nc, tag) as s:
        stats = s.sb("stats", [P, KD, nb, 6])
        mv = s.sb("mv", [P, KD, 2])
        with stage(nc, tag, "stat", "eps", "root", "step") as (block, stat, eps, root, step):
            @block.vector
            def _(dve):
                link = Link(dve, step)
                for k in range(KD):
                    for b in range(nb):
                        dve.bn_stats(stats[:, k, b, :], fm[:, k, b * n:min((b + 1) * n, N)]).then_inc(stat, 1)
                dve.wait_ge(stat, KD * nb)
                for k in range(KD):
                    link(dve.bn_aggr(mv[:, k, :], stats[:, k].rearrange("p b s -> p (b s)")))
                dve.tensor_scalar(scale[:], mv[:, :, 1], 1e-5, None, ALU.add).then_inc(eps, 1)
                dve.wait_ge(root, 1)
                link(dve.reciprocal(scale[:], scale[:]))
                link(dve.tensor_tensor(scale[:], scale[:], gamma[:], ALU.mult))
                link(dve.tensor_tensor(shift[:], mv[:, :, 0], scale[:], ALU.mult))
                link(dve.tensor_tensor(shift[:], beta[:], shift[:], ALU.subtract))

            @block.scalar
            def _(act):
                act.wait_ge(eps, 1)
                act.activation(scale[:], scale[:], ACT.Sqrt).then_inc(root, 1)


def scale_relu(nc, tag, fm, scale, shift):
    with stage(nc, tag, "done") as (block, done):
        @block.scalar
        def _(act):
            act.activation(fm[:, 0, :], fm[:, 0, :], ACT.Relu, bias=shift[:, 0:1], scale=scale[:, 0:1]).then_inc(done, 1)

        @block.vector
        def _(dve):
            dve.tensor_scalar(fm[:, 1, :], fm[:, 1, :], scale[:, 1:2], shift[:, 1:2], ALU.mult, ALU.add).then_inc(done, 1)
            dve.wait_ge(done, 1)
            dve.wait_ge(done, 2)
            dve.tensor_scalar(fm[:, 1, :], fm[:, 1, :], 0.0, None, ALU.max)


class Consts:
    pass


def vec_cols(v):
    return v.rearrange("(m p) -> p m", p=P)


def build(nc, a, out):
    size1, size2 = NP * NP + W * P, N2 * N2 + W * P
    table1 = nc.dram_tensor("table1", (size1, 1), F32, kind="Internal").ap()
    table2 = nc.dram_tensor("table2", (size2, 1), F32, kind="Internal").ap()
    far1 = nc.dram_tensor("far1", (NP, NP), BF16, kind="Internal").ap()
    far2 = nc.dram_tensor("far2", (N2, N2), BF16, kind="Internal").ap()
    keys = nc.dram_tensor("edge_keys", ((NCH1 + NCH2) * P,), F32, kind="Internal").ap()
    dram = nc.dram_tensor("row_scratch", (P * P,), F32, kind="Internal").ap()
    with Scope(nc, "all") as top:
        c = Consts()
        c.routed = (nc.dram_tensor("routed_in", (ROUTED + NP, D), F32, kind="Internal").ap(),
                    nc.dram_tensor("routed_out", (ROUTED, D), F32, kind="Internal").ap())
        c.ident = top.sb("ident", [P, P])
        c.zero = top.sb("zero", [1, 512], BF16)
        degree = top.sb("degree", [P, T])
        x = top.sb("x", [P, T, D])
        full = N // P
        rest = N - full * P
        with stage(nc, "start", "set", "pad", "xin") as (block, set_, pad, xin):
            @block.gpsimd
            def _(pool):
                pool.memset(x[:, T - 1, :], 0.0).then_inc(pad, 1)
                pool.memset(c.ident[:], 0.0).then_inc(set_, 1)
                pool.memset(c.zero[:], 0.0).then_inc(set_, 1)
                pool.wait_ge(set_, 1)
                pool.wait_ge(set_, 2)
                pool.affine_select(out=c.ident[:], in_=c.ident[:], compare_op=ALU.not_equal, fill=1.0, base=0,
                                   pattern=[[-1, P]], channel_multiplier=1).then_inc(set_, 1)

            @block.sync
            def _(sp):
                sp.dma_start(x[:, 0:full, :], a["x"][0:full * P, :].rearrange("(t p) d -> p t d", p=P)).then_inc(xin, 16)
                sp.wait_ge(pad, 1)
                sp.dma_start(x[0:rest, full, :], a["x"][full * P:N, :]).then_inc(xin, 16)
                sp.wait_ge(xin, 32)
        landed = [top.cx.enter_context(nc.semaphore(f"edges{i}_landed")) for i in (1, 2)]
        c.put_landed = top.cx.enter_context(nc.semaphore("put_landed"))
        c.get_landed = [top.cx.enter_context(nc.semaphore(f"get{g}_landed")) for g in range(T // G1)]
        count_edges(nc, [(a["L0_ffn_edge_index"][0, :], a["L0_ffn_edge_index"][1, :], NCH2, N2, table2),
                         (a["src"], a["dst"], NCH1, NP, table1)], keys, c.ident, landed)
        mask_and_degrees(nc, "m1", table1, T, G1, far1, c.ident, degree)
        mask_and_degrees(nc, "m2", table2, T2, G2, far2, c.ident, None)
        dinv = top.sb("dinv", [P, T])
        with stage(nc, "dinv", "clamped", "root") as (block, clamped, root):
            @block.vector
            def _(dve):
                dve.tensor_scalar(dinv[:], degree[:], 1e-30, None, ALU.max).then_inc(clamped, 1)
                dve.wait_ge(root, 1)
                dve.reciprocal(dinv[:], dinv[:])

            @block.scalar
            def _(act):
                act.wait_ge(clamped, 1)
                act.activation(dinv[:], dinv[:], ACT.Sqrt).then_inc(root, 1)

        for name, part in PARTS:
            part(nc, c, a, x, (table1, far1, table2, far2), dinv, dram)

        with stage(nc, "end", "out") as (block, out_sem):
            @block.sync
            def _(sp):
                sp.dma_start(out[0:full * P, :].rearrange("(t p) d -> p t d", p=P), x[:, 0:full, :]).then_inc(out_sem, 16)
                sp.dma_start(out[full * P:N, :], x[0:rest, full, :]).then_inc(out_sem, 16)
                sp.wait_ge(out_sem, 32)


def l0_gnn(nc, c, a, x, tables, dinv, dram):
    with Scope(nc, "l0g") as s:
        xn = s.sb("xn", [P, T, D])
        xt = s.sb("xt", [P, KD, NP])
        h = s.sb("h", [P, T, D])
        w = s.sb("w", [P, 2, KD, D])
        gram = s.sb("gram", [P, KD, D])
        gw = s.sb("gw", [P, KD, D])
        bias = s.sb("bias", [P, D])
        load(nc, "l0g_load", (w[:, 0], a["L0_gnn_W_gcn"].rearrange("(k p) n -> p k n", p=P)),
             (w[:, 1], a["L0_gnn_W_V"].rearrange("(k p) n -> p k n", p=P)), (bias[:], across(a["L0_gnn_b_gcn"], D)))
        layernorm(nc, "l0g_ln", x, xn, unit=True)
        turn(nc, "l0g_t", xn, xt, c.ident)
        product_nm(nc, "l0g_w", xt, w[:, 0], D,
                   lambda dve, t, ps: dve.tensor_scalar(h[:, t, :], ps, dinv[:, t:t + 1], None, ALU.mult))
        with Scope(nc, "l0gg") as q:
            pg = q.ps("pg", [P, 2, KD, 512])
            with stage(nc, "l0g_gram", "gram_ps", "gram_sb", "gw_ps") as (block, gram_ps, gram_sb, gw_ps):
                @block.tensor
                def _(pe):
                    for m in range(KD):
                        for t in range(T):
                            last = pe.matmul(pg[:, 0, m, 0:D], xn[:, t, m * P:(m + 1) * P], xn[:, t, :],
                                             start=(t == 0), stop=(t == T - 1))
                    last.then_inc(gram_ps, 1)
                    pe.wait_ge(gram_sb, 1)
                    for m in range(KD):
                        for k in range(KD):
                            last = pe.matmul(pg[:, 1, m, 0:D], gram[:, k, m * P:(m + 1) * P], w[:, 1, k, :],
                                             start=(k == 0), stop=(k == KD - 1))
                    last.then_inc(gw_ps, 1)

                @block.vector
                def _(dve):
                    dve.wait_ge(gram_ps, 1)
                    dve.tensor_copy(gram[:], pg[:, 0, :, 0:D]).then_inc(gram_sb, 1)
                    dve.wait_ge(gw_ps, 1)
                    dve.tensor_copy(gw[:], pg[:, 1, :, 0:D])
        agg = xn
        aggregate(nc, "l0g_agg", c, tables[0], T, G1, lambda t: h[:, ds(t, 1), :].rearrange("p a d -> p (a d)"), D,
                  lambda t: agg[:, ds(t, 1), :].rearrange("p a d -> p (a d)"), scale=dinv)
        product_nm(nc, "l0g_z", xt, gw, D, lambda dve, t, ps: dve.scalar_tensor_tensor(
            out=agg[:, t, :], in0=ps, scalar=0.1 / N, in1=agg[:, t, :], op0=ALU.mult, op1=ALU.add))
        finish_rows(nc, "l0g_end", x, agg, bias, True, True)


def l0_ffn(nc, c, a, x, tables, dinv, dram):
    hd, ne = 4, 4
    with Scope(nc, "l0f") as s:
        xt = s.sb("xt", [P, KD, NP])
        gate = s.sb("gate", [P, T, ne])
        with Scope(nc, "l0fa") as q:
            xn = q.sb("xn", [P, T, D])
            layernorm(nc, "l0f_ln", x, xn)
            turn(nc, "l0f_t", xn, xt, c.ident)
        with Scope(nc, "l0fb") as q:
            agg = q.sb("agg", [P, T, hd * ne])
            rows = q.sb("rows", [P, 3, hd * ne])
            gat(nc, "l0f_gat", c, xt, a["L0_ffn_W_gat"], hd * ne, a["L0_ffn_att_src"].rearrange("h c -> (h c)"),
                a["L0_ffn_att_dst"].rearrange("h c -> (h c)"), hd, tables[2], tables[3], T2, G2, dram,
                lambda t, i: agg[:, ds(t, 1), i * ne:(i + 1) * ne].rearrange("p a d -> p (a d)"), 1e-16,
                tail=lambda t: agg[:, t, :])
            load(nc, "l0f_vec", (rows[:, 0], across(a["L0_ffn_b_gat"], hd * ne)),
                 (rows[:, 1], across(a["L0_ffn_ln_gamma"], hd * ne)), (rows[:, 2], across(a["L0_ffn_ln_beta"], hd * ne)))
            score = q.sb("score", [P, T, ne])
            sq = q.sb("sq", [P, T, hd * ne])
            m = q.sb("m", [P, T])
            v = q.sb("v", [P, T])
            with stage(nc, "l0f_score", "step", "ready", "root") as (block, step, ready, root):
                @block.vector
                def _(dve):
                    link = Link(dve, step)
                    n = hd * ne
                    link(dve.tensor_tensor(agg[:], agg[:], over_mid(rows[:, 0, :], T), ALU.add))
                    link(dve.tensor_reduce(m[:], agg[:], AX, ALU.add))
                    link(dve.tensor_scalar(m[:], m[:], 1.0 / n, None, ALU.mult))
                    link(dve.tensor_tensor(agg[:], agg[:], over_last(m[:], n), ALU.subtract))
                    link(dve.tensor_tensor(sq[:], agg[:], agg[:], ALU.mult))
                    link(dve.tensor_reduce(v[:], sq[:], AX, ALU.add))
                    dve.tensor_scalar(v[:], v[:], 1.0 / n, 1e-5, ALU.mult, ALU.add).then_inc(ready, 1)
                    dve.wait_ge(root, 1)
                    link(dve.reciprocal(v[:], v[:]))
                    link(dve.tensor_tensor(agg[:], agg[:], over_last(v[:], n), ALU.mult))
                    link(dve.tensor_tensor(agg[:], agg[:], over_mid(rows[:, 1, :], T), ALU.mult))
                    link(dve.tensor_tensor(agg[:], agg[:], over_mid(rows[:, 2, :], T), ALU.add))
                    link(dve.tensor_tensor(score[:], agg[:, :, 0:ne], agg[:, :, ne:2 * ne], ALU.add))
                    for i in range(2, hd):
                        link(dve.tensor_tensor(score[:], score[:], agg[:, :, i * ne:(i + 1) * ne], ALU.add))
                    link(dve.tensor_scalar(score[:], score[:], 1.0 / hd, None, ALU.mult))

                @block.scalar
                def _(act):
                    act.wait_ge(ready, 1)
                    act.activation(v[:], v[:], ACT.Sqrt).then_inc(root, 1)
            top2_gates(nc, "l0f_top", c, score, ne, gate)
        w1 = s.sb("w1", [P, ne, KD, 2 * D])
        b1 = s.sb("b1", [P, ne, 2 * KD])
        w2 = s.sb("w2", [P, ne, 2 * KD, D])
        b2 = s.sb("b2", [ne, D])
        load(nc, "l0f_load", *[(w1[:, e], a["L0_ffn_W1"][e].rearrange("(k p) n -> p k n", p=P)) for e in range(ne)],
             *[(w2[:, e], a["L0_ffn_W2"][e].rearrange("(k p) n -> p k n", p=P)) for e in range(ne)],
             *[(b1[:, e], vec_cols(a["L0_ffn_b1"][e])) for e in range(ne)], (b2[:], a["L0_ffn_b2"]))
        experts(nc, "l0f_moe", c, xt, x, gate, ne, [(w1, KD, 2 * KD, ACT.Gelu, None, b1)], w2, b2)


def l1_gnn(nc, c, a, x, tables, dinv, dram):
    with Scope(nc, "l1g") as s:
        xt = s.sb("xt", [P, KD, NP])
        agg = s.sb("agg", [P, T, D])
        bias = s.sb("bias", [P, KD])
        bias2 = s.sb("bias2", [P, D])
        with Scope(nc, "l1ga") as q:
            h = q.sb("h", [P, T, D])
            w = q.sb("w", [P, KD, D])
            load(nc, "l1g_load", (w[:], a["L1_gnn_W1"].rearrange("(k p) n -> p k n", p=P)),
                 (bias[:], vec_cols(a["L1_gnn_b1"])), (bias2[:], across(a["L1_gnn_b2"], D)))
            layernorm(nc, "l1g_ln", x, h)
            turn(nc, "l1g_t", h, xt, c.ident)
            product_nm(nc, "l1g_w", xt, w, D,
                       lambda dve, t, ps: dve.tensor_scalar(h[:, t, :], ps, dinv[:, t:t + 1], None, ALU.mult))
            aggregate(nc, "l1g_agg", c, tables[0], T, G1, lambda t: h[:, ds(t, 1), :].rearrange("p a d -> p (a d)"), D,
                      lambda t: agg[:, ds(t, 1), :].rearrange("p a d -> p (a d)"), scale=dinv)
        turn(nc, "l1g_t2", agg, xt, c.ident, bias=bias, func=ACT.Relu)
        gat(nc, "l1g_gat", c, xt, a["L1_gnn_W2"], D, a["L1_gnn_att_src"], a["L1_gnn_att_dst"], 1, tables[0], tables[1],
            T, G1, dram, lambda t, i: agg[:, ds(t, 1), :].rearrange("p a d -> p (a d)"), 1e-16)
        finish_rows(nc, "l1g_end", x, agg, bias2, True, False)


def normal_input(nc, tag, c, x, xt):
    with Scope(nc, tag + "n") as q:
        xn = q.sb("xn", [P, T, D])
        layernorm(nc, tag + "_ln", x, xn)
        turn(nc, tag + "_t", xn, xt, c.ident)


def l1_ffn(nc, c, a, x, tables, dinv, dram):
    ne = 8
    f = "L1_ffn_"
    with Scope(nc, "l1f") as s:
        xt = s.sb("xt", [P, KD, NP])
        gate = s.sb("gate", [P, T, ne])
        normal_input(nc, "l1f", c, x, xt)
        wr = s.sb("wr", [P, KD, ne])
        br = s.sb("br", [P, ne])
        ws = [s.sb(f"w{i}", [P, ne, KD, D]) for i in range(3)]
        vec = s.sb("vec", [P, 2, 5, ne, KD])
        bo = s.sb("bo", [ne, D])
        names = [["b1", "g1", "be1", "m1", "v1"], ["b2", "g2", "be2", "m2", "v2"]]
        load(nc, "l1f_load", (wr[:], a[f + "Wr"].rearrange("(k p) n -> p k n", p=P)), (br[:], across(a[f + "br"], ne)),
             *[(ws[i][:, e], a[f + n][e].rearrange("(k p) n -> p k n", p=P)) for i, n in enumerate(["W1", "W2", "Wo"])
               for e in range(ne)],
             *[(vec[:, i, j, e], vec_cols(a[f + names[i][j]][e])) for i in range(2) for j in range(5) for e in range(ne)],
             (bo[:], a[f + "bo"]))
        with stage(nc, "l1f_bn", "step", "ready", "root") as (block, step, ready, root):
            @block.vector
            def _(dve):
                link = Link(dve, step)
                dve.tensor_scalar(vec[:, :, 4], vec[:, :, 4], 1e-3, None, ALU.add).then_inc(ready, 1)
                dve.wait_ge(root, 1)
                link(dve.reciprocal(vec[:, :, 4], vec[:, :, 4]))
                link(dve.tensor_tensor(vec[:, :, 1], vec[:, :, 1], vec[:, :, 4], ALU.mult))
                link(dve.tensor_tensor(vec[:, :, 0], vec[:, :, 0], vec[:, :, 3], ALU.subtract))
                link(dve.tensor_tensor(vec[:, :, 0], vec[:, :, 0], vec[:, :, 1], ALU.mult))
                link(dve.tensor_tensor(vec[:, :, 0], vec[:, :, 0], vec[:, :, 2], ALU.add))

            @block.scalar
            def _(act):
                act.wait_ge(ready, 1)
                act.activation(vec[:, :, 4], vec[:, :, 4], ACT.Sqrt).then_inc(root, 1)
        product_nm(nc, "l1f_r", xt, wr, ne, lambda dve, t, ps: dve.tensor_copy(gate[:, t, :], ps))
        softmax(nc, "l1f_sm", gate, ne, br)
        experts(nc, "l1f_moe", c, xt, x, gate, ne,
                [(ws[i], KD, KD, ACT.Relu, vec[:, i, 1], vec[:, i, 0]) for i in range(2)], ws[2], bo)


def l2_gnn(nc, c, a, x, tables, dinv, dram):
    f = "L2_gnn_"
    with Scope(nc, "l2g") as s:
        xt = s.sb("xt", [P, KD, NP])
        agg = s.sb("agg", [P, T, D])
        vec = s.sb("vec", [P, 3, KD])
        bias = s.sb("bias", [P, D])
        scale = s.sb("scale", [P, KD])
        shift = s.sb("shift", [P, KD])
        normal_input(nc, "l2g", c, x, xt)
        load(nc, "l2g_load", (vec[:, 0], vec_cols(a[f + "b0"])), (vec[:, 1], vec_cols(a[f + "gamma0"])),
             (vec[:, 2], vec_cols(a[f + "beta0"])), (bias[:], across(a[f + "b1"], D)))
        gat(nc, "l2g_a", c, xt, a[f + "W0"], D, a[f + "a_src0"].rearrange("h c -> (h c)"),
            a[f + "a_dst0"].rearrange("h c -> (h c)"), 4, tables[0], tables[1], T, G1, dram,
            lambda t, i: agg[:, ds(t, 1), i * 64:(i + 1) * 64].rearrange("p a d -> p (a d)"), 0.0)
        turn(nc, "l2g_t2", agg, xt, c.ident, bias=vec[:, 0])
        batchnorm_columns(nc, "l2g_bn", xt, vec[:, 1], vec[:, 2], scale, shift)
        with Scope(nc, "l2e") as q:
            low = q.sb("low", [P, KD, NP])
            with stage(nc, "l2g_elu", "step", "ready", "expd") as (block, step, ready, expd):
                @block.vector
                def _(dve):
                    for k in range(KD):
                        dve.tensor_scalar(xt[:, k, :], xt[:, k, :], scale[:, k:k + 1], shift[:, k:k + 1],
                                          ALU.mult, ALU.add).then_inc(step, 1)
                        dve.wait_ge(step, 2 * k + 1)
                        dve.tensor_scalar(low[:, k, :], xt[:, k, :], 0.0, None, ALU.min).then_inc(ready, 1)
                        dve.tensor_scalar(xt[:, k, :], xt[:, k, :], 0.0, -1.0, ALU.max, ALU.add).then_inc(step, 1)
                        dve.wait_ge(step, 2 * k + 2)
                    for k in range(KD):
                        dve.wait_ge(expd, k + 1)
                        dve.tensor_tensor(xt[:, k, :], xt[:, k, :], low[:, k, :], ALU.add)

                @block.scalar
                def _(act):
                    for k in range(KD):
                        act.wait_ge(ready, k + 1)
                        act.activation(low[:, k, :], low[:, k, :], ACT.Exp).then_inc(expd, 1)
        gat(nc, "l2g_b", c, xt, a[f + "W1"], D, a[f + "a_src1"].rearrange("h c -> (h c)"),
            a[f + "a_dst1"].rearrange("h c -> (h c)"), 1, tables[0], tables[1], T, G1, dram,
            lambda t, i: agg[:, ds(t, 1), :].rearrange("p a d -> p (a d)"), 0.0)
        finish_rows(nc, "l2g_end", x, agg, bias, False, True)


def l2_ffn(nc, c, a, x, tables, dinv, dram):
    ne, fh = 8, 1024
    cap = -(-5 * N // (4 * ne))
    room = -(-cap // P) * P
    f = "L2_ffn_"
    with Scope(nc, "l2f") as s:
        xn = s.sb("xn", [P, T, D])
        factor = s.sb("factor", [P, T])
        put = s.sb("put", [P, T], U32)
        get = s.sb("get", [P, T], U32)
        layernorm(nc, "l2f_ln", x, xn)
        with Scope(nc, "l2fr") as q:
            xt = q.sb("xt", [P, KD, NP])
            gate = q.sb("gate", [P, T, ne])
            wr = q.sb("wr", [P, KD, ne])
            br = q.sb("br", [P, ne])
            prio = q.sb("prio", [P, ne])
            base = q.sb("base", [P, ne])
            behind = q.sb("behind", [P, T])
            upto = q.sb("upto", [P, P])
            ones = q.sb("ones", [P, P])
            prob = q.sb("prob", [P, T])
            tmp = q.sb("tmp", [P, T])
            kept = q.sb("kept", [P, T])
            place = q.sb("place", [P, T])
            one = q.sb("one", [P, T, ne])
            pos = q.sb("pos", [P, T, ne])
            tot = q.sb("tot", [P, T + 1, ne])
            turn(nc, "l2f_t", xn, xt, c.ident)
            load(nc, "l2f_loadr", (wr[:], a[f + "gate_w"].rearrange("(k p) n -> p k n", p=P)),
                 (br[:], across(a[f + "gate_b"], ne)))
            product_nm(nc, "l2f_r", xt, wr, ne, lambda dve, t, ps: dve.tensor_copy(gate[:, t, :], ps))
            softmax(nc, "l2f_sm", gate, ne, br)
            pp = q.ps("pp", [P, 2, 512])
            with stage(nc, "l2f_pos", "sets", "step", "chosen", "summed") as (block, sets, step, chosen, summed):
                @block.gpsimd
                def _(pool):
                    pool.iota(prio[:], pattern=[[-1, ne]], base=ne, channel_multiplier=0,
                              allow_small_or_imprecise_dtypes=True).then_inc(sets, 1)
                    pool.iota(base[:], pattern=[[room, ne]], base=-1, channel_multiplier=0,
                              allow_small_or_imprecise_dtypes=True).then_inc(sets, 1)
                    pool.iota(behind[:], pattern=[[P, T]], base=ne * room, channel_multiplier=1,
                              allow_small_or_imprecise_dtypes=True).then_inc(sets, 1)
                    pool.memset(ones[:], 1.0).then_inc(sets, 1)
                    pool.memset(upto[:], 1.0).then_inc(sets, 1)
                    pool.wait_ge(sets, 5)
                    pool.affine_select(out=upto[:], in_=upto[:], compare_op=ALU.is_ge, fill=0.0, base=0,
                                       pattern=[[1, P]], channel_multiplier=-1).then_inc(sets, 1)

                @block.vector
                def _(dve):
                    link = Link(dve, step)
                    dve.wait_ge(sets, 6)
                    first_max(dve, link, gate, ne, prio, prob, one, tmp)
                    dve.sem_inc(chosen, 1)
                    link(dve.memset(tot[:], 0.0))
                    dve.wait_ge(summed, 1)
                    link(dve.tensor_copy(pos[:].rearrange("p t e -> p (t e)"), pp[:, 1, 0:T * ne]))
                    for t in range(1, T):
                        link(dve.tensor_tensor(tot[:, t, :], tot[:, t - 1, :], pos[:, t - 1, :], ALU.add))
                    link(dve.tensor_tensor(pos[:].rearrange("p t e -> p (t e)"), pp[:, 0, 0:T * ne],
                                           tot[:, 0:T, :].rearrange("p t e -> p (t e)"), ALU.add))
                    link(dve.tensor_tensor(pos[:], pos[:], one[:], ALU.mult))
                    link(dve.tensor_reduce(place[:], pos[:], AX, ALU.add))
                    link(dve.tensor_scalar(kept[:], place[:], cap + 0.5, None, ALU.is_lt))
                    link(dve.tensor_tensor(factor[:], prob[:], kept[:], ALU.mult))
                    link(dve.tensor_tensor(one[:], one[:], over_mid(base[:], T), ALU.mult))
                    link(dve.tensor_reduce(tmp[:], one[:], AX, ALU.add))
                    link(dve.scalar_tensor_tensor(out=place[:], in0=place[:], scalar=float(cap), in1=tmp[:],
                                                  op0=ALU.min, op1=ALU.add))
                    link(dve.tensor_copy(get[:], place[:]))
                    link(dve.tensor_tensor(place[:], place[:], behind[:], ALU.subtract))
                    link(dve.tensor_tensor(place[:], place[:], kept[:], ALU.mult))
                    link(dve.tensor_tensor(put[:], place[:], behind[:], ALU.add))

                @block.tensor
                def _(pe):
                    pe.wait_ge(chosen, 1)
                    pe.matmul(pp[:, 0, 0:T * ne], upto[:], one[:].rearrange("p t e -> p (t e)"), start=True, stop=True)
                    pe.matmul(pp[:, 1, 0:T * ne], ones[:], one[:].rearrange("p t e -> p (t e)"), start=True, stop=True
                              ).then_inc(summed, 1)
        routed_experts(nc, "l2f_moe", c, a, x, xn, put, get, factor, ne, room, fh)


def routed_experts(nc, tag, c, a, x, xn, put, get, factor, ne, room, fh):
    f = "L2_ffn_"
    rt = room // P
    mh = fh // P
    n_zero = 1024
    rows_in, rows_out = c.routed
    put_landed, get_landed = c.put_landed, c.get_landed
    with Scope(nc, tag) as s:
        w1 = s.sb("w1", [P, 2, KD, fh])
        w2 = s.sb("w2", [P, 2, mh, D])
        b1 = s.sb("b1", [P, ne, mh])
        b2 = s.sb("b2", [P, 2, D])
        rows = s.sb("rows", [P, 2, rt, D])
        cols = s.sb("cols", [P, 2, KD, room])
        hid = s.sb("hid", [P, 2, mh, room])
        res = s.sb("res", [P, 2, rt, D])
        zero = s.sb("zero", [P, n_zero])
        y = xn
        held = s.sb("held", [P, G1, D])
        flag = s.sb("flag", [P, G1, D], U8)
        pt = s.ps("pt", [P, KD, room])
        ph = s.ps("ph", [P, 4, room])
        py = s.ps("py", [P, 2, 512])
        with stage(nc, tag, "zero_set", "zeroed", "b1_in", "w_in0", "w_in1", "rows_in0", "rows_in1", "res_out0",
                   "res_out1", "turned", "cols_ready", "hid_ps", "hid_ready", "y_ps", "y_read", "put_done",
                   "stored", "scaled", "step") as (
                block, zero_set, zeroed, b1_in, w_in0, w_in1, rows_in0, rows_in1, res_out0, res_out1, turned,
                cols_ready, hid_ps, hid_ready, y_ps, y_read, put_done, stored, scaled, step):
            w_loaded, rows_loaded, res_out = [w_in0, w_in1], [rows_in0, rows_in1], [res_out0, res_out1]

            def each_expert(eng, body):
                with eng.Fori(0, ne // 2) as i:
                    for b in range(2):
                        body(b, i, 2 * i + b)

            @block.sync
            def _(sp):
                def load_weights(b, e):
                    sp.dma_start(w1[:, b], a[f + "w1"][ds(e, 1)].rearrange("o (k p) n -> p (o k) n", p=P)
                                 ).then_inc(w_loaded[b], 16)
                    sp.dma_start(w2[:, b], a[f + "w2"][ds(e, 1)].rearrange("o (k p) n -> p (o k) n", p=P)
                                 ).then_inc(w_loaded[b], 16)
                    sp.dma_start(b2[:, b], a[f + "b2"][ds(e, 1), :].to_broadcast([P, D])).then_inc(w_loaded[b], 16)

                def load_rows(b, e):
                    sp.dma_start(rows[:, b], rows_in[ds(e * room, room), :].rearrange("(t p) d -> p t d", p=P)
                                 ).then_inc(rows_loaded[b], 16)

                def store_results(b, e):
                    sp.wait_ge(y_read, e * rt + (rt + 2))
                    sp.dma_start(rows_out[ds(e * room, room), :].rearrange("(t p) d -> p t d", p=P), res[:, b]
                                 ).then_inc(res_out[b], 16)

                with nc.allow_non_contiguous_dma(reason="biases by columns"):
                    for e in range(ne):
                        sp.dma_start(b1[:, e], vec_cols(a[f + "b1"][e])).then_inc(b1_in, 16)
                for b in range(2):
                    sp.sem_inc(res_out[b], 16)
                    load_weights(b, b)
                sp.wait_ge(put_done, 1)
                for b in range(2):
                    load_rows(b, b)
                with sp.Fori(1, ne // 2) as i:
                    for b in range(2):
                        store_results(b, 2 * i + (b - 2))
                        load_weights(b, 2 * i + b)
                        load_rows(b, 2 * i + b)
                for b in range(2):
                    store_results(b, ne - 2 + b)
                for b in range(2):
                    sp.wait_ge(res_out[b], 16 * (ne // 2 + 1))
                sp.sem_inc(stored, 1)

            @block.gpsimd
            def _(pool):
                pool.memset(zero[:], 0.0).then_inc(zero_set, 1)
                n_cols = ne * room * D // P
                pool.wait_ge(zeroed, 16 * (n_cols // n_zero))
                for t in range(T):
                    pool.indirect_dma_start(rows_in, bass.IndirectOffsetOnAxis(ap=put[:, t:t + 1], axis=0),
                                            xn[:, t, :], None, bounds_check=ne * room + NP - 1, oob_is_err=True
                                            ).then_inc(put_landed, 16)
                pool.wait_ge(put_landed, 16 * T)
                pool.sem_inc(put_done, 1)
                pool.wait_ge(stored, 1)
                for t in range(T):
                    pool.indirect_dma_start(y[:, t, :], None, rows_out,
                                            bass.IndirectOffsetOnAxis(ap=get[:, t:t + 1], axis=0),
                                            bounds_check=ne * room - 1, oob_is_err=True
                                            ).then_inc(get_landed[t // G1], 16)

            @block.scalar
            def _(act):
                act.wait_ge(zero_set, 1)
                n_cols = ne * room * D // P
                for i in range(n_cols // n_zero):
                    act.dma_start(rows_in[0:ne * room, :].rearrange("(p r) d -> p (r d)", p=P)[
                        :, i * n_zero:(i + 1) * n_zero], zero[:]).then_inc(zeroed, 16)
                act.wait_ge(b1_in, 16 * ne)

                def body(b, i, e):
                    for m in range(mh):
                        act.wait_ge(hid_ps, e * mh + (m + 1))
                        act.activation(hid[:, b, m, :], ph[:, m % 4, :], ACT.Relu, bias=b1[:, ds(e, 1), m]
                                       ).then_inc(hid_ready, 1)
                each_expert(act, body)
                for g in range(T // G1):
                    act.wait_ge(get_landed[g], 16 * G1)
                    for t in range(g * G1, (g + 1) * G1):
                        act.activation(y[:, t, :], y[:, t, :], ACT.Copy, scale=factor[:, t:t + 1]).then_inc(scaled, 1)

            @block.tensor
            def _(pe):
                pe.sem_inc(hid_ready, 4)
                pe.sem_inc(cols_ready, 2)
                pe.sem_inc(y_read, 2)

                def body(b, i, e):
                    pe.wait_ge(rows_loaded[b], (i + 1) * 16)
                    pe.wait_ge(cols_ready, 2 * e + 2)
                    for k in range(KD):
                        for t in range(rt):
                            last = pe.transpose(pt[:, k, t * P:(t + 1) * P], rows[:, b, t, k * P:(k + 1) * P], c.ident[:])
                        last.then_inc(turned, 1)
                    pe.wait_ge(w_loaded[b], (i + 1) * 48)
                    pe.wait_ge(cols_ready, 2 * e + 4)
                    for m in range(mh):
                        pe.wait_ge(hid_ready, e * mh + (m + 1))
                        for k in range(KD):
                            last = pe.matmul(ph[:, m % 4, :], w1[:, b, k, m * P:(m + 1) * P], cols[:, b, k, :],
                                             start=(k == 0), stop=(k == KD - 1))
                        last.then_inc(hid_ps, 1)
                    pe.wait_ge(hid_ready, e * mh + (mh + 4))
                    for t in range(rt):
                        pe.wait_ge(y_read, e * rt + (t + 1))
                        for m in range(mh):
                            last = pe.matmul(py[:, t % 2, 0:D], hid[:, b, m, t * P:(t + 1) * P], w2[:, b, m, :],
                                             start=(m == 0), stop=(m == mh - 1))
                        last.then_inc(y_ps, 1)
                each_expert(pe, body)

            @block.vector
            def _(dve):
                def body(b, i, e):
                    for k in range(KD):
                        dve.wait_ge(turned, 2 * e + (k + 1))
                        dve.tensor_copy(cols[:, b, k, :], pt[:, k, :]).then_inc(cols_ready, 1)
                    dve.wait_ge(res_out[b], (i + 1) * 16)
                    dve.wait_ge(w_loaded[b], (i + 1) * 48)
                    for t in range(rt):
                        dve.wait_ge(y_ps, e * rt + (t + 1))
                        dve.tensor_tensor(res[:, b, t, :], py[:, t % 2, 0:D], b2[:, b, :], ALU.add).then_inc(y_read, 1)
                each_expert(dve, body)
                link = Link(dve, step)
                for g in range(T // G1):
                    dve.wait_ge(scaled, (g + 1) * G1)
                    yg = y[:, g * G1:(g + 1) * G1, :]
                    xg = x[:, g * G1:(g + 1) * G1, :]
                    link(dve.tensor_tensor(flag[:], yg, yg, ALU.not_equal))
                    link(dve.copy_predicated(yg, flag[:], over_mid(zero[:, 0:D], G1)))
                    link(dve.tensor_scalar(held[:], yg, 1e4, -1e4, ALU.min, ALU.max))
                    link(dve.tensor_scalar(flag[:], yg, 0.0, 0.0, ALU.mult, ALU.not_equal))
                    link(dve.copy_predicated(yg, flag[:], held[:]))
                    link(dve.tensor_tensor(xg, xg, yg, ALU.add))


def l3_gnn(nc, c, a, x, tables, dinv, dram):
    f = "L3_gnn_"
    with Scope(nc, "l3g") as s:
        vec = s.sb("vec", [P, 5, 3, KD])
        w = s.sb("w", [P, 6, KD, D])
        scale = s.sb("scale", [P, KD])
        shift = s.sb("shift", [P, KD])
        rows = s.sb("rows", [P, T, D])
        agg_x = s.sb("agg_x", [P, KD, NP])
        h_fm = s.sb("h_fm", [P, KD, NP])
        agg_h = s.sb("agg_h", [P, KD, NP])

        def slot(i):
            return (0, 1, 2, 4, 5)[i]
        load(nc, "l3g_load",
             *[(w[:, slot(i)], a[f + f"W{i + 1}"].rearrange("(k p) n -> p k n", p=P)) for i in (0, 1, 3, 4)],
             (w[:, 2:4].rearrange("p a k n -> p (a k) n"), a[f + "W3"].rearrange("(k p) n -> p k n", p=P)),
             *[(vec[:, i, j], vec_cols(a[f + n + str(i + 1)])) for i in range(5) for j, n in enumerate(["b", "g", "be"])])

        def lin_bn_relu(i, srcs, dst):
            wi = w[:, 2:4].rearrange("p a k n -> p (a k) n") if i == 2 else w[:, slot(i)]
            product_fm(nc, f"l3g_w{i}", srcs, wi, dst, ACT.Identity, vec[:, i, 0])
            batchnorm_columns(nc, f"l3g_bn{i}", dst, vec[:, i, 1], vec[:, i, 2], scale, shift)
            scale_relu(nc, f"l3g_relu{i}", dst, scale, shift)

        def halves(t):
            return [t[:, k] for k in range(KD)]

        with Scope(nc, "l3ga") as q:
            agg = q.sb("agg", [P, T, D])
            layernorm(nc, "l3g_ln", x, rows)
            aggregate(nc, "l3g_agg", c, tables[0], T, G1, lambda t: rows[:, ds(t, 1), :].rearrange("p a d -> p (a d)"),
                      D, lambda t: agg[:, ds(t, 1), :].rearrange("p a d -> p (a d)"))
            turn(nc, "l3g_t", agg, agg_x, c.ident)
            lin_bn_relu(0, halves(agg_x), h_fm)
            lin_bn_relu(1, halves(h_fm), agg_h)
            unturn(nc, "l3g_u", agg_h, rows, c.ident)
            aggregate(nc, "l3g_agg2", c, tables[0], T, G1, lambda t: rows[:, ds(t, 1), :].rearrange("p a d -> p (a d)"),
                      D, lambda t: agg[:, ds(t, 1), :].rearrange("p a d -> p (a d)"))
            turn(nc, "l3g_t2", agg, agg_h, c.ident)
        lin_bn_relu(2, halves(agg_x) + halves(agg_h), h_fm)
        lin_bn_relu(3, halves(h_fm), agg_x)
        lin_bn_relu(4, halves(agg_x), h_fm)
        unturn(nc, "l3g_u2", h_fm, x, c.ident, add=True)


def unturn(nc, tag, fm, nm, ident, add=False):
    with Scope(nc, tag) as s:
        pt = s.ps("pt", [P, 8, 512])
        with stage(nc, tag, "turned", "out") as (block, turned, out):
            @block.tensor
            def _(pe):
                for t in range(T):
                    if t >= 8:
                        pe.wait_ge(out, t - 7)
                    for k in range(KD):
                        last = pe.transpose(pt[:, t % 8, k * P:(k + 1) * P], fm[:, k, t * P:(t + 1) * P], ident[:])
                    last.then_inc(turned, 1)

            @block.vector
            def _(dve):
                for t in range(T):
                    dve.wait_ge(turned, t + 1)
                    if add:
                        dve.tensor_tensor(nm[:, t, :], pt[:, t % 8, 0:D], nm[:, t, :], ALU.add).then_inc(out, 1)
                    else:
                        dve.tensor_copy(nm[:, t, :], pt[:, t % 8, 0:D]).then_inc(out, 1)


def l3_ffn(nc, c, a, x, tables, dinv, dram):
    ne = 6
    f = "L3_ffn_"
    with Scope(nc, "l3f") as s:
        xt = s.sb("xt", [P, KD, NP])
        gate = s.sb("gate", [P, T, ne])
        normal_input(nc, "l3f", c, x, xt)
        with Scope(nc, "l3fr") as q:
            w1 = q.sb("w1", [P, KD, P])
            b1 = q.sb("b1", [P, 1])
            w2 = q.sb("w2", [P, 1, ne])
            br = q.sb("br", [P, ne])
            rh = q.sb("rh", [P, 1, NP])
            score = q.sb("score", [P, T, ne])
            load(nc, "l3f_loadr", (w1[:], a[f + "router_w1"].rearrange("(k p) n -> p k n", p=P)),
                 (b1[:], vec_cols(a[f + "router_b1"])), (w2[:, 0], a[f + "router_w2"]), (br[:], across(a[f + "router_b2"], ne)))
            product_fm(nc, "l3f_r1", [xt[:, k] for k in range(KD)], w1, rh, ACT.Relu, b1)
            product_nm(nc, "l3f_r2", rh, w2, ne, lambda dve, t, ps: dve.tensor_copy(score[:, t, :], ps))
            softmax(nc, "l3f_sm", score, ne, br)
            top2_gates(nc, "l3f_top", c, score, ne, gate)
        ws = [s.sb(f"w{i}", [P, ne, KD, D]) for i in range(3)]
        b = s.sb("b", [P, 2, ne, KD])
        b3 = s.sb("b3", [ne, D])
        load(nc, "l3f_load",
             *[(ws[i][:, e], a[f + f"expert_w{i + 1}"][e].rearrange("(k p) n -> p k n", p=P)) for i in range(3)
               for e in range(ne)],
             *[(b[:, i, e], vec_cols(a[f + f"expert_b{i + 1}"][e])) for i in range(2) for e in range(ne)],
             (b3[:], a[f + "expert_b3"]))
        experts(nc, "l3f_moe", c, xt, x, gate, ne, [(ws[i], KD, KD, ACT.Relu, None, b[:, i]) for i in range(2)], ws[2], b3)


PARTS = [("l0_gnn", l0_gnn), ("l0_ffn", l0_ffn), ("l1_gnn", l1_gnn), ("l1_ffn", l1_ffn), ("l2_gnn", l2_gnn),
         ("l2_ffn", l2_ffn), ("l3_gnn", l3_gnn), ("l3_ffn", l3_ffn)]
_INS = "x src dst".split() + """L0_gnn_W_gcn L0_gnn_b_gcn L0_gnn_W_V
L0_ffn_W_gat L0_ffn_att_src L0_ffn_att_dst L0_ffn_b_gat L0_ffn_ln_gamma L0_ffn_ln_beta L0_ffn_W1 L0_ffn_b1 L0_ffn_W2
L0_ffn_b2 L0_ffn_edge_index L1_gnn_W1 L1_gnn_b1 L1_gnn_W2 L1_gnn_att_src L1_gnn_att_dst L1_gnn_b2 L1_ffn_Wr L1_ffn_br
L1_ffn_W1 L1_ffn_b1 L1_ffn_g1 L1_ffn_be1 L1_ffn_m1 L1_ffn_v1 L1_ffn_W2 L1_ffn_b2 L1_ffn_g2 L1_ffn_be2 L1_ffn_m2
L1_ffn_v2 L1_ffn_Wo L1_ffn_bo L2_gnn_W0 L2_gnn_a_src0 L2_gnn_a_dst0 L2_gnn_b0 L2_gnn_gamma0 L2_gnn_beta0 L2_gnn_W1
L2_gnn_a_src1 L2_gnn_a_dst1 L2_gnn_b1 L2_ffn_gate_w L2_ffn_gate_b L2_ffn_w1 L2_ffn_b1 L2_ffn_w2 L2_ffn_b2""".split() + [
    f"L3_gnn_{v}{i}" for i in range(1, 6) for v in ("W", "b", "g", "be")] + [
    "L3_ffn_router_w1", "L3_ffn_router_b1", "L3_ffn_router_w2", "L3_ffn_router_b2"] + [
    f"L3_ffn_expert_{v}{i}" for i in range(1, 4) for v in ("w", "b")]


def kernel(**inputs):
    import concourse.bacc as bacc
    import numpy as np
    from concourse.bass_utils import run_bass_kernel_spmd

    nc = bacc.Bacc("TRN2", target_bir_lowering=False, num_devices=1)
    arrays, args = {}, {}
    for name in _INS:
        v = np.ascontiguousarray(inputs[name])
        if name in ("src", "dst"):
            v = np.concatenate([v, np.full(NCH1 * P - E1, NP - 1, v.dtype)])
        arrays["in_" + name] = v
        args[name] = nc.dram_tensor("in_" + name, v.shape, mybir.dt.from_np(v.dtype), kind="ExternalInput").ap()
    out = nc.dram_tensor("out_x", (N, D), F32, kind="ExternalOutput").ap()
    build(nc, args, out)
    r = run_bass_kernel_spmd(nc, [arrays], core_ids=[0])
    return r.results[0]["out_x"]
```

```python
from contextlib import ExitStack, contextmanager

import concourse.bass as bass
from concourse import mybir

F32 = mybir.dt.float32
I32 = mybir.dt.int32
U32 = mybir.dt.uint32
U8 = mybir.dt.uint8
BF16 = mybir.dt.bfloat16
ALU = mybir.AluOpType
ACT = mybir.ActivationFunctionType
AX = mybir.AxisListType.X
ds = bass.ds

P = 128
N = 3125
T = -(-N // P)
NP = T * P
D = 256
KD = D // P
G1 = 5
N2 = 2048
T2 = N2 // P
G2 = 4
W = 8
E1 = 53125
NCH1 = 2 * W * -(-E1 // (2 * W * P))
E2 = 32768
NCH2 = E2 // P
FAR = -1e30
SLOPE = 0.2
ROUTED = 8 * 512
SEM0 = 150


@contextmanager
def stage(nc, name, *names):
    with ExitStack() as cx:
        sems = [cx.enter_context(nc.semaphore(f"{name}_{s}", num=SEM0 + i)) for i, s in enumerate(names)]
        with nc.Block() as block:
            yield (block, *sems)
        nc.all_engine_barrier(sems_to_clear=range(SEM0, SEM0 + len(names)))


class Link:

    def __init__(self, eng, sem):
        self.eng, self.sem, self.n = eng, sem, 0

    def __call__(self, ins):
        self.n += 1
        ins.then_inc(self.sem, 1)
        self.eng.wait_ge(self.sem, self.n)


class Scope:

    def __init__(self, nc, tag):
        self.nc, self.tag, self.cx = nc, tag, ExitStack()

    def __enter__(self):
        return self

    def __exit__(self, *a):
        return self.cx.__exit__(*a)

    def sb(self, name, shape, dt=F32):
        return self.cx.enter_context(self.nc.sbuf_tensor(f"{self.tag}_{name}", shape, dt))

    def ps(self, name, shape, dt=F32):
        return self.cx.enter_context(self.nc.psum_tensor(f"{self.tag}_{name}", shape, dt))


def across(vec, n):
    return vec.rearrange("(o n) -> o n", o=1).to_broadcast([P, n])


def over_last(ap, n):
    a, t = ap.shape
    return ap.rearrange("p (t o) -> p t o", o=1).to_broadcast([a, t, n])


def over_mid(ap, t):
    a, n = ap.shape
    return ap.rearrange("p (o n) -> p o n", o=1).to_broadcast([a, t, n])



def count_edges(nc, graphs, ids, key_rows, set_later, table_set, ident, cells, counts, adder):
    n_win = [nch // W for nch, _ in graphs]
    n_all = graphs[0][0] + graphs[1][0]
    first = [0, graphs[0][0]]
    span = (W + 1) * P
    blocks = [(at, min(P, n_all - at)) for at in range(0, n_all, P)]
    with Scope(nc, "count") as s:
        key = s.sb("key", [P, n_all])
        apart = s.sb("apart", [P, n_all])
        key_turned = s.sb("key_turned", [P, len(blocks), P])
        keys = s.sb("keys", [P, 2, W * P])
        same = s.sb("same", [P, 2, W, span], BF16)
        same_own = s.sb("same_own", [P, 2, W, P], BF16)
        below = s.sb("below", [P, P], BF16)
        picks = s.sb("picks", [P, 4], BF16)
        sign = s.sb("sign", [P, 2, W])
        sums = s.ps("sums", [P, 2, 512])
        turned = s.ps("turned", [P, len(blocks), 512])
        with stage(nc, "count", "consts", "keyed", "keys_turned",
                   "turned_out", "keys_out", "keys_in0", "keys_in1", "compared", "own_ready", "counted",
                   "sums_read", "cells_ready", "copied", "begun", "clear") as (
                block, consts, keyed, keys_turned,
                turned_out, keys_out, keys_in0, keys_in1, compared, own_ready, counted,
                sums_read, cells_ready, copied, begun, clear):
            keys_in = [keys_in0, keys_in1]

            def windows(eng, body, between=None):
                for g, shift in ((0, 0), (1, n_win[0])):
                    if g and between is not None:
                        between(eng)
                    with eng.Fori(shift // 2, (shift + n_win[g]) // 2) as i:
                        for b in range(2):
                            body(b, g, 2 * i + (b - shift), 2 * i + b, i)

            @block.sync
            def _(sp):
                sp.wait_ge(turned_out, len(blocks))
                for i, (at, m) in enumerate(blocks):
                    sp.dma_start(key_rows[at * P:(at + m) * P].rearrange("(c p) -> c p", p=P), key_turned[0:m, i, :]
                                 ).then_inc(keys_out, 16)
                sp.wait_ge(keys_out, 16 * len(blocks))

                def body(b, g, w, n, i):
                    sp.wait_ge(compared, n * W + W)
                    sp.dma_start(keys[:, b, :], key_rows.rearrange("(o n) -> o n", o=1)[
                        :, ds(w * (W * P) + first[g] * P, W * P)].to_broadcast([P, W * P])).then_inc(keys_in[b], 16)
                windows(sp, body)

            @block.vector
            def _(dve):
                for g, (nch, n_pad) in enumerate(graphs):
                    own = slice(first[g], first[g] + nch)
                    dve.scalar_tensor_tensor(out=key[:, own], in0=ids[:, 0, own], scalar=float(n_pad),
                                             in1=ids[:, 1, own], op0=ALU.mult, op1=ALU.add).then_inc(keyed, 1)
                for i, (at, m) in enumerate(blocks):
                    dve.wait_ge(keys_turned, i + 1)
                    dve.tensor_copy(key_turned[0:m, i, :], turned[0:m, i, 0:P]).then_inc(turned_out, 1)
                dve.wait_ge(consts, 7)
                dve.wait_ge(keyed, 2)
                dve.tensor_tensor(apart[:], apart[:], key[:], ALU.subtract).then_inc(keyed, 2)
                dve.sem_inc(compared, 2 * W)
                dve.sem_inc(counted, 2)

                def body(b, g, w, n, i):
                    dve.wait_ge(keys_in[b], (i + 1) * 16)
                    dve.wait_ge(counted, n + 1)
                    for j in range(W):
                        dve.tensor_scalar(same[:, b].rearrange("p j s -> p (j s)")[:, j * W * P:(j + 1) * W * P],
                                          keys[:, b, :], key[:, ds(w * W + (first[g] + j), 1)], None, ALU.is_equal
                                          ).then_inc(compared, 1)
                    dve.wait_ge(compared, n * W + 3 * W)
                    dve.tensor_tensor(same_own[:, b], same[:, b, :, 0:P], over_mid(below[:], W), ALU.mult
                                      ).then_inc(own_ready, 1)
                windows(dve, body)

            @block.tensor
            def _(pe):
                pe.wait_ge(keyed, 2)
                for i, (at, m) in enumerate(blocks):
                    pe.transpose(turned[0:m, i, 0:P], key[:, at:at + m], ident[:]).then_inc(keys_turned, 1)
                pe.wait_ge(consts, 7)
                pe.sem_inc(sums_read, 4)

                def body(b, g, w, n, i):
                    pe.wait_ge(own_ready, n + 1)
                    pe.wait_ge(sums_read, 2 * n + 2)
                    flat = same[:, b].rearrange("p j s -> p (j s)")
                    for k in range(W):
                        for j in range(W):
                            at = (j * W + k) * P
                            pe.matmul(sums[:, b, 2 * k:2 * k + 2], flat[:, at:at + P],
                                      picks[:, 0:2] if j < k else picks[:, 1:3], start=(j == 0), stop=False)
                        last = pe.matmul(sums[:, b, 2 * k:2 * k + 2], same_own[:, b, k, :], picks[:, 2:4],
                                         start=False, stop=True)
                    last.then_inc(counted, 1)
                windows(pe, body)

            @block.scalar
            def _(act):
                act.wait_ge(keyed, 4)

                def body(b, g, w, n, i):
                    act.wait_ge(counted, n + 3)
                    both_sums = sums[:, b, 0:2 * W].rearrange("p (k a) -> p k a", a=2)
                    act.activation(sign[:, b, :], both_sums[:, :, 1], ACT.Sign).then_inc(sums_read, 1)
                    act.activation(counts[g][:, ds(w * W, W)], both_sums[:, :, 0], ACT.Copy).then_inc(sums_read, 1)
                    act.wait_ge(sums_read, 2 * n + 6)
                    for j in range(W):
                        at = w * W + (first[g] + j)
                        last = act.activation(cells[g][:, ds(w * W + j, 1)], sign[:, b, j:j + 1], ACT.Identity,
                                              scale=apart[:, ds(at, 1)], bias=key[:, ds(at, 1)])
                        last.then_inc(cells_ready, 1)
                windows(act, body, set_later)

            @block.gpsimd
            def _(pool):
                pool.memset(below[:], 1.0).then_inc(clear, 1)
                pool.memset(picks[:], 1.0).then_inc(clear, 1)
                pool.wait_ge(clear, 2)
                pool.memset(picks[:, 2:3], 0.0).then_inc(consts, 1)
                pool.affine_select(out=below[:], in_=below[:], compare_op=ALU.is_gt, fill=0.0, base=0,
                                   pattern=[[1, P]], channel_multiplier=-1).then_inc(consts, 1)
                for g, (nch, n_pad) in enumerate(graphs):
                    pool.iota(apart[:, first[g]:first[g] + nch], pattern=[[0, nch // W], [P, W]], base=n_pad * n_pad,
                              channel_multiplier=1, allow_small_or_imprecise_dtypes=True).then_inc(consts, 1)
                pool.wait_ge(consts, 4)
                pool.sem_inc(consts, 3)
                pool.wait_ge(table_set[0], 16 * (graphs[0][1] // P))
                adder[0].run(pool, 0, n_win[0], copied, begun, ready=lambda w: pool.wait_ge(cells_ready, w * W + W))


class Adder:

    def __init__(self, table, n_pad, cells, counts, cell, count, landed):
        self.table, self.n_pad, self.cells, self.counts = table, n_pad, cells, counts
        self.cell, self.count, self.landed = cell, count, landed

    def run(self, pool, start, end, copied, begun, ready=None):
        def window(b, w, after):
            if ready is not None:
                ready(w)
            pool.sem_inc(begun, 1)
            pool.tensor_copy(self.cell[:, b, :], self.cells[:, ds(w * W, W)]).then_inc(copied, 1)
            pool.tensor_copy(self.count[:, b, :], self.counts[:, ds(w * W, W)]).then_inc(copied, 1)
            pool.wait_ge(copied, 2 * (w - start) + 2)
            if after:
                pool.wait_ge(self.landed, w * (16 * W))
            pool.sem_inc(begun, 1)
            for j in range(W):
                pool.indirect_dma_start(
                    self.table, bass.IndirectOffsetOnAxis(ap=self.cell[:, b, j:j + 1], axis=0),
                    self.count[:, b, j:j + 1], None, compute_op=ALU.add,
                    bounds_check=self.n_pad * self.n_pad + W * P - 1, oob_is_err=True).then_inc(self.landed, 16)

        for b in range(2):
            window(b, start + b, start + b > 0)
        with pool.Fori(start // 2 + 1, end // 2) as i:
            for b in range(2):
                window(b, 2 * i + b, True)
        pool.wait_ge(self.landed, end * (16 * W))


def mask_and_degrees(nc, tag, table, nt, gt, far, ident, degree, beside=None):
    n_pad = nt * P
    ngr = -(-nt // 4)
    table2 = table[0:n_pad * n_pad, 0].rearrange("(r n) -> r n", n=n_pad)
    with Scope(nc, tag) as s:
        panel = s.sb("panel", [P, gt, nt, P])
        turned = s.sb("turned", [P, ngr, 4 * P])
        mask = s.sb("mask", [P, gt, n_pad], BF16)
        part = s.sb("part", [P, nt, ngr])
        pt = s.ps("pt", [P, ngr, 4 * P])
        with stage(nc, tag, *[f"panel_in{u}" for u in range(gt)], *[f"mask_out{u}" for u in range(gt)],
                   "panel_free", "turned_ps", "copied", "masked", "summed", "cells_copied", "begun") as (block, *sems):
            panel_in, mask_out = sems[:gt], sems[gt:2 * gt]
            panel_free, turned_ps, copied, masked, summed, cells_copied, begun = sems[2 * gt:]

            if beside is not None:
                @block.gpsimd
                def _(pool):
                    adder, start, end = beside
                    adder.run(pool, start, end, cells_copied, begun)

            @block.sync
            def _(sp):
                def load_panel(k, u):
                    sp.wait_ge(panel_free, k * gt + u + 1)
                    sp.dma_start(panel[:, u], table2[:, ds((k * gt + u) * P, P)].rearrange("(t p) d -> p t d", p=P)
                                 ).then_inc(panel_in[u], 16)

                def store_mask(k, u):
                    sp.wait_ge(masked, (k * gt + u + 2) * ngr)
                    sp.dma_start(far[ds((k * gt + u) * P, P), :], mask[:, u, :]).then_inc(mask_out[u], 16)

                for u in range(gt):
                    sp.sem_inc(mask_out[u], 16)
                    load_panel(0, u)
                with sp.Fori(1, nt // gt) as k:
                    for u in range(gt):
                        load_panel(k, u)
                        store_mask(k - 1, u)
                for u in range(gt):
                    store_mask(nt // gt - 1, u)
                for u in range(gt):
                    sp.wait_ge(mask_out[u], (nt // gt + 1) * 16)

            @block.tensor
            def _(pe):
                pe.sem_inc(panel_free, gt)
                with pe.Fori(0, nt // gt) as k:
                    for u in range(gt):
                        j = k * gt + u
                        pe.wait_ge(panel_in[u], (k + 1) * 16)
                        for q in range(ngr):
                            pe.wait_ge(copied, j * ngr + q + 1)
                            for t in range(4 * q, min(4 * q + 4, nt)):
                                last = pe.transpose(pt[:, q, (t - 4 * q) * P:(t - 4 * q + 1) * P], panel[:, u, t, :],
                                                    ident[:])
                            last.then_inc(turned_ps, 1)
                        pe.wait_ge(turned_ps, j * ngr + ngr)
                        pe.sem_inc(panel_free, 1)

            @block.scalar
            def _(act):
                act.sem_inc(copied, ngr)
                act.sem_inc(masked, ngr)
                with act.Fori(0, nt // gt) as k:
                    for u in range(gt):
                        j = k * gt + u
                        for q in range(ngr):
                            n = (min(4 * q + 4, nt) - 4 * q) * P
                            act.wait_ge(turned_ps, j * ngr + q + 1)
                            act.wait_ge(masked, j * ngr + q + 1)
                            act.activation(turned[:, q, 0:n], pt[:, q, 0:n], ACT.Copy,
                                           accum_out=part[:, ds(j, 1), q]).then_inc(copied, 1)

            @block.vector
            def _(dve):
                with dve.Fori(0, nt // gt) as k:
                    for u in range(gt):
                        j = k * gt + u
                        dve.wait_ge(mask_out[u], (k + 1) * 16)
                        for q in range(ngr):
                            n = (min(4 * q + 4, nt) - 4 * q) * P
                            dve.wait_ge(copied, j * ngr + q + 1 + ngr)
                            dve.tensor_scalar(mask[:, u, 4 * q * P:4 * q * P + n], turned[:, q, 0:n], 0.5, FAR,
                                              ALU.is_lt, ALU.mult).then_inc(masked, 1)
                dve.wait_ge(copied, (nt + 1) * ngr)
                if degree is not None:
                    dve.tensor_reduce(degree[:, 0:nt], part[:], AX, ALU.add).then_inc(summed, 1)



def layernorm(nc, tag, c, x, xn, fm=None, unit=False, ahead=()):
    with Scope(nc, tag) as s:
        stats = s.sb("stats", [P, T, 6])
        mv = s.sb("mv", [P, T, 2])
        rstd = s.sb("rstd", [P, T])
        size = s.sb("size", [P, T])
        pt = s.ps("pt", [P, 4, KD, 2 * P])
        with stage(nc, tag, "stat", "agg", "eps", "root", "step", "done", "turned", "out") as (
                block, stat, agg, eps, root, step, done, turned, out):
            if ahead:
                @block.sync
                def _(sp):
                    with nc.allow_non_contiguous_dma(reason="short vectors by columns"):
                        for i, pairs in enumerate(ahead):
                            for dst, src in pairs:
                                sp.dma_start(dst, src).then_inc(c.loaded[i], 16)
                                c.n_loaded[i] += 16

            @block.vector
            def _(dve):
                link = Link(dve, step)
                for t in range(T):
                    dve.bn_stats(stats[:, t, :], x[:, t, :]).then_inc(stat, 1)
                for t in range(T):
                    dve.wait_ge(stat, t + 1)
                    dve.bn_aggr(mv[:, t, :], stats[:, t, :]).then_inc(agg, 1)
                dve.wait_ge(agg, T)
                if unit:
                    dve.tensor_scalar(size[:], mv[:, :, 1], float(D), None, ALU.mult).then_inc(eps, 1)
                dve.tensor_scalar(rstd[:], mv[:, :, 1], 1e-5, None, ALU.add).then_inc(eps, 1)
                dve.wait_ge(root, 2 if unit else 1)
                link(dve.reciprocal(rstd[:], rstd[:]))
                if unit:
                    link(dve.tensor_tensor(size[:], size[:], rstd[:], ALU.mult))
                    link(dve.tensor_scalar(size[:], size[:], 1e-12, None, ALU.max))
                    link(dve.reciprocal(size[:], size[:]))
                    link(dve.tensor_tensor(rstd[:], rstd[:], size[:], ALU.mult))
                for t in range(T):
                    dve.tensor_scalar(xn[:, t, :], x[:, t, :], mv[:, t, 0:1], rstd[:, t:t + 1],
                                      ALU.subtract, ALU.mult).then_inc(done, 1)

            @block.scalar
            def _(act):
                if unit:
                    act.wait_ge(eps, 1)
                    act.activation(size[:], size[:], ACT.Sqrt).then_inc(root, 1)
                act.wait_ge(eps, 2 if unit else 1)
                act.activation(rstd[:], rstd[:], ACT.Sqrt).then_inc(root, 1)
                if fm is not None:
                    copy_turned(act, pt, fm, turned, out)

            if fm is not None:
                @block.tensor
                def _(pe):
                    turn_tiles(pe, xn, pt, c.ident, turned, out, done)


def turn_tiles(pe, nm, pt, ident, turned, out, written=None):
    for i, t in enumerate(range(0, T, 2)):
        n = min(2, T - t)
        if written is not None:
            pe.wait_ge(written, t + n)
        if i >= 4:
            pe.wait_ge(out, i - 3)
        for j in range(n):
            for k in range(KD):
                last = pe.transpose(pt[:, i % 4, k, j * P:(j + 1) * P], nm[:, t + j, k * P:(k + 1) * P], ident[:])
        last.then_inc(turned, 1)


def copy_turned(act, pt, fm, turned, out, bias=None, func=ACT.Identity):
    for i, t in enumerate(range(0, T, 2)):
        n = min(2, T - t)
        act.wait_ge(turned, i + 1)
        if bias is None:
            last = act.activation(fm[:, :, t * P:(t + n) * P], pt[:, i % 4, :, 0:n * P], func)
        else:
            for k in range(KD):
                last = act.activation(fm[:, k, t * P:(t + n) * P], pt[:, i % 4, k, 0:n * P], func,
                                      bias=bias[:, k:k + 1])
        last.then_inc(out, 1)


def turn(nc, tag, nm, fm, ident, bias=None, func=ACT.Identity):
    with Scope(nc, tag) as s:
        pt = s.ps("pt", [P, 4, KD, 2 * P])
        with stage(nc, tag, "turned", "out") as (block, turned, out):
            @block.tensor
            def _(pe):
                turn_tiles(pe, nm, pt, ident, turned, out)

            @block.scalar
            def _(act):
                copy_turned(act, pt, fm, turned, out, bias, func)


def product_nm(nc, tag, fm, w, width, store):
    kk = w.shape[1]
    with Scope(nc, tag) as s:
        acc = s.ps("acc", [P, 8, 512])
        with stage(nc, tag, "done", "stored") as (block, done, stored):
            @block.tensor
            def _(pe):
                for t in range(T):
                    if t >= 8:
                        pe.wait_ge(stored, t - 7)
                    for k in range(kk):
                        last = pe.matmul(acc[:, t % 8, 0:width], fm[:, k, t * P:(t + 1) * P], w[:, k, :],
                                         start=(k == 0), stop=(k == kk - 1))
                    last.then_inc(done, 1)

            @block.vector
            def _(dve):
                for t in range(T):
                    dve.wait_ge(done, t + 1)
                    store(dve, t, acc[:, t % 8, 0:width]).then_inc(stored, 1)


def product_fm(nc, tag, srcs, w, dst, func, bias, stats=None):
    kk, m_all = w.shape[1], w.shape[2]
    mm = m_all // P
    n = 400
    with Scope(nc, tag) as s:
        acc = s.ps("acc", [P, 2, mm, 512])
        with stage(nc, tag, "done", "stored") as (block, done, stored):
            @block.tensor
            def _(pe):
                pe.sem_inc(stored, 2 * mm)
                with pe.Fori(0, NP // n // 2) as i:
                    for b in range(2):
                        for m in range(mm):
                            pe.wait_ge(stored, (2 * i + b) * mm + m + 1)
                            for k in range(kk):
                                last = pe.matmul(acc[:, b, m, 0:n], w[:, k, m * P:(m + 1) * P],
                                                 srcs[k][:, ds((2 * i + b) * n, n)], start=(k == 0), stop=(k == kk - 1))
                            last.then_inc(done, 1)

            @block.scalar
            def _(act):
                with act.Fori(0, NP // n // 2) as i:
                    for b in range(2):
                        for m in range(mm):
                            act.wait_ge(done, (2 * i + b) * mm + m + 1)
                            act.activation(dst[:, m, ds((2 * i + b) * n, n)], acc[:, b, m, 0:n], func,
                                           bias=bias[:, m:m + 1]).then_inc(stored, 1)

            if stats is not None:
                @block.vector
                def _(dve):
                    for j in range(NP // n):
                        for m in range(mm):
                            dve.wait_ge(stored, (j + 2) * mm + m + 1)
                            dve.bn_stats(stats[:, m, j, :], dst[:, m, j * n:min((j + 1) * n, N)])


def settle(nc, tag, c, i):
    with stage(nc, tag) as (block,):
        @block.sync
        def _(sp):
            sp.wait_ge(c.loaded[i], c.n_loaded[i])


def load(nc, tag, *pairs):
    with stage(nc, tag, "loaded") as (block, loaded):
        @block.sync
        def _(sp):
            with nc.allow_non_contiguous_dma(reason="short vectors by columns"):
                for dst, src in pairs:
                    sp.dma_start(dst, src).then_inc(loaded, 16)
            sp.wait_ge(loaded, 16 * len(pairs))


def columns_out(nc, tag, cols, n, ident, dram):
    parts = [(at, min(P, n - at)) for at in range(0, n, P)]
    with Scope(nc, tag) as s:
        pt = s.ps("pt", [P, len(parts), 512])
        flat = s.sb("flat", [P, len(parts), P])
        with stage(nc, tag, "turned", "copied", "moved") as (block, turned, copied, moved):
            @block.tensor
            def _(pe):
                for i, (at, m) in enumerate(parts):
                    pe.transpose(pt[0:m, i, 0:P], cols[:, at:at + m], ident[:]).then_inc(turned, 1)

            @block.vector
            def _(dve):
                for i, (at, m) in enumerate(parts):
                    dve.wait_ge(turned, i + 1)
                    dve.tensor_copy(flat[0:m, i, :], pt[0:m, i, 0:P]).then_inc(copied, 1)

            @block.sync
            def _(sp):
                for i, (at, m) in enumerate(parts):
                    sp.wait_ge(copied, i + 1)
                    sp.dma_start(dram[at * P:(at + m) * P].rearrange("(q p) -> q p", p=P), flat[0:m, i, :]
                                 ).then_inc(moved, 16)
                sp.wait_ge(moved, 16 * len(parts))



def aggregate(nc, tag, c, table, nt, gt, rhs, width, out, scale=None, attention=None, heads=1, eps=0.0,
              bias=None, beside=None):
    n_pad = nt * P
    ng = nt // gt
    cols = gt * P
    table2 = table[0:n_pad * n_pad, 0].rearrange("(r n) -> r n", n=n_pad)
    with Scope(nc, tag) as s:
        counts = s.sb("counts", [P, gt, cols])
        narrow = width <= P
        acc = s.ps("acc", [P, 4 if narrow else gt, 512])
        if narrow:
            half = cols // 2
            flat = s.sb("flat", [width, cols])
            back = s.ps("back", [P, gt, width])
        if attention:
            row_dram, es, es2 = attention
            rows = s.sb("rows", [P, min(heads, 2), 2, n_pad])
            p = s.sb("p", [P, gt, cols])
            total = s.sb("total", [P, gt])
            warm = s.sb("warm", [P, 1])
        with stage(nc, tag, *[f"counts_in{u}" for u in range(gt)], "counts_free", "sums_ready", "sums_free",
                   "low_ready", "score_ready", "exp_ready", "clamped", "weighted_dve", "weighted_pool", "step",
                   "flat_ready", "back_ready", "begun", "begun_pe", "rows_in0", "rows_in1") as (
                block, *sems):
            counts_in = sems[:gt]
            (counts_free, sums_ready, sums_free, low_ready, score_ready, exp_ready, clamped, weighted_dve,
             weighted_pool, step, flat_ready, back_ready,
             begun, begun_pe, rows_in0, rows_in1) = sems[gt:]
            rows_in = [rows_in0, rows_in1]
            weighted = [weighted_dve, weighted_pool]
            pool_slots = sorted(range(gt - 1, 2, -4)) if narrow else (0, 3)

            def by_pool(u):
                return u in pool_slots

            def nth(u, round_):
                mine = [v for v in range(gt) if by_pool(v) == by_pool(u)]
                return round_ * len(mine) + mine.index(u)

            def num(i, g):
                return g + i * ng

            @block.sync
            def _(sp):
                def load_rows(i):
                    if i > 1:
                        sp.wait_ge(score_ready, (i - 1) * (ng * ng * gt))
                    n = 2 * n_pad
                    sp.dma_start(rows[:, i % 2].rearrange("p a n -> p (a n)"), across(row_dram[i * n:(i + 1) * n], n)
                                 ).then_inc(rows_in[i % 2], 16)

                if attention:
                    load_rows(0)
                for i in range(heads):
                    with sp.Fori(0, ng) as g:
                        with sp.Fori(0, ng) as k:
                            for u in range(gt):
                                sp.wait_ge(counts_free, (num(i, g) * ng + k) * gt + u + 1)
                                sp.dma_start(counts[:, u, :], table2[ds((k * gt + u) * P, P), ds(g * cols, cols)]
                                             ).then_inc(counts_in[u], 16)
                    if i == 0 and heads > 1:
                        load_rows(1)
                    if i + 2 < heads:
                        load_rows(i + 2)

            def groups(eng, body):
                for i in range(heads):
                    body(eng, i, 0, num(i, 0) % 2, (i - 1, ng - 1) if i else None)
                    if ng > 2:
                        with eng.Fori(0, (ng - 1) // 2) as q:
                            body(eng, i, 2 * q + 1, num(i, 1) % 2, (i, 2 * q))
                            body(eng, i, 2 * q + 2, num(i, 2) % 2, (i, 2 * q + 1))
                    if ng % 2 == 0:
                        body(eng, i, ng - 1, num(i, ng - 1) % 2, (i, ng - 2))

            def wait_rows(eng, i):
                eng.wait_ge(rows_in[i % 2], 16 * (i // 2 + 1))

            def narrow_back(pe, i, g):
                pe.wait_ge(flat_ready, num(i, g) + 1)
                pe.wait_ge(sums_free, num(i, g) + 1)
                pe.sem_inc(begun_pe, 1)
                for j in range(gt):
                    last = pe.transpose(back[:, j, :], flat[:, j * P:(j + 1) * P], c.ident[0:width, 0:width])
                last.then_inc(back_ready, 1)

            def narrow_group(pe, i, g, b, prev):
                for t in range(nt):
                    u = t % gt
                    if t == gt and prev:
                        narrow_back(pe, *prev)
                    pe.wait_ge(weighted[by_pool(u)], nth(u, num(i, g) * ng + t // gt + 1) + 1)
                    for j in range(2):
                        last = pe.matmul(acc[0:width, 2 * b + j, 0:half], rhs(t, i), counts[:, u, j * half:(j + 1) * half],
                                         start=(t == 0), stop=(t == nt - 1), skip_group_check=True)
                    last.then_inc(counts_free, 1)
                pe.wait_ge(counts_free, num(i, g) * nt + (nt + gt))
                pe.sem_inc(sums_ready, 1)

            def wide_group(pe, g):
                for j in range(gt):
                    pe.wait_ge(sums_free, g * gt + (j + 1))
                    pe.matmul(acc[:, j, 0:width], c.zero[0:1, 0:P], c.zero[0:1, 0:width], start=True, stop=False,
                              skip_group_check=True)
                with pe.Fori(0, ng) as k:
                    for u in range(gt):
                        if attention:
                            pe.wait_ge(weighted[by_pool(u)], nth(u, g * ng + k + 1) + 1)
                        else:
                            pe.wait_ge(counts_in[u], (g * ng + k + 1) * 16)
                        for j in range(gt):
                            last = pe.matmul(acc[:, j, 0:width], counts[:, u, j * P:(j + 1) * P],
                                             rhs(k * gt + u, 0), start=False, stop=False, skip_group_check=True)
                        last.then_inc(counts_free, 1)
                for j in range(gt):
                    last = pe.matmul(acc[:, j, 0:width], c.zero[0:1, 0:P], c.zero[0:1, 0:width], start=False,
                                     stop=True, skip_group_check=True)
                last.then_inc(sums_ready, 1)

            @block.tensor
            def _(pe):
                pe.sem_inc(counts_free, gt)
                pe.sem_inc(sums_free, 1 if narrow else gt)
                if attention:
                    pe.sem_inc(weighted_pool, len(pool_slots))
                    pe.sem_inc(weighted_dve, gt - len(pool_slots))
                if narrow:
                    groups(pe, narrow_group)
                    narrow_back(pe, heads - 1, ng - 1)
                else:
                    with pe.Fori(0, ng) as g:
                        wide_group(pe, g)

            if beside is not None:
                @block.gpsimd
                def _(pool):
                    adder, start, end = beside
                    adder.run(pool, start, end, step, begun)

            if attention:
                @block.gpsimd
                def _(pool):
                    with pool.Fori(0, heads * ng) as n:
                        with pool.Fori(0, ng) as k:
                            for u in pool_slots:
                                pool.wait_ge(exp_ready, (n * ng + k) * gt + u + 1)
                                pool.sem_inc(begun, 1)
                                pool.tensor_scalar(p[:, u, :], p[:, u, :], 1.0, None, ALU.min).then_inc(clamped, 1)
                                pool.wait_ge(counts_in[u], (n * ng + k + 1) * 16)
                                pool.wait_ge(clamped, nth(u, n * ng + k) + 1)
                                pool.tensor_tensor(counts[:, u, :], p[:, u, :], counts[:, u, :], ALU.mult
                                                   ).then_inc(weighted_pool, 1)

                @block.scalar
                def _(act):
                    act.activation(warm[:], c.ident[:, 0:1], ACT.Exp)
                    for i in range(heads):
                        wait_rows(act, i)
                        with act.Fori(0, ng) as g:
                            with act.Fori(0, ng) as k:
                                turn_no = num(i, g) * ng + k
                                for u in range(gt):
                                    act.wait_ge(weighted[by_pool(u)], nth(u, turn_no) + 1)
                                    act.activation(p[:, u, :], rows[:, i % 2, 1, ds(g * cols, cols)], ACT.Identity,
                                                   bias=es2[:, i, ds(k * gt + u, 1)]).then_inc(low_ready, 1)
                                for u in range(gt):
                                    act.wait_ge(score_ready, turn_no * gt + u + 1)
                                    act.activation(p[:, u, :], p[:, u, :], ACT.Exp).then_inc(exp_ready, 1)

            def scores(dve, i, g, k):
                for u in range(gt):
                    dve.wait_ge(low_ready, (num(i, g) * ng + k) * gt + (u + 1))
                    dve.scalar_tensor_tensor(out=p[:, u, :], in0=rows[:, i % 2, 0, ds(g * cols, cols)],
                                             scalar=es[:, i, ds(k * gt + u, 1)], in1=p[:, u, :],
                                             op0=ALU.add, op1=ALU.max).then_inc(score_ready, 1)

            def weights(dve, i, g, k, slots):
                for u in slots:
                    if by_pool(u):
                        continue
                    dve.wait_ge(exp_ready, (num(i, g) * ng + k) * gt + (u + 1))
                    dve.wait_ge(counts_in[u], (num(i, g) * ng + k + 1) * 16)
                    dve.scalar_tensor_tensor(out=counts[:, u, :], in0=p[:, u, :], scalar=1.0, in1=counts[:, u, :],
                                             op0=ALU.min, op1=ALU.mult).then_inc(weighted_dve, 1)

            def flatten(dve, i, g, b):
                dve.wait_ge(sums_ready, num(i, g) + 1)
                dve.wait_ge(back_ready, num(i, g) + 1)
                dve.tensor_copy(flat[:].rearrange("w (j n) -> w j n", j=2), acc[0:width, 2 * b:2 * b + 2, 0:half]
                                ).then_inc(flat_ready, 1)

            def finish(dve, i, g):
                n = num(i, g)
                dve.wait_ge(*((back_ready, n + 2) if narrow else (sums_ready, n + 1)))
                sums = back if narrow else acc
                f = width - 1
                dve.tensor_scalar(total[:], sums[:, :, f], eps, None, ALU.add).then_inc(step, 1)
                dve.wait_ge(step, 2 * n + 1)
                dve.reciprocal(total[:], total[:]).then_inc(step, 1)
                dve.wait_ge(step, 2 * n + 2)
                for j in range(gt):
                    if bias is None:
                        last = dve.tensor_scalar(out(g * gt + j, i), sums[:, j, 0:f], total[:, j:j + 1], None, ALU.mult)
                    else:
                        last = dve.scalar_tensor_tensor(out=out(g * gt + j, i), in0=sums[:, j, 0:f],
                                                        scalar=total[:, j:j + 1], in1=bias[:], op0=ALU.mult,
                                                        op1=ALU.add)
                    if not narrow:
                        last.then_inc(sums_free, 1)
                if narrow:
                    last.then_inc(sums_free, 1)

            def narrow_rounds(dve, i, g, b, prev):
                if not (prev and prev[0] == i):
                    wait_rows(dve, i)
                scores(dve, i, g, 0)
                weights(dve, i, g, 0, range(gt))
                if prev:
                    flatten(dve, *prev, 1 - b)
                scores(dve, i, g, 1)
                weights(dve, i, g, 1, range(gt))
                if prev:
                    finish(dve, *prev)
                if ng > 2:
                    with dve.Fori(2, ng) as k:
                        scores(dve, i, g, k)
                        weights(dve, i, g, k, range(gt))

            def wide_rounds(dve, i, g, b, prev):
                if not (prev and prev[0] == i):
                    wait_rows(dve, i)
                scores(dve, i, g, 0)
                weights(dve, i, g, 0, range(gt - 1))
                if prev:
                    finish(dve, *prev)
                weights(dve, i, g, 0, range(gt - 1, gt))
                with dve.Fori(1, ng) as k:
                    scores(dve, i, g, k)
                    weights(dve, i, g, k, range(gt))

            @block.vector
            def _(dve):
                if narrow:
                    dve.sem_inc(back_ready, 1)
                    groups(dve, narrow_rounds)
                    flatten(dve, heads - 1, ng - 1, num(heads - 1, ng - 1) % 2)
                    finish(dve, heads - 1, ng - 1)
                elif attention:
                    groups(dve, wide_rounds)
                    finish(dve, 0, ng - 1)
                else:
                    with dve.Fori(0, ng) as g:
                        dve.wait_ge(sums_ready, g + 1)
                        for j in range(gt):
                            if scale is None:
                                ins = dve.tensor_copy(out(g * gt + j, 0), acc[:, j, 0:width])
                            else:
                                ins = dve.tensor_scalar(out(g * gt + j, 0), acc[:, j, 0:width],
                                                        scale[:, ds(g * gt + j, 1)], None, ALU.mult)
                            ins.then_inc(sums_free, 1)


def neighbour_max(nc, tag, far, nt, gt, heads, es_dram, smax):
    n_pad = nt * P
    with Scope(nc, tag) as s:
        es_rows = s.sb("es_rows", [P, heads, n_pad])
        mask = s.sb("mask", [P, gt, n_pad], BF16)
        junk = s.sb("junk", [P, 2, n_pad], BF16)
        with stage(nc, tag, *[f"mask_in{u}" for u in range(gt)], *[f"es_in{h}" for h in range(heads)],
                   "seen") as (block, *sems):
            mask_in, es_in, seen = sems[:gt], sems[gt:gt + heads], sems[gt + heads]

            @block.sync
            def _(sp):
                for t in range(nt):
                    if t >= gt:
                        sp.wait_ge(seen, (t - gt + 1) * heads if t - gt >= gt else gt * (heads - 1) + t - gt + 1
                                   )
                    sp.dma_start(mask[:, t % gt, :], far[t * P:(t + 1) * P, :]).then_inc(mask_in[t % gt], 16)
                    if t < heads:
                        sp.dma_start(es_rows[:, t, :], across(es_dram[t * n_pad:(t + 1) * n_pad], n_pad)
                                     ).then_inc(es_in[t], 16)

            @block.vector
            def _(dve):
                steps = [(t, h) for h in range(heads) for t in range(gt)]
                steps += [(t, h) for t in range(gt, nt) for h in range(heads)]
                for n, (t, h) in enumerate(steps):
                    if h == 0:
                        dve.wait_ge(mask_in[t % gt], (t // gt + 1) * 16)
                    if t == 0:
                        dve.wait_ge(es_in[h], 16)
                    if n >= 2:
                        dve.wait_ge(seen, n - 1)
                    dve.tensor_tensor_reduce(junk[:, n % 2, :], es_rows[:, h, :], mask[:, t % gt, :], 1.0, -3e38,
                                             ALU.add, ALU.max, smax[:, h, t:t + 1]).then_inc(seen, 1)


def gat(nc, tag, c, fm, w, w_cols, a_src, a_dst, heads, table, far, nt, gt, dram, out_tile, eps, tail=None,
        bias=None):
    ch = w_cols // heads
    n_pad = nt * P
    with Scope(nc, tag) as s:
        h = s.sb("h", [P, T, heads, ch + 1])
        ec = s.sb("ec", [P, 2 * heads, nt])
        smax = s.sb("smax", [P, heads, nt])
        es2 = s.sb("es2", [P, heads, nt])
        shift = s.sb("shift", [P, heads, 2, nt])
        with Scope(nc, tag + "w") as q:
            wx = q.sb("wx", [P, KD, w_cols + 2 * heads])
            att = q.sb("att", [P, 2, w_cols])
            prod = q.sb("prod", [P, KD, 2, w_cols])
            load(nc, tag + "_load", (wx[:, :, 0:w_cols], w.rearrange("(k p) n -> p k n", p=P)),
                 (att[:, 0, :], across(a_src, w_cols)), (att[:, 1, :], across(a_dst, w_cols)))
            with stage(nc, tag + "_wa", "mul", "red") as (block, mul, red):
                @block.vector
                def _(dve):
                    for k in range(KD):
                        for a in range(2):
                            dve.tensor_tensor(prod[:, k, a, :], wx[:, k, 0:w_cols], att[:, a, :], ALU.mult).then_inc(mul, 1)
                    dve.wait_ge(mul, 2 * KD)
                    for k in range(KD):
                        for a in range(2):
                            dve.tensor_reduce(wx[:, k, w_cols + a * heads:w_cols + (a + 1) * heads],
                                              prod[:, k, a, :].rearrange("p (h c) -> p h c", h=heads), AX, ALU.add
                                              ).then_inc(red, 1)
                    dve.memset(h[:, :, :, ch:ch + 1], 1.0)

            def store(dve, t, ps):
                if t < nt:
                    dve.tensor_copy(ec[:, :, t], ps[:, w_cols:w_cols + 2 * heads])
                if t >= nt and tail is not None:
                    dve.tensor_copy(tail(t), ps[:, 0:w_cols])
                return dve.tensor_copy(h[:, t, :, 0:ch], ps[:, 0:w_cols].rearrange("p (h c) -> p h c", h=heads))

            product_nm(nc, tag + "_h", fm, wx, w_cols + 2 * heads, store)
        columns_out(nc, tag + "_es", ec[:, 0:heads, :].rearrange("p h t -> p (h t)"), heads * nt, c.ident, dram)
        neighbour_max(nc, tag + "_max", far, nt, gt, heads, dram, smax)
        with stage(nc, tag + "_shift", "step") as (block, step):
            @block.vector
            def _(dve):
                link = Link(dve, step)
                ed = ec[:, heads:2 * heads, :]
                link(dve.tensor_tensor(smax[:], smax[:], ed, ALU.add))
                link(dve.scalar_tensor_tensor(out=smax[:], in0=smax[:], scalar=SLOPE, in1=smax[:], op0=ALU.mult, op1=ALU.max))
                link(dve.tensor_tensor(shift[:, :, 0, :], ed, smax[:], ALU.subtract))
                link(dve.scalar_tensor_tensor(out=shift[:, :, 1, :], in0=ed, scalar=SLOPE, in1=smax[:], op0=ALU.mult,
                                              op1=ALU.subtract))
                link(dve.tensor_scalar(es2[:], ec[:, 0:heads, :], SLOPE, None, ALU.mult))
        columns_out(nc, tag + "_rows", shift[:].rearrange("p h a t -> p (h a t)"), heads * 2 * nt, c.ident, dram)
        aggregate(nc, tag + "_agg", c, table, nt, gt, lambda t, i: h[:, ds(t, 1), i, :].rearrange("p a c -> p (a c)"),
                  ch + 1, out_tile, attention=(dram, ec[:, 0:heads, :], es2), heads=heads, eps=eps,
                  bias=bias)



def first_max(dve, link, s, n, prio, top, onehot, tmp):
    link(dve.tensor_reduce(top[:], s[:], AX, ALU.max))
    link(dve.tensor_tensor(onehot[:], s[:], over_last(top[:], n), ALU.is_equal))
    link(dve.tensor_tensor(onehot[:], onehot[:], over_mid(prio[:, 0:n], T), ALU.mult))
    link(dve.tensor_reduce(tmp[:], onehot[:], AX, ALU.max))
    link(dve.tensor_tensor(onehot[:], onehot[:], over_last(tmp[:], n), ALU.is_equal))


def top2_gates(nc, tag, c, score, n, gate):
    with Scope(nc, tag) as s:
        prio = s.sb("prio", [P, n])
        top = s.sb("top", [P, T])
        top_b = s.sb("top_b", [P, T])
        one = s.sb("one", [P, T, n])
        tmp = s.sb("tmp", [P, T])
        ratio = s.sb("ratio", [P, T])
        with stage(nc, tag, "prio_set", "step", "diff", "expd") as (block, prio_set, step, diff, expd):
            @block.gpsimd
            def _(pool):
                pool.iota(prio[:], pattern=[[-1, n]], base=n, channel_multiplier=0,
                          allow_small_or_imprecise_dtypes=True).then_inc(prio_set, 1)

            @block.vector
            def _(dve):
                link = Link(dve, step)
                dve.wait_ge(prio_set, 1)
                first_max(dve, link, score, n, prio, top, gate, tmp)
                link(dve.scalar_tensor_tensor(out=score[:], in0=gate[:], scalar=-3e38, in1=score[:], op0=ALU.mult,
                                              op1=ALU.add))
                first_max(dve, link, score, n, prio, top_b, one, tmp)
                link(dve.tensor_tensor(ratio[:], top_b[:], top[:], ALU.subtract))
                dve.sem_inc(diff, 1)
                dve.wait_ge(expd, 1)
                link(dve.tensor_scalar(tmp[:], ratio[:], 1.0, None, ALU.add))
                link(dve.reciprocal(tmp[:], tmp[:]))
                link(dve.tensor_tensor(ratio[:], ratio[:], tmp[:], ALU.mult))
                link(dve.tensor_tensor(gate[:], gate[:], over_last(tmp[:], n), ALU.mult))
                link(dve.tensor_tensor(one[:], one[:], over_last(ratio[:], n), ALU.mult))
                link(dve.tensor_tensor(gate[:], gate[:], one[:], ALU.add))

            @block.scalar
            def _(act):
                act.wait_ge(diff, 1)
                act.activation(ratio[:], ratio[:], ACT.Exp).then_inc(expd, 1)


def softmax(nc, tag, logit, n, bias):
    with Scope(nc, tag) as s:
        top = s.sb("top", [P, T])
        with stage(nc, tag, "step", "shifted", "expd") as (block, step, shifted, expd):
            @block.vector
            def _(dve):
                link = Link(dve, step)
                link(dve.tensor_tensor(logit[:], logit[:], over_mid(bias[:], T), ALU.add))
                link(dve.tensor_reduce(top[:], logit[:], AX, ALU.max))
                dve.tensor_tensor(logit[:], logit[:], over_last(top[:], n), ALU.subtract).then_inc(shifted, 1)
                dve.wait_ge(expd, 1)
                link(dve.tensor_reduce(top[:], logit[:], AX, ALU.add))
                link(dve.reciprocal(top[:], top[:]))
                link(dve.tensor_tensor(logit[:], logit[:], over_last(top[:], n), ALU.mult))

            @block.scalar
            def _(act):
                act.wait_ge(shifted, 1)
                act.activation(logit[:], logit[:], ACT.Exp).then_inc(expd, 1)


def turn_gates(nc, tag, c, gate, n, gate_fm):
    with Scope(nc, tag) as s:
        pt = s.ps("pt", [n, 4, 4 * P])
        with stage(nc, tag, "turned", "out") as (block, turned, out):
            quads = [(t, min(4, T - t)) for t in range(0, T, 4)]

            @block.tensor
            def _(pe):
                for i, (t, m) in enumerate(quads):
                    if i >= 4:
                        pe.wait_ge(out, i - 3)
                    for j in range(m):
                        last = pe.transpose(pt[:, i % 4, j * P:(j + 1) * P], gate[:, t + j, :], c.ident[:])
                    last.then_inc(turned, 1)

            @block.vector
            def _(dve):
                for i, (t, m) in enumerate(quads):
                    dve.wait_ge(turned, i + 1)
                    dve.tensor_copy(gate_fm[:, t * P:(t + m) * P], pt[:, i % 4, 0:m * P]).then_inc(out, 1)


def experts(nc, tag, c, fm, x, gate, n_e, layers, last_w, last_bias):
    half = G1 * P // 2
    chunk = G1 * P
    nh = [2 if i == 0 else 1 for i in range(len(layers))]
    k_last = layers[-1][2]
    with Scope(nc, tag) as s:
        gate_fm = s.sb("gate_fm", [n_e, NP])
        turn_gates(nc, tag + "_gt", c, gate, n_e, gate_fm)
        gate_c = s.sb("gate_c", [n_e, chunk])
        hid = [s.sb(f"hid{i}", [P, nh[i], m, chunk]) for i, (_, _, m, _, _, _) in enumerate(layers)]
        ph = s.ps("ph", [P, 2, 2, 512])
        py = s.ps("py", [P, 4, 512])
        nl = len(layers)
        with stage(nc, tag, "gate_in", "hid_ready", *[f"act{i}" for i in range(nl)], "y_ready", "y_free") as (
                block, *sems):
            gate_in, hid_ready = sems[:2]
            acted = sems[2:2 + nl]
            y_ready, y_free = sems[2 + nl:]

            order = [(0, 0)]
            for e in range(n_e):
                order += [(i, e) for i in range(1, min(2, nl))]
                order += [(0, e + 1)] * (e + 1 < n_e)
                order += [(i, e) for i in range(2, nl)] + [("y", e)]
            parts = [(kind, e, m) for kind, e in order if kind != "y" for m in range(layers[kind][2])]
            nb_all, ny_all = len(parts), G1 * (n_e + 1)

            def wait_block(eng, g, nb):
                eng.wait_ge(hid_ready, g * nb_all + (nb_all + nb + 1))

            def wait_y(eng, g, ny):
                eng.wait_ge(y_ready, g * ny_all + (ny_all + ny + 1))

            def wait_acted(eng, g, nb):
                kind, e, m = parts[nb]
                mm = layers[kind][2]
                eng.wait_ge(acted[kind], g * (n_e * mm) + ((n_e * mm if nb >= 0 else 0) + e * mm + m + 1))

            def wait_unused(eng, g, kind, e):
                last, back = (e - nh[kind]) % n_e, e < nh[kind]
                if kind + 1 < nl:
                    wait_block(eng, g, parts.index((kind + 1, last, layers[kind + 1][2] - 1)) - (nb_all if back else 0))
                else:
                    wait_y(eng, g, G1 * (last + 2) - 1 - (ny_all if back else 0))

            @block.gpsimd
            def _(pool):
                with pool.Fori(0, T // G1) as g:
                    wait_y(pool, g, G1 - 1 - ny_all)
                    pool.tensor_copy(gate_c[:], gate_fm[:, ds(g * chunk, chunk)]).then_inc(gate_in, 1)

            @block.tensor
            def _(pe):
                pe.sem_inc(y_free, 5)
                pe.sem_inc(y_ready, ny_all)
                pe.sem_inc(hid_ready, nb_all)
                for i in range(nl):
                    pe.sem_inc(acted[i], n_e * layers[i][2])
                with pe.Fori(0, T // G1) as g:
                    pe.wait_ge(gate_in, g + 1)
                    for tt in range(G1):
                        pe.wait_ge(y_free, g * ny_all + max(tt + 2, 5))
                        pe.matmul(py[:, tt % 4, 0:D], gate_c[:, tt * P:(tt + 1) * P], last_bias[:],
                                  start=True, stop=True).then_inc(y_ready, 1)
                    nb, ny = 0, G1
                    for kind, e in order:
                        if kind == "y":
                            wait_acted(pe, g, parts.index((nl - 1, e, k_last - 1)))
                            for tt in range(G1):
                                pe.wait_ge(y_free, g * ny_all + (ny + 2))
                                for k in range(k_last):
                                    last = pe.matmul(py[:, ny % 4, 0:D], hid[-1][:, e % nh[-1], k, tt * P:(tt + 1) * P],
                                                     last_w[:, e, k, :], start=(k == 0), stop=(k == k_last - 1))
                                last.then_inc(y_ready, 1)
                                ny += 1
                            continue
                        w, kk, mm, _, _, _ = layers[kind]
                        if kind:
                            wait_acted(pe, g, parts.index((kind - 1, e, layers[kind - 1][2] - 1)))
                        for m in range(mm):
                            wait_acted(pe, g, nb - 2)
                            for j in range(2):
                                for k in range(kk):
                                    rhs = (fm[:, k, ds(g * chunk + j * half, half)] if kind == 0 else
                                           hid[kind - 1][:, e % nh[kind - 1], k, j * half:(j + 1) * half])
                                    last = pe.matmul(ph[:, nb % 2, j, 0:half], w[:, e, k, m * P:(m + 1) * P], rhs,
                                                     start=(k == 0), stop=(k == kk - 1))
                            last.then_inc(hid_ready, 1)
                            nb += 1

            @block.scalar
            def _(act):
                with act.Fori(0, T // G1) as g:
                    for nb, (kind, e, m) in enumerate(parts):
                        _, _, mm, func, scale, bias = layers[kind]
                        if m == 0:
                            wait_unused(act, g, kind, e)
                        wait_block(act, g, nb)
                        act.activation(hid[kind][:, e % nh[kind], m, :].rearrange("p (j n) -> p j n", j=2),
                                       ph[:, nb % 2, :, 0:half], func, bias=bias[:, e, m:m + 1],
                                       scale=1.0 if scale is None else scale[:, e, m:m + 1]).then_inc(acted[kind], 1)

            @block.vector
            def _(dve):
                with dve.Fori(0, T // G1) as g:
                    ny = 0
                    for e in range(-1, n_e):
                        for tt in range(G1):
                            xt = x[:, ds(g * G1 + tt, 1), :].rearrange("p a d -> p (a d)")
                            wait_y(dve, g, ny)
                            dve.wait_ge(y_free, g * ny_all + (ny + 1))
                            if e < 0:
                                ins = dve.tensor_tensor(xt, py[:, ny % 4, 0:D], xt, ALU.add)
                            else:
                                ins = dve.scalar_tensor_tensor(
                                    out=xt, in0=py[:, ny % 4, 0:D], scalar=gate[:, ds(g * G1 + tt, 1), e], in1=xt,
                                    op0=ALU.mult, op1=ALU.add)
                            ins.then_inc(y_free, 1)
                            ny += 1



def add_relu(nc, tag, x, a):
    with stage(nc, tag) as (block,):
        @block.vector
        def _(dve):
            dve.scalar_tensor_tensor(out=x[:], in0=a[:], scalar=0.0, in1=x[:], op0=ALU.max, op1=ALU.add)


def add_unit_rows(nc, tag, x, a, bias=None):
    gs = [(g * G1, (g + 1) * G1) for g in range(T // G1)]
    with Scope(nc, tag) as s:
        sq = s.sb("sq", [P, 2, D])
        ss = s.sb("ss", [P, T])
        with stage(nc, tag, "biased", "squared", "root", "step", "added") as (block, biased, squared, root, step, added):
            @block.vector
            def _(dve):
                link = Link(dve, step)
                if bias is not None:
                    for lo, hi in gs:
                        link(dve.tensor_tensor(a[:, lo:hi, :], a[:, lo:hi, :], over_mid(bias[:], G1), ALU.add))
                        dve.tensor_scalar(a[:, lo:hi, :], a[:, lo:hi, :], 0.0, None, ALU.max).then_inc(biased, 1)
                for g, (lo, hi) in enumerate(gs):
                    dve.wait_ge(root, g + 1)
                    link(dve.tensor_scalar(ss[:, lo:hi], ss[:, lo:hi], 1e-12, None, ALU.max))
                    link(dve.reciprocal(ss[:, lo:hi], ss[:, lo:hi]))
                    for t in range(lo, hi):
                        dve.scalar_tensor_tensor(out=x[:, t, :], in0=a[:, t, :], scalar=ss[:, t:t + 1], in1=x[:, t, :],
                                                 op0=ALU.mult, op1=ALU.add).then_inc(added, 1)

            @block.scalar
            def _(act):
                for g, (lo, hi) in enumerate(gs):
                    if bias is not None:
                        act.wait_ge(biased, g + 1)
                    for t in range(lo, hi):
                        if t >= 2:
                            act.wait_ge(squared, t - 1)
                        act.activation(sq[:, t % 2, :], a[:, t, :], ACT.Square, accum_out=ss[:, t:t + 1]
                                       ).then_inc(squared, 1)
                    act.wait_ge(squared, hi)
                    act.activation(ss[:, lo:hi], ss[:, lo:hi], ACT.Sqrt).then_inc(root, 1)


def batchnorm_columns(nc, tag, fm, gamma, beta, scale, shift, given=None, relu=False):
    n = 500
    nb = -(-N // n)
    with Scope(nc, tag) as s:
        stats = s.sb("stats", [P, KD, nb, 6]) if given is None else given
        mv = s.sb("mv", [P, KD, 2])
        with stage(nc, tag, "stat", "eps", "root", "step", "scaled") as (block, stat, eps, root, step, scaled):
            @block.vector
            def _(dve):
                link = Link(dve, step)
                for k in range(KD if given is None else 0):
                    for b in range(nb):
                        dve.bn_stats(stats[:, k, b, :], fm[:, k, b * n:min((b + 1) * n, N)]).then_inc(stat, 1)
                if given is None:
                    dve.wait_ge(stat, KD * nb)
                for k in range(KD):
                    link(dve.bn_aggr(mv[:, k, :], stats[:, k].rearrange("p b s -> p (b s)")))
                dve.tensor_scalar(scale[:], mv[:, :, 1], 1e-5, None, ALU.add).then_inc(eps, 1)
                dve.wait_ge(root, 1)
                link(dve.reciprocal(scale[:], scale[:]))
                link(dve.tensor_tensor(scale[:], scale[:], gamma[:], ALU.mult))
                link(dve.tensor_tensor(shift[:], mv[:, :, 0], scale[:], ALU.mult))
                link(dve.tensor_tensor(shift[:], beta[:], shift[:], ALU.subtract))
                if relu:
                    dve.sem_inc(scaled, 1)
                    link(dve.tensor_scalar(fm[:, 1, :], fm[:, 1, :], scale[:, 1:2], shift[:, 1:2], ALU.mult, ALU.add))
                    dve.tensor_scalar(fm[:, 1, :], fm[:, 1, :], 0.0, None, ALU.max)

            @block.scalar
            def _(act):
                act.wait_ge(eps, 1)
                act.activation(scale[:], scale[:], ACT.Sqrt).then_inc(root, 1)
                if relu:
                    act.wait_ge(scaled, 1)
                    act.activation(fm[:, 0, :], fm[:, 0, :], ACT.Relu, bias=shift[:, 0:1], scale=scale[:, 0:1])


class Consts:
    pass


def vec_cols(v):
    return v.rearrange("(m p) -> p m", p=P)


def build(nc, a, out):
    size1, size2 = NP * NP + W * P, N2 * N2 + W * P
    table1 = nc.dram_tensor("table1", (size1, 1), F32, kind="Internal").ap()
    table2 = nc.dram_tensor("table2", (size2, 1), F32, kind="Internal").ap()
    far1 = nc.dram_tensor("far1", (NP, NP), BF16, kind="Internal").ap()
    far2 = nc.dram_tensor("far2", (N2, N2), BF16, kind="Internal").ap()
    keys = nc.dram_tensor("edge_keys", ((NCH1 + NCH2) * P,), F32, kind="Internal").ap()
    dram = nc.dram_tensor("row_scratch", (2 * P * P,), F32, kind="Internal").ap()
    with Scope(nc, "all") as top:
        c = Consts()
        c.routed = (nc.dram_tensor("routed_in", (ROUTED + NP, D), F32, kind="Internal").ap(),
                    nc.dram_tensor("routed_out", (ROUTED, D), F32, kind="Internal").ap())
        c.ident = top.sb("ident", [P, P])
        c.zero = top.sb("zero", [1, 512], BF16)
        degree = top.sb("degree", [P, T])
        dinv = top.sb("dinv", [P, T])
        x = top.sb("x", [P, T, D])
        full = N // P
        rest = N - full * P
        landed = [top.cx.enter_context(nc.semaphore(f"edges{i}_landed")) for i in (1, 2)]
        table_set = [top.cx.enter_context(nc.semaphore(f"table{i}_set")) for i in (1, 2)]
        c.loaded = [top.cx.enter_context(nc.semaphore(f"loaded{i}")) for i in range(2)]
        c.n_loaded = [0, 0]
        c.put_landed = top.cx.enter_context(nc.semaphore("put_landed"))
        c.get_landed = [top.cx.enter_context(nc.semaphore(f"get{g}_landed")) for g in range(T // G1)]
        first = Scope(nc, "first")
        xt0 = first.sb("xt", [P, KD, NP])
        w0 = first.sb("w", [P, 2, KD, D])
        gw = first.sb("gw", [P, KD, D])
        bias0 = first.sb("bias", [P, D])
        cell2 = first.sb("cell2", [P, NCH2], U32)
        count2 = first.sb("count2", [P, NCH2])
        cell = first.sb("cell", [P, 2, W], U32)
        count = first.sb("count", [P, 2, W])
        counting = Scope(nc, "counting")
        eye_rows = counting.sb("eye_rows", [P, 2 * NP])
        cell1 = counting.sb("cell1", [P, NCH1], U32)
        count1 = counting.sb("count1", [P, NCH1])
        ids = counting.sb("ids", [P, 2, NCH1 + NCH2], I32)

        def set_table(eng, g, table, n_pad):
            for t in range(n_pad // P):
                eng.dma_start(table[0:n_pad * n_pad, 0].rearrange("(r n) -> r n", n=n_pad)[t * P:(t + 1) * P, :],
                              eye_rows[:, NP - t * P:NP - t * P + n_pad]).then_inc(table_set[g], 16)

        with stage(nc, "start", "set", "pad", "xin", "eye") as (block, set_, pad, xin, eye):
            @block.gpsimd
            def _(pool):
                pool.memset(eye_rows[:], 0.0).then_inc(eye, 1)
                pool.memset(x[:, T - 1, :], 0.0).then_inc(pad, 1)
                pool.wait_ge(eye, 1)
                pool.affine_select(out=eye_rows[:], in_=eye_rows[:], compare_op=ALU.not_equal, fill=1.0,
                                   base=-NP, pattern=[[1, 2 * NP]], channel_multiplier=-1).then_inc(eye, 1)
                pool.memset(c.ident[:], 0.0).then_inc(set_, 1)
                pool.memset(c.zero[:], 0.0).then_inc(set_, 1)
                pool.wait_ge(set_, 1)
                pool.wait_ge(set_, 2)
                pool.affine_select(out=c.ident[:], in_=c.ident[:], compare_op=ALU.not_equal, fill=1.0, base=0,
                                   pattern=[[-1, P]], channel_multiplier=1).then_inc(set_, 1)

            @block.scalar
            def _(act):
                act.wait_ge(eye, 2)
                set_table(act, 0, table1, NP)

            @block.sync
            def _(sp):
                for at, nch, src, dst in ((0, NCH1, a["src"], a["dst"]),
                                          (NCH1, NCH2, a["L0_ffn_edge_index"][0, :], a["L0_ffn_edge_index"][1, :])):
                    for i, ends in enumerate((src, dst)):
                        sp.dma_start(ids[:, i, at:at + nch], ends.rearrange("(p c) -> p c", p=P)).then_inc(xin, 16)
                for dst, src in ((w0[:, 0], a["L0_gnn_W_gcn"].rearrange("(k p) n -> p k n", p=P)),
                                 (w0[:, 1], a["L0_gnn_W_V"].rearrange("(k p) n -> p k n", p=P)),
                                 (bias0[:], across(a["L0_gnn_b_gcn"], D))):
                    sp.dma_start(dst, src).then_inc(xin, 16)
                sp.dma_start(x[:, 0:full, :], a["x"][0:full * P, :].rearrange("(t p) d -> p t d", p=P)).then_inc(xin, 16)
                sp.wait_ge(pad, 1)
                sp.dma_start(x[0:rest, full, :], a["x"][full * P:N, :]).then_inc(xin, 16)
                sp.wait_ge(xin, 16 * 9)
        adder = [Adder(table1, NP, cell1, count1, cell, count, landed[0]),
                 Adder(table2, N2, cell2, count2, cell, count, landed[1])]
        l0_gnn_start(nc, c, x, xt0, w0, gw)
        count_edges(nc, [(NCH1, NP), (NCH2, N2)], ids, keys, lambda eng: set_table(eng, 1, table2, N2), table_set,
                    c.ident, [cell1, cell2], [count1, count2], adder)
        counting.__exit__(None, None, None)
        with stage(nc, "table2", "z") as (block, z):
            @block.gpsimd
            def _(pool):
                pool.wait_ge(table_set[1], 16 * T2)
        some = 6
        mask_and_degrees(nc, "m1", table1, T, G1, far1, c.ident, degree, (adder[1], 0, some))
        with stage(nc, "dinv", "clamped", "root") as (block, clamped, root):
            @block.vector
            def _(dve):
                dve.tensor_scalar(dinv[:], degree[:], 1e-30, None, ALU.max).then_inc(clamped, 1)
                dve.wait_ge(root, 1)
                dve.reciprocal(dinv[:], dinv[:])

            @block.scalar
            def _(act):
                act.wait_ge(clamped, 1)
                act.activation(dinv[:], dinv[:], ACT.Sqrt).then_inc(root, 1)

        l0_gnn(nc, c, x, xt0, w0, gw, bias0, table1, dinv, (adder[1], some, NCH2 // W))
        first.__exit__(None, None, None)
        for name, part in PARTS:
            part(nc, c, a, x, (table1, far1, table2, far2), dinv, dram)

        with stage(nc, "end", "out") as (block, out_sem):
            @block.sync
            def _(sp):
                sp.dma_start(out[0:full * P, :].rearrange("(t p) d -> p t d", p=P), x[:, 0:full, :]).then_inc(out_sem, 16)
                sp.dma_start(out[full * P:N, :], x[0:rest, full, :]).then_inc(out_sem, 16)
                sp.wait_ge(out_sem, 32)


def l0_gnn_start(nc, c, x, xt, w, gw):
    with Scope(nc, "l0s") as s:
        xn = s.sb("xn", [P, T, D])
        gram = s.sb("gram", [P, KD, D])
        layernorm(nc, "l0g_ln", c, x, xn, xt, unit=True)
        with Scope(nc, "l0gg") as q:
            pg = q.ps("pg", [P, 2, KD, 512])
            with stage(nc, "l0g_gram", "gram_ps", "gram_sb", "gw_ps") as (block, gram_ps, gram_sb, gw_ps):
                @block.tensor
                def _(pe):
                    for m in range(KD):
                        for t in range(T):
                            last = pe.matmul(pg[:, 0, m, 0:D], xn[:, t, m * P:(m + 1) * P], xn[:, t, :],
                                             start=(t == 0), stop=(t == T - 1))
                    last.then_inc(gram_ps, 1)
                    pe.wait_ge(gram_sb, 1)
                    for m in range(KD):
                        for k in range(KD):
                            last = pe.matmul(pg[:, 1, m, 0:D], gram[:, k, m * P:(m + 1) * P], w[:, 1, k, :],
                                             start=(k == 0), stop=(k == KD - 1))
                    last.then_inc(gw_ps, 1)

                @block.vector
                def _(dve):
                    dve.wait_ge(gram_ps, 1)
                    dve.tensor_copy(gram[:], pg[:, 0, :, 0:D]).then_inc(gram_sb, 1)
                    dve.wait_ge(gw_ps, 1)
                    dve.tensor_copy(gw[:], pg[:, 1, :, 0:D])


def l0_gnn(nc, c, x, xt, w, gw, bias, table, dinv, beside):
    with Scope(nc, "l0g") as s:
        h = s.sb("h", [P, T, D])
        agg = s.sb("agg", [P, T, D])
        product_nm(nc, "l0g_w", xt, w[:, 0], D,
                   lambda dve, t, ps: dve.tensor_scalar(h[:, t, :], ps, dinv[:, t:t + 1], None, ALU.mult))
        aggregate(nc, "l0g_agg", c, table, T, G1, lambda t, i: h[:, ds(t, 1), :].rearrange("p a d -> p (a d)"), D,
                  lambda t, i: agg[:, ds(t, 1), :].rearrange("p a d -> p (a d)"), scale=dinv, beside=beside)
        product_nm(nc, "l0g_z", xt, gw, D, lambda dve, t, ps: dve.scalar_tensor_tensor(
            out=agg[:, t, :], in0=ps, scalar=0.1 / N, in1=agg[:, t, :], op0=ALU.mult, op1=ALU.add))
        add_unit_rows(nc, "l0g_end", x, agg, bias)


def l0_ffn(nc, c, a, x, tables, dinv, dram):
    hd, ne = 4, 4
    mask_and_degrees(nc, "m2", tables[2], T2, G2, tables[3], c.ident, None)
    with Scope(nc, "l0f") as s:
        xt = s.sb("xt", [P, KD, NP])
        gate = s.sb("gate", [P, T, ne])
        w1 = s.sb("w1", [P, ne, KD, 2 * D])
        b1 = s.sb("b1", [P, ne, 2 * KD])
        w2 = s.sb("w2", [P, ne, 2 * KD, D])
        b2 = s.sb("b2", [ne, D])
        rows = s.sb("rows", [P, 3, hd * ne])
        normal_input(nc, "l0f", c, x, xt, [
            [(rows[:, 0], across(a["L0_ffn_b_gat"], hd * ne)), (rows[:, 1], across(a["L0_ffn_ln_gamma"], hd * ne)),
             (rows[:, 2], across(a["L0_ffn_ln_beta"], hd * ne)), (b2[:], a["L0_ffn_b2"]),
             (b1[:].rearrange("p e k -> p (e k)"), vec_cols(a["L0_ffn_b1"].rearrange("e n -> (e n)")))] +
            [(w1[:, e], a["L0_ffn_W1"][e].rearrange("(k p) n -> p k n", p=P)) for e in range(ne)] +
            [(w2[:, e], a["L0_ffn_W2"][e].rearrange("(k p) n -> p k n", p=P)) for e in range(ne)]])
        with Scope(nc, "l0fb") as q:
            agg = q.sb("agg", [P, T, hd * ne])
            gat(nc, "l0f_gat", c, xt, a["L0_ffn_W_gat"], hd * ne, a["L0_ffn_att_src"].rearrange("h c -> (h c)"),
                a["L0_ffn_att_dst"].rearrange("h c -> (h c)"), hd, tables[2], tables[3], T2, 2 * G2, dram,
                lambda t, i: agg[:, ds(t, 1), i * ne:(i + 1) * ne].rearrange("p a d -> p (a d)"), 1e-16,
                tail=lambda t: agg[:, t, :])
            settle(nc, "l0f_settle", c, 0)
            score = q.sb("score", [P, T, ne])
            sq = q.sb("sq", [P, T, hd * ne])
            m = q.sb("m", [P, T])
            v = q.sb("v", [P, T])
            with stage(nc, "l0f_score", "step", "ready", "root") as (block, step, ready, root):
                @block.vector
                def _(dve):
                    link = Link(dve, step)
                    n = hd * ne
                    link(dve.tensor_tensor(agg[:], agg[:], over_mid(rows[:, 0, :], T), ALU.add))
                    link(dve.tensor_reduce(m[:], agg[:], AX, ALU.add))
                    link(dve.tensor_scalar(m[:], m[:], 1.0 / n, None, ALU.mult))
                    link(dve.tensor_tensor(agg[:], agg[:], over_last(m[:], n), ALU.subtract))
                    link(dve.tensor_tensor(sq[:], agg[:], agg[:], ALU.mult))
                    link(dve.tensor_reduce(v[:], sq[:], AX, ALU.add))
                    dve.tensor_scalar(v[:], v[:], 1.0 / n, 1e-5, ALU.mult, ALU.add).then_inc(ready, 1)
                    dve.wait_ge(root, 1)
                    link(dve.reciprocal(v[:], v[:]))
                    link(dve.tensor_tensor(agg[:], agg[:], over_last(v[:], n), ALU.mult))
                    link(dve.tensor_tensor(agg[:], agg[:], over_mid(rows[:, 1, :], T), ALU.mult))
                    link(dve.tensor_tensor(agg[:], agg[:], over_mid(rows[:, 2, :], T), ALU.add))
                    link(dve.tensor_tensor(score[:], agg[:, :, 0:ne], agg[:, :, ne:2 * ne], ALU.add))
                    for i in range(2, hd):
                        link(dve.tensor_tensor(score[:], score[:], agg[:, :, i * ne:(i + 1) * ne], ALU.add))
                    link(dve.tensor_scalar(score[:], score[:], 1.0 / hd, None, ALU.mult))

                @block.scalar
                def _(act):
                    act.wait_ge(ready, 1)
                    act.activation(v[:], v[:], ACT.Sqrt).then_inc(root, 1)
            top2_gates(nc, "l0f_top", c, score, ne, gate)
        experts(nc, "l0f_moe", c, xt, x, gate, ne, [(w1, KD, 2 * KD, ACT.Gelu, None, b1)], w2, b2)


def l1_gnn(nc, c, a, x, tables, dinv, dram):
    with Scope(nc, "l1g") as s:
        xt = s.sb("xt", [P, KD, NP])
        agg = s.sb("agg", [P, T, D])
        bias = s.sb("bias", [P, KD])
        bias2 = s.sb("bias2", [P, D])
        with Scope(nc, "l1ga") as q:
            h = q.sb("h", [P, T, D])
            w = q.sb("w", [P, KD, D])
            load(nc, "l1g_load", (w[:], a["L1_gnn_W1"].rearrange("(k p) n -> p k n", p=P)),
                 (bias[:], vec_cols(a["L1_gnn_b1"])), (bias2[:], across(a["L1_gnn_b2"], D)))
            layernorm(nc, "l1g_ln", c, x, h, xt)
            product_nm(nc, "l1g_w", xt, w, D,
                       lambda dve, t, ps: dve.tensor_scalar(h[:, t, :], ps, dinv[:, t:t + 1], None, ALU.mult))
            aggregate(nc, "l1g_agg", c, tables[0], T, G1, lambda t, i: h[:, ds(t, 1), :].rearrange("p a d -> p (a d)"), D,
                      lambda t, i: agg[:, ds(t, 1), :].rearrange("p a d -> p (a d)"), scale=dinv)
        turn(nc, "l1g_t2", agg, xt, c.ident, bias=bias, func=ACT.Relu)
        gat(nc, "l1g_gat", c, xt, a["L1_gnn_W2"], D, a["L1_gnn_att_src"], a["L1_gnn_att_dst"], 1, tables[0], tables[1],
            T, G1, dram, lambda t, i: agg[:, ds(t, 1), :].rearrange("p a d -> p (a d)"), 1e-16, bias=bias2)
        add_relu(nc, "l1g_end", x, agg)


def normal_input(nc, tag, c, x, xt, ahead=()):
    with Scope(nc, tag + "n") as q:
        xn = q.sb("xn", [P, T, D])
        layernorm(nc, tag + "_ln", c, x, xn, xt, ahead=ahead)


def l1_ffn(nc, c, a, x, tables, dinv, dram):
    ne = 8
    f = "L1_ffn_"
    with Scope(nc, "l1f") as s:
        xt = s.sb("xt", [P, KD, NP])
        gate = s.sb("gate", [P, T, ne])
        wr = s.sb("wr", [P, KD, ne])
        br = s.sb("br", [P, ne])
        ws = [s.sb(f"w{i}", [P, ne, KD, D]) for i in range(3)]
        vec = s.sb("vec", [P, 2, 5, ne, KD])
        bo = s.sb("bo", [ne, D])
        names = [["b1", "g1", "be1", "m1", "v1"], ["b2", "g2", "be2", "m2", "v2"]]
        normal_input(nc, "l1f", c, x, xt, [
            [(wr[:], a[f + "Wr"].rearrange("(k p) n -> p k n", p=P)), (br[:], across(a[f + "br"], ne))],
            [(vec[:, i, j].rearrange("p e k -> p (e k)"), vec_cols(a[f + names[i][j]].rearrange("e n -> (e n)")))
             for i in range(2) for j in range(5)] + [(bo[:], a[f + "bo"])] +
            [(ws[i][:, e], a[f + n][e].rearrange("(k p) n -> p k n", p=P)) for i, n in enumerate(["W1", "W2", "Wo"])
             for e in range(ne)]])
        settle(nc, "l1f_settle0", c, 0)
        product_nm(nc, "l1f_r", xt, wr, ne, lambda dve, t, ps: dve.tensor_copy(gate[:, t, :], ps))
        softmax(nc, "l1f_sm", gate, ne, br)
        settle(nc, "l1f_settle1", c, 1)
        with stage(nc, "l1f_bn", "step", "ready", "root") as (block, step, ready, root):
            @block.vector
            def _(dve):
                link = Link(dve, step)
                dve.tensor_scalar(vec[:, :, 4], vec[:, :, 4], 1e-3, None, ALU.add).then_inc(ready, 1)
                dve.wait_ge(root, 1)
                link(dve.reciprocal(vec[:, :, 4], vec[:, :, 4]))
                link(dve.tensor_tensor(vec[:, :, 1], vec[:, :, 1], vec[:, :, 4], ALU.mult))
                link(dve.tensor_tensor(vec[:, :, 0], vec[:, :, 0], vec[:, :, 3], ALU.subtract))
                link(dve.tensor_tensor(vec[:, :, 0], vec[:, :, 0], vec[:, :, 1], ALU.mult))
                link(dve.tensor_tensor(vec[:, :, 0], vec[:, :, 0], vec[:, :, 2], ALU.add))

            @block.scalar
            def _(act):
                act.wait_ge(ready, 1)
                act.activation(vec[:, :, 4], vec[:, :, 4], ACT.Sqrt).then_inc(root, 1)
        experts(nc, "l1f_moe", c, xt, x, gate, ne,
                [(ws[i], KD, KD, ACT.Relu, vec[:, i, 1], vec[:, i, 0]) for i in range(2)], ws[2], bo)


def l2_gnn(nc, c, a, x, tables, dinv, dram):
    f = "L2_gnn_"
    with Scope(nc, "l2g") as s:
        xt = s.sb("xt", [P, KD, NP])
        agg = s.sb("agg", [P, T, D])
        vec = s.sb("vec", [P, 3, KD])
        bias = s.sb("bias", [P, D])
        scale = s.sb("scale", [P, KD])
        shift = s.sb("shift", [P, KD])
        normal_input(nc, "l2g", c, x, xt)
        load(nc, "l2g_load", (vec[:, 0], vec_cols(a[f + "b0"])), (vec[:, 1], vec_cols(a[f + "gamma0"])),
             (vec[:, 2], vec_cols(a[f + "beta0"])), (bias[:], across(a[f + "b1"], D)))
        gat(nc, "l2g_a", c, xt, a[f + "W0"], D, a[f + "a_src0"].rearrange("h c -> (h c)"),
            a[f + "a_dst0"].rearrange("h c -> (h c)"), 4, tables[0], tables[1], T, G1, dram,
            lambda t, i: agg[:, ds(t, 1), i * 64:(i + 1) * 64].rearrange("p a d -> p (a d)"), 0.0)
        turn(nc, "l2g_t2", agg, xt, c.ident, bias=vec[:, 0])
        batchnorm_columns(nc, "l2g_bn", xt, vec[:, 1], vec[:, 2], scale, shift)
        with Scope(nc, "l2e") as q:
            low = q.sb("low", [P, KD, NP])
            with stage(nc, "l2g_elu", "step", "ready", "expd") as (block, step, ready, expd):
                @block.vector
                def _(dve):
                    for k in range(KD):
                        dve.tensor_scalar(xt[:, k, :], xt[:, k, :], scale[:, k:k + 1], shift[:, k:k + 1],
                                          ALU.mult, ALU.add).then_inc(step, 1)
                        dve.wait_ge(step, 2 * k + 1)
                        dve.tensor_scalar(low[:, k, :], xt[:, k, :], 0.0, None, ALU.min).then_inc(ready, 1)
                        dve.tensor_scalar(xt[:, k, :], xt[:, k, :], 0.0, -1.0, ALU.max, ALU.add).then_inc(step, 1)
                        dve.wait_ge(step, 2 * k + 2)
                    for k in range(KD):
                        dve.wait_ge(expd, k + 1)
                        dve.tensor_tensor(xt[:, k, :], xt[:, k, :], low[:, k, :], ALU.add)

                @block.scalar
                def _(act):
                    for k in range(KD):
                        act.wait_ge(ready, k + 1)
                        act.activation(low[:, k, :], low[:, k, :], ACT.Exp).then_inc(expd, 1)
        gat(nc, "l2g_b", c, xt, a[f + "W1"], D, a[f + "a_src1"].rearrange("h c -> (h c)"),
            a[f + "a_dst1"].rearrange("h c -> (h c)"), 1, tables[0], tables[1], T, G1, dram,
            lambda t, i: agg[:, ds(t, 1), :].rearrange("p a d -> p (a d)"), 0.0, bias=bias)
        add_unit_rows(nc, "l2g_end", x, agg)


def l2_ffn(nc, c, a, x, tables, dinv, dram):
    ne, fh = 8, 1024
    cap = -(-5 * N // (4 * ne))
    room = -(-cap // P) * P
    f = "L2_ffn_"
    with Scope(nc, "l2f") as s:
        xn = s.sb("xn", [P, T, D])
        factor = s.sb("factor", [P, T])
        put = s.sb("put", [P, T], U32)
        get = s.sb("get", [P, T], U32)
        with Scope(nc, "l2fr") as q:
            xt = q.sb("xt", [P, KD, NP])
            gate = q.sb("gate", [P, T, ne])
            wr = q.sb("wr", [P, KD, ne])
            br = q.sb("br", [P, ne])
            prio = q.sb("prio", [P, ne])
            base = q.sb("base", [P, ne])
            behind = q.sb("behind", [P, T])
            upto = q.sb("upto", [P, P])
            ones = q.sb("ones", [P, P])
            prob = q.sb("prob", [P, T])
            tmp = q.sb("tmp", [P, T])
            kept = q.sb("kept", [P, T])
            place = q.sb("place", [P, T])
            one = q.sb("one", [P, T, ne])
            pos = q.sb("pos", [P, T, ne])
            tot = q.sb("tot", [P, T + 1, ne])
            zero = q.sb("zero", [P, 1024])
            with stage(nc, "l2f_zero", "zero_set") as (block, zero_set):
                @block.gpsimd
                def _(pool):
                    pool.memset(zero[:], 0.0).then_inc(zero_set, 1)
            room_cols = c.routed[0][0:ne * room, :].rearrange("(p r) d -> p (r d)", p=P)
            layernorm(nc, "l2f_ln", c, x, xn, xt, ahead=[
                [(room_cols[:, at:at + 1024], zero[:]) for at in range(0, ne * room * D // P, 1024)]])
            load(nc, "l2f_loadr", (wr[:], a[f + "gate_w"].rearrange("(k p) n -> p k n", p=P)),
                 (br[:], across(a[f + "gate_b"], ne)))
            product_nm(nc, "l2f_r", xt, wr, ne, lambda dve, t, ps: dve.tensor_copy(gate[:, t, :], ps))
            softmax(nc, "l2f_sm", gate, ne, br)
            pp = q.ps("pp", [P, 2, 512])
            settle(nc, "l2f_settle", c, 0)
            with stage(nc, "l2f_pos", "sets", "step", "chosen", "summed") as (block, sets, step, chosen, summed):
                @block.gpsimd
                def _(pool):
                    pool.iota(prio[:], pattern=[[-1, ne]], base=ne, channel_multiplier=0,
                              allow_small_or_imprecise_dtypes=True).then_inc(sets, 1)
                    pool.iota(base[:], pattern=[[room, ne]], base=-1, channel_multiplier=0,
                              allow_small_or_imprecise_dtypes=True).then_inc(sets, 1)
                    pool.iota(behind[:], pattern=[[P, T]], base=ne * room, channel_multiplier=1,
                              allow_small_or_imprecise_dtypes=True).then_inc(sets, 1)
                    pool.memset(ones[:], 1.0).then_inc(sets, 1)
                    pool.memset(upto[:], 1.0).then_inc(sets, 1)
                    pool.wait_ge(sets, 5)
                    pool.affine_select(out=upto[:], in_=upto[:], compare_op=ALU.is_ge, fill=0.0, base=0,
                                       pattern=[[1, P]], channel_multiplier=-1).then_inc(sets, 1)

                @block.vector
                def _(dve):
                    link = Link(dve, step)
                    dve.wait_ge(sets, 6)
                    first_max(dve, link, gate, ne, prio, prob, one, tmp)
                    dve.sem_inc(chosen, 1)
                    link(dve.memset(tot[:], 0.0))
                    dve.wait_ge(summed, 1)
                    link(dve.tensor_copy(pos[:].rearrange("p t e -> p (t e)"), pp[:, 1, 0:T * ne]))
                    for t in range(1, T):
                        link(dve.tensor_tensor(tot[:, t, :], tot[:, t - 1, :], pos[:, t - 1, :], ALU.add))
                    link(dve.tensor_tensor(pos[:].rearrange("p t e -> p (t e)"), pp[:, 0, 0:T * ne],
                                           tot[:, 0:T, :].rearrange("p t e -> p (t e)"), ALU.add))
                    link(dve.tensor_tensor(pos[:], pos[:], one[:], ALU.mult))
                    link(dve.tensor_reduce(place[:], pos[:], AX, ALU.add))
                    link(dve.tensor_scalar(kept[:], place[:], cap + 0.5, None, ALU.is_lt))
                    link(dve.tensor_tensor(factor[:], prob[:], kept[:], ALU.mult))
                    link(dve.tensor_tensor(one[:], one[:], over_mid(base[:], T), ALU.mult))
                    link(dve.tensor_reduce(tmp[:], one[:], AX, ALU.add))
                    link(dve.scalar_tensor_tensor(out=place[:], in0=place[:], scalar=float(cap), in1=tmp[:],
                                                  op0=ALU.min, op1=ALU.add))
                    link(dve.tensor_copy(get[:], place[:]))
                    link(dve.tensor_tensor(place[:], place[:], behind[:], ALU.subtract))
                    link(dve.tensor_tensor(place[:], place[:], kept[:], ALU.mult))
                    link(dve.tensor_tensor(put[:], place[:], behind[:], ALU.add))

                @block.tensor
                def _(pe):
                    pe.wait_ge(chosen, 1)
                    pe.matmul(pp[:, 0, 0:T * ne], upto[:], one[:].rearrange("p t e -> p (t e)"), start=True, stop=True)
                    pe.matmul(pp[:, 1, 0:T * ne], ones[:], one[:].rearrange("p t e -> p (t e)"), start=True, stop=True
                              ).then_inc(summed, 1)
        routed_experts(nc, "l2f_moe", c, a, x, xn, put, get, factor, ne, room, fh)


def routed_experts(nc, tag, c, a, x, xn, put, get, factor, ne, room, fh):
    f = "L2_ffn_"
    rt = room // P
    mh = fh // P
    rows_in, rows_out = c.routed
    put_landed, get_landed = c.put_landed, c.get_landed
    with Scope(nc, tag) as s:
        w1 = s.sb("w1", [P, 2, KD, fh])
        w2 = s.sb("w2", [P, 2, mh, D])
        b1 = s.sb("b1", [P, ne, mh])
        b2 = s.sb("b2", [P, 2, D])
        rows = s.sb("rows", [P, 2, rt, D])
        cols = s.sb("cols", [P, 2, KD, room])
        hid = s.sb("hid", [P, 2, mh, room])
        res = s.sb("res", [P, 2, rt, D])
        nought = s.sb("nought", [P, D])
        y = xn
        held = s.sb("held", [P, G1, D])
        flag = s.sb("flag", [P, G1, D], U8)
        pt = s.ps("pt", [P, KD, room])
        ph = s.ps("ph", [P, 4, room])
        py = s.ps("py", [P, 2, 512])
        with stage(nc, tag, "nought_set", "b1_in", "w_in0", "w_in1", "rows_in0", "rows_in1", "res_out0",
                   "res_out1", "turned", "cols_ready", "hid_ps", "hid_ready", "y_ps", "y_read", "put_done",
                   "stored", "scaled", "step") as (
                block, nought_set, b1_in, w_in0, w_in1, rows_in0, rows_in1, res_out0, res_out1, turned,
                cols_ready, hid_ps, hid_ready, y_ps, y_read, put_done, stored, scaled, step):
            w_loaded, rows_loaded, res_out = [w_in0, w_in1], [rows_in0, rows_in1], [res_out0, res_out1]

            def each_expert(eng, body):
                with eng.Fori(0, ne // 2) as i:
                    for b in range(2):
                        body(b, i, 2 * i + b)

            @block.sync
            def _(sp):
                def load_weights(b, e):
                    sp.dma_start(w1[:, b], a[f + "w1"][ds(e, 1)].rearrange("o (k p) n -> p (o k) n", p=P)
                                 ).then_inc(w_loaded[b], 16)
                    sp.dma_start(w2[:, b], a[f + "w2"][ds(e, 1)].rearrange("o (k p) n -> p (o k) n", p=P)
                                 ).then_inc(w_loaded[b], 16)
                    sp.dma_start(b2[:, b], a[f + "b2"][ds(e, 1), :].to_broadcast([P, D])).then_inc(w_loaded[b], 16)

                def load_rows(b, e):
                    sp.dma_start(rows[:, b], rows_in[ds(e * room, room), :].rearrange("(t p) d -> p t d", p=P)
                                 ).then_inc(rows_loaded[b], 16)

                def store_results(b, e):
                    sp.wait_ge(y_read, e * rt + (rt + 2))
                    sp.dma_start(rows_out[ds(e * room, room), :].rearrange("(t p) d -> p t d", p=P), res[:, b]
                                 ).then_inc(res_out[b], 16)

                with nc.allow_non_contiguous_dma(reason="biases by columns"):
                    sp.dma_start(b1[:].rearrange("p e m -> p (e m)"), vec_cols(a[f + "b1"].rearrange("e n -> (e n)"))
                                 ).then_inc(b1_in, 16)
                for b in range(2):
                    sp.sem_inc(res_out[b], 16)
                    load_weights(b, b)
                sp.wait_ge(put_done, 1)
                for b in range(2):
                    load_rows(b, b)
                with sp.Fori(1, ne // 2) as i:
                    for b in range(2):
                        store_results(b, 2 * i + (b - 2))
                        load_weights(b, 2 * i + b)
                        load_rows(b, 2 * i + b)
                for b in range(2):
                    store_results(b, ne - 2 + b)
                for b in range(2):
                    sp.wait_ge(res_out[b], 16 * (ne // 2 + 1))
                sp.sem_inc(stored, 1)

            @block.gpsimd
            def _(pool):
                pool.memset(nought[:], 0.0).then_inc(nought_set, 1)
                for t in range(T):
                    pool.indirect_dma_start(rows_in, bass.IndirectOffsetOnAxis(ap=put[:, t:t + 1], axis=0),
                                            xn[:, t, :], None, bounds_check=ne * room + NP - 1, oob_is_err=True
                                            ).then_inc(put_landed, 16)
                pool.wait_ge(put_landed, 16 * T)
                pool.sem_inc(put_done, 1)
                pool.wait_ge(stored, 1)
                for t in range(T):
                    pool.indirect_dma_start(y[:, t, :], None, rows_out,
                                            bass.IndirectOffsetOnAxis(ap=get[:, t:t + 1], axis=0),
                                            bounds_check=ne * room - 1, oob_is_err=True
                                            ).then_inc(get_landed[t // G1], 16)

            @block.scalar
            def _(act):
                act.wait_ge(b1_in, 16)

                def body(b, i, e):
                    for m in range(mh):
                        act.wait_ge(hid_ps, e * mh + (m + 1))
                        act.activation(hid[:, b, m, :], ph[:, m % 4, :], ACT.Relu, bias=b1[:, ds(e, 1), m]
                                       ).then_inc(hid_ready, 1)
                each_expert(act, body)
                for g in range(T // G1):
                    act.wait_ge(get_landed[g], 16 * G1)
                    for t in range(g * G1, (g + 1) * G1):
                        act.activation(y[:, t, :], y[:, t, :], ACT.Copy, scale=factor[:, t:t + 1]).then_inc(scaled, 1)

            @block.tensor
            def _(pe):
                pe.sem_inc(hid_ready, 4)
                pe.sem_inc(cols_ready, 2)
                pe.sem_inc(y_read, 2)

                def body(b, i, e):
                    pe.wait_ge(rows_loaded[b], (i + 1) * 16)
                    pe.wait_ge(cols_ready, 2 * e + 2)
                    for k in range(KD):
                        for t in range(rt):
                            last = pe.transpose(pt[:, k, t * P:(t + 1) * P], rows[:, b, t, k * P:(k + 1) * P], c.ident[:])
                        last.then_inc(turned, 1)
                    pe.wait_ge(w_loaded[b], (i + 1) * 48)
                    pe.wait_ge(cols_ready, 2 * e + 4)
                    for m in range(mh):
                        pe.wait_ge(hid_ready, e * mh + (m + 1))
                        for k in range(KD):
                            last = pe.matmul(ph[:, m % 4, :], w1[:, b, k, m * P:(m + 1) * P], cols[:, b, k, :],
                                             start=(k == 0), stop=(k == KD - 1))
                        last.then_inc(hid_ps, 1)
                    pe.wait_ge(hid_ready, e * mh + (mh + 4))
                    for t in range(rt):
                        pe.wait_ge(y_read, e * rt + (t + 1))
                        for m in range(mh):
                            last = pe.matmul(py[:, t % 2, 0:D], hid[:, b, m, t * P:(t + 1) * P], w2[:, b, m, :],
                                             start=(m == 0), stop=(m == mh - 1))
                        last.then_inc(y_ps, 1)
                each_expert(pe, body)

            @block.vector
            def _(dve):
                def body(b, i, e):
                    for k in range(KD):
                        dve.wait_ge(turned, 2 * e + (k + 1))
                        dve.tensor_copy(cols[:, b, k, :], pt[:, k, :]).then_inc(cols_ready, 1)
                    dve.wait_ge(res_out[b], (i + 1) * 16)
                    dve.wait_ge(w_loaded[b], (i + 1) * 48)
                    for t in range(rt):
                        dve.wait_ge(y_ps, e * rt + (t + 1))
                        dve.tensor_tensor(res[:, b, t, :], py[:, t % 2, 0:D], b2[:, b, :], ALU.add).then_inc(y_read, 1)
                each_expert(dve, body)
                link = Link(dve, step)
                dve.wait_ge(nought_set, 1)
                for g in range(T // G1):
                    dve.wait_ge(scaled, (g + 1) * G1)
                    yg = y[:, g * G1:(g + 1) * G1, :]
                    xg = x[:, g * G1:(g + 1) * G1, :]
                    link(dve.tensor_tensor(flag[:], yg, yg, ALU.not_equal))
                    link(dve.copy_predicated(yg, flag[:], over_mid(nought[:], G1)))
                    link(dve.tensor_scalar(held[:], yg, 1e4, -1e4, ALU.min, ALU.max))
                    link(dve.tensor_scalar(flag[:], yg, 0.0, 0.0, ALU.mult, ALU.not_equal))
                    link(dve.copy_predicated(yg, flag[:], held[:]))
                    link(dve.tensor_tensor(xg, xg, yg, ALU.add))


def l3_gnn(nc, c, a, x, tables, dinv, dram):
    f = "L3_gnn_"
    with Scope(nc, "l3g") as s:
        vec = s.sb("vec", [P, 5, 3, KD])
        w = s.sb("w", [P, 6, KD, D])
        scale = s.sb("scale", [P, KD])
        shift = s.sb("shift", [P, KD])
        stats = s.sb("stats", [P, KD, NP // 400, 6])
        rows = s.sb("rows", [P, T, D])
        agg_x = s.sb("agg_x", [P, KD, NP])
        h_fm = s.sb("h_fm", [P, KD, NP])
        agg_h = s.sb("agg_h", [P, KD, NP])

        def slot(i):
            return (0, 1, 2, 4, 5)[i]
        loads = (
             *[(w[:, slot(i)], a[f + f"W{i + 1}"].rearrange("(k p) n -> p k n", p=P)) for i in (0, 1, 3, 4)],
             (w[:, 2:4].rearrange("p a k n -> p (a k) n"), a[f + "W3"].rearrange("(k p) n -> p k n", p=P)),
             *[(vec[:, i, j], vec_cols(a[f + n + str(i + 1)])) for i in range(5) for j, n in enumerate(["b", "g", "be"])])

        def lin_bn_relu(i, srcs, dst):
            wi = w[:, 2:4].rearrange("p a k n -> p (a k) n") if i == 2 else w[:, slot(i)]
            product_fm(nc, f"l3g_w{i}", srcs, wi, dst, ACT.Identity, vec[:, i, 0], stats)
            batchnorm_columns(nc, f"l3g_bn{i}", dst, vec[:, i, 1], vec[:, i, 2], scale, shift, stats, relu=True)

        def halves(t):
            return [t[:, k] for k in range(KD)]

        with Scope(nc, "l3ga") as q:
            agg = q.sb("agg", [P, T, D])
            layernorm(nc, "l3g_ln", c, x, rows, ahead=[[], loads])
            aggregate(nc, "l3g_agg", c, tables[0], T, G1, lambda t, i: rows[:, ds(t, 1), :].rearrange("p a d -> p (a d)"),
                      D, lambda t, i: agg[:, ds(t, 1), :].rearrange("p a d -> p (a d)"))
            turn(nc, "l3g_t", agg, agg_x, c.ident)
            settle(nc, "l3g_settle", c, 1)
            lin_bn_relu(0, halves(agg_x), h_fm)
            lin_bn_relu(1, halves(h_fm), agg_h)
            unturn(nc, "l3g_u", agg_h, rows, c.ident)
            aggregate(nc, "l3g_agg2", c, tables[0], T, G1, lambda t, i: rows[:, ds(t, 1), :].rearrange("p a d -> p (a d)"),
                      D, lambda t, i: agg[:, ds(t, 1), :].rearrange("p a d -> p (a d)"))
            turn(nc, "l3g_t2", agg, agg_h, c.ident)
        lin_bn_relu(2, halves(agg_x) + halves(agg_h), h_fm)
        lin_bn_relu(3, halves(h_fm), agg_x)
        lin_bn_relu(4, halves(agg_x), h_fm)
        unturn(nc, "l3g_u2", h_fm, x, c.ident, add=True)


def unturn(nc, tag, fm, nm, ident, add=False):
    with Scope(nc, tag) as s:
        pt = s.ps("pt", [P, 8, 512])
        with stage(nc, tag, "turned", "out") as (block, turned, out):
            @block.tensor
            def _(pe):
                for t in range(T):
                    if t >= 8:
                        pe.wait_ge(out, t - 7)
                    for k in range(KD):
                        last = pe.transpose(pt[:, t % 8, k * P:(k + 1) * P], fm[:, k, t * P:(t + 1) * P], ident[:])
                    last.then_inc(turned, 1)

            @block.vector
            def _(dve):
                for t in range(T):
                    dve.wait_ge(turned, t + 1)
                    if add:
                        dve.tensor_tensor(nm[:, t, :], pt[:, t % 8, 0:D], nm[:, t, :], ALU.add).then_inc(out, 1)
                    else:
                        dve.tensor_copy(nm[:, t, :], pt[:, t % 8, 0:D]).then_inc(out, 1)


def l3_ffn(nc, c, a, x, tables, dinv, dram):
    ne = 6
    f = "L3_ffn_"
    with Scope(nc, "l3f") as s:
        xt = s.sb("xt", [P, KD, NP])
        gate = s.sb("gate", [P, T, ne])
        ws = [s.sb(f"w{i}", [P, ne, KD, D]) for i in range(3)]
        b = s.sb("b", [P, 2, ne, KD])
        b3 = s.sb("b3", [ne, D])
        with Scope(nc, "l3fr") as q:
            w1 = q.sb("w1", [P, KD, P])
            b1 = q.sb("b1", [P, 1])
            w2 = q.sb("w2", [P, 1, ne])
            br = q.sb("br", [P, ne])
            rh = q.sb("rh", [P, 1, NP])
            score = q.sb("score", [P, T, ne])
            normal_input(nc, "l3f", c, x, xt, [
                [(w1[:], a[f + "router_w1"].rearrange("(k p) n -> p k n", p=P)), (b1[:], vec_cols(a[f + "router_b1"])),
                 (w2[:, 0], a[f + "router_w2"]), (br[:], across(a[f + "router_b2"], ne))],
                [(b[:, i].rearrange("p e k -> p (e k)"), vec_cols(a[f + f"expert_b{i + 1}"].rearrange("e n -> (e n)")))
                 for i in range(2)] + [(b3[:], a[f + "expert_b3"])] +
                [(ws[i][:, e], a[f + f"expert_w{i + 1}"][e].rearrange("(k p) n -> p k n", p=P)) for i in range(3)
                 for e in range(ne)]])
            settle(nc, "l3f_settle0", c, 0)
            product_fm(nc, "l3f_r1", [xt[:, k] for k in range(KD)], w1, rh, ACT.Relu, b1)
            product_nm(nc, "l3f_r2", rh, w2, ne, lambda dve, t, ps: dve.tensor_copy(score[:, t, :], ps))
            softmax(nc, "l3f_sm", score, ne, br)
            top2_gates(nc, "l3f_top", c, score, ne, gate)
        settle(nc, "l3f_settle1", c, 1)
        experts(nc, "l3f_moe", c, xt, x, gate, ne, [(ws[i], KD, KD, ACT.Relu, None, b[:, i]) for i in range(2)], ws[2], b3)


PARTS = [("l0_ffn", l0_ffn), ("l1_gnn", l1_gnn), ("l1_ffn", l1_ffn), ("l2_gnn", l2_gnn),
         ("l2_ffn", l2_ffn), ("l3_gnn", l3_gnn), ("l3_ffn", l3_ffn)]
_INS = "x src dst".split() + """L0_gnn_W_gcn L0_gnn_b_gcn L0_gnn_W_V
L0_ffn_W_gat L0_ffn_att_src L0_ffn_att_dst L0_ffn_b_gat L0_ffn_ln_gamma L0_ffn_ln_beta L0_ffn_W1 L0_ffn_b1 L0_ffn_W2
L0_ffn_b2 L0_ffn_edge_index L1_gnn_W1 L1_gnn_b1 L1_gnn_W2 L1_gnn_att_src L1_gnn_att_dst L1_gnn_b2 L1_ffn_Wr L1_ffn_br
L1_ffn_W1 L1_ffn_b1 L1_ffn_g1 L1_ffn_be1 L1_ffn_m1 L1_ffn_v1 L1_ffn_W2 L1_ffn_b2 L1_ffn_g2 L1_ffn_be2 L1_ffn_m2
L1_ffn_v2 L1_ffn_Wo L1_ffn_bo L2_gnn_W0 L2_gnn_a_src0 L2_gnn_a_dst0 L2_gnn_b0 L2_gnn_gamma0 L2_gnn_beta0 L2_gnn_W1
L2_gnn_a_src1 L2_gnn_a_dst1 L2_gnn_b1 L2_ffn_gate_w L2_ffn_gate_b L2_ffn_w1 L2_ffn_b1 L2_ffn_w2 L2_ffn_b2""".split() + [
    f"L3_gnn_{v}{i}" for i in range(1, 6) for v in ("W", "b", "g", "be")] + [
    "L3_ffn_router_w1", "L3_ffn_router_b1", "L3_ffn_router_w2", "L3_ffn_router_b2"] + [
    f"L3_ffn_expert_{v}{i}" for i in range(1, 4) for v in ("w", "b")]


def kernel(**inputs):
    import concourse.bacc as bacc
    import numpy as np
    from concourse.bass_utils import run_bass_kernel_spmd

    nc = bacc.Bacc("TRN2", target_bir_lowering=False, num_devices=1)
    arrays, args = {}, {}
    for name in _INS:
        v = np.ascontiguousarray(inputs[name])
        if name in ("src", "dst"):
            v = np.concatenate([v, np.full(NCH1 * P - E1, NP - 1, v.dtype)])
        arrays["in_" + name] = v
        args[name] = nc.dram_tensor("in_" + name, v.shape, mybir.dt.from_np(v.dtype), kind="ExternalInput").ap()
    out = nc.dram_tensor("out_x", (N, D), F32, kind="ExternalOutput").ap()
    build(nc, args, out)
    r = run_bass_kernel_spmd(nc, [arrays], core_ids=[0])
    return r.results[0]["out_x"]
```
